# Optimizing a Trainium2 kernel written in Bass

```python
import numpy as np
import jax
import jax.numpy as jnp

def _softmax(x, axis=-1):
    return jax.nn.softmax(x, axis=axis)

def _gelu(x):
    return jax.nn.gelu(x, approximate=True)

def _silu(x):
    return jax.nn.silu(x)

def _sigmoid(x):
    return jax.nn.sigmoid(x)

def _layernorm(x, axis=-1, eps=1e-05):
    m = jnp.mean(x, axis=axis, keepdims=True)
    v = jnp.var(x, axis=axis, keepdims=True)
    return (x - m) / jnp.sqrt(v + eps)

def _scatter_add(tgt, idx, src, axis=0):
    return tgt.at[idx].add(src)

def _segment_sum(src, seg, n):
    return jax.ops.segment_sum(src, seg, n)
kernel_name = 'mk_xattn_ffn_d4_seqx_r8_bd91ca'

def setup_inputs(seed: int=0):
    np.random.seed(seed)
    _w = jnp.asarray

    def _rec_inputs():
        import jax
        import jax.numpy as jnp
        _rk = jax.random.key(seed)
        x = 7.22e-05 + 1 * jax.random.normal(jax.random.fold_in(_rk, 1), (4, 256, 128), jnp.float32)
        _lenS = 256 - jax.random.randint(jax.random.fold_in(_rk, 7), (4,), 0, max(1, 256 // 4) + 1, jnp.int32)
        _lenS2 = 256 - jax.random.randint(jax.random.fold_in(_rk, 8), (4,), 0, max(1, 256 // 4) + 1, jnp.int32)
        _ctx_1024P = jax.random.normal(jax.random.fold_in(_rk, 11), (4, 16, 128), jnp.float32)
        _ctx_1024c = jax.random.dirichlet(jax.random.fold_in(_rk, 511), 0.3 * jnp.ones((16,), jnp.float32), (4, 256))
        _ctx_1024t = jnp.einsum('bsk,bkd->bsd', _ctx_1024c, _ctx_1024P)
        _ctx_1024t = _ctx_1024t * jax.lax.rsqrt(jnp.mean(jnp.square(_ctx_1024t)) + 1e-12) * 0.953939
        ctx_1024 = 4.13588e-05 + 0.999923 * (_ctx_1024t + 0.3 * jax.random.normal(jax.random.fold_in(_rk, 611), (4, 256, 128), jnp.float32))
        _validS = jnp.arange(256)[None, :] < _lenS[:, None]
        _validS2 = jnp.arange(256)[None, :] < _lenS2[:, None]
        _causal = jnp.tril(jnp.ones((256, 256), dtype=bool))
        mask_1x1xSxS2_bk0 = jnp.logical_not(jnp.broadcast_to(_validS2[0:1, None, None, :], (1, 1, 256, 256)))
        mask_BxSxS2_ik0 = jnp.where(jnp.broadcast_to(_validS2[:, None, :], (4, 256, 256)), 0, 1).astype(jnp.int32)
        return (x, ctx_1024, mask_1x1xSxS2_bk0, mask_BxSxS2_ik0)
    x, ctx_1024, mask_1x1xSxS2_bk0, mask_BxSxS2_ik0 = _rec_inputs()

    def _L0_xattn_setup():
        import jax, jax.numpy as jnp
        import numpy as np
        B, N, M, D = (4, 256, 256, 128)
        H, HS, OUT = (16, 64, 128)
        key0 = jax.random.key(seed)
        ks = jax.random.split(key0, 7)
        return {'query': jax.random.normal(ks[0], (B, N, D), jnp.float32), 'key': jax.random.normal(ks[1], (B, M, D), jnp.float32), 'value': jax.random.normal(ks[2], (B, M, D), jnp.float32), 'query_kernel': jax.random.normal(ks[3], (H, D, HS), jnp.float32) * 0.02, 'key_kernel': jax.random.normal(ks[4], (H, D, HS), jnp.float32) * 0.02, 'value_kernel': jax.random.normal(ks[5], (H, D, HS), jnp.float32) * 0.02, 'projection_kernel': jax.random.normal(ks[6], (H, HS, OUT), jnp.float32) * 0.02, 'projection_bias': jnp.zeros((OUT,), jnp.float32)}
    _L0_xattn_all = _L0_xattn_setup()
    _L0_xattn_in = {k: v for k, v in _L0_xattn_all.items() if k in ('query_kernel', 'key_kernel', 'value_kernel', 'projection_kernel', 'projection_bias')}
    del _L0_xattn_all

    def _L0_ffn_setup():
        import jax, jax.numpy as jnp
        import numpy as np
        ALPHA = 2.0
        TOP_K = 2
        key = jax.random.key(seed)
        ks = jax.random.split(key, 8)
        B, S, D, H, E = (2, 256, 128, 512, 8)
        Er = E - 1
        s_in = 1.0 / np.sqrt(D)
        s_hid = 1.0 / np.sqrt(H)
        return {'x': jax.random.normal(ks[0], (B, S, D), dtype=jnp.float32), 'router_w': jax.random.normal(ks[1], (D, E), dtype=jnp.float32) * s_in, 'up_w': jax.random.normal(ks[2], (Er, D, H), dtype=jnp.float32) * s_in, 'gate_w': jax.random.normal(ks[3], (Er, D, H), dtype=jnp.float32) * s_in, 'down_w': jax.random.normal(ks[4], (Er, H, D), dtype=jnp.float32) * s_hid * 0.1, 'shared_up_w': jax.random.normal(ks[5], (D, H), dtype=jnp.float32) * s_in, 'shared_gate_w': jax.random.normal(ks[6], (D, H), dtype=jnp.float32) * s_in, 'shared_down_w': jax.random.normal(ks[7], (H, D), dtype=jnp.float32) * s_hid * 0.1}
    _L0_ffn_all = _L0_ffn_setup()
    _L0_ffn_in = {k: v for k, v in _L0_ffn_all.items() if k in ('router_w', 'up_w', 'gate_w', 'down_w', 'shared_up_w', 'shared_gate_w', 'shared_down_w')}
    del _L0_ffn_all

    def _L1_xattn_setup():
        import jax, jax.numpy as jnp
        import numpy as np
        B, L, D, H = (4, 256, 128, 16)
        HD = D // H

        def _rope_tables(seq_len, head_dim):
            inv_freq = 1.0 / 10000.0 ** (np.arange(0, head_dim, 2, dtype=np.float32) / head_dim)
            t = np.arange(seq_len, dtype=np.float32)
            freqs = np.outer(t, inv_freq)
            emb = np.concatenate([freqs, freqs], axis=-1)
            return (jnp.asarray(np.cos(emb)), jnp.asarray(np.sin(emb)))

        def _alibi_slopes(n):
            assert n & n - 1 == 0
            s = 2.0 ** (-2.0 ** (-(np.log2(n) - 3)) * np.arange(1, n + 1, dtype=np.float32))
            return jnp.asarray(s, dtype=jnp.float32)

        def _rotate_half(x):
            x1, x2 = jnp.split(x, 2, axis=-1)
            return jnp.concatenate([-x2, x1], axis=-1)
        key = jax.random.key(seed)
        ks = jax.random.split(key, 11)
        std = 1.0 / np.sqrt(D)
        inp = {'query': jax.random.normal(ks[0], (B, L, D), jnp.float32), 'key': jax.random.normal(ks[1], (B, L, D), jnp.float32), 'value': jax.random.normal(ks[2], (B, L, D), jnp.float32), 'mask': jnp.tril(jnp.ones((L, L), jnp.bool_))[None, None], 'Wq': jax.random.normal(ks[3], (D, D), jnp.float32) * std, 'bq': jnp.zeros((D,), jnp.float32), 'Wk': jax.random.normal(ks[4], (D, D), jnp.float32) * std, 'bk': jnp.zeros((D,), jnp.float32), 'Wv': jax.random.normal(ks[5], (D, D), jnp.float32) * std, 'bv': jnp.zeros((D,), jnp.float32), 'Wo': jax.random.normal(ks[6], (D, D), jnp.float32) * std, 'bo': jnp.zeros((D,), jnp.float32)}
        return inp
    _L1_xattn_all = _L1_xattn_setup()
    _L1_xattn_in = {k: v for k, v in _L1_xattn_all.items() if k in ('Wq', 'bq', 'Wk', 'bk', 'Wv', 'bv', 'Wo', 'bo')}
    del _L1_xattn_all

    def _L1_ffn_setup():
        import jax, jax.numpy as jnp
        import numpy as np
        B, S, D = (4, 512, 128)
        E, F_EXP = (16, 256)
        F_C = 2.0
        F_SH = 256
        key = jax.random.key(seed)
        ks = jax.random.split(key, 8)
        s = 0.02
        return {'hidden_states': jax.random.normal(ks[0], (B, S, D), jnp.float32), 'gate_w': jax.random.normal(ks[1], (E, D), jnp.float32) * s, 'Wg': jax.random.normal(ks[2], (E, F_EXP, D), jnp.float32) * s, 'Wu': jax.random.normal(ks[3], (E, F_EXP, D), jnp.float32) * s, 'Wd': jax.random.normal(ks[4], (E, D, F_EXP), jnp.float32) * s, 'Ws_g': jax.random.normal(ks[5], (F_SH, D), jnp.float32) * s, 'Ws_u': jax.random.normal(ks[6], (F_SH, D), jnp.float32) * s, 'Ws_d': jax.random.normal(ks[7], (D, F_SH), jnp.float32) * s}
    _L1_ffn_all = _L1_ffn_setup()
    _L1_ffn_in = {k: v for k, v in _L1_ffn_all.items() if k in ('gate_w', 'Wg', 'Wu', 'Wd', 'Ws_g', 'Ws_u', 'Ws_d')}
    del _L1_ffn_all

    def _L2_xattn_setup():
        import jax, jax.numpy as jnp
        import numpy as np
        from jax import lax
        BIG = jnp.float32(1e+30)

        def _pairwise_euclidean(a, b):
            aa = jnp.sum(a * a, axis=-1)[:, None]
            bb = jnp.sum(b * b, axis=-1)[None, :]
            ab = a @ b.T
            return jnp.sqrt(jnp.maximum(aa + bb - 2.0 * ab, 0.0))

        def _dtw_cost(D):
            row0 = jnp.cumsum(D[0])

            def row_step(prev_row, d_row):
                first = d_row[0] + prev_row[0]

                def col_step(left, inp):
                    d_ij, up, diag = inp
                    r = d_ij + jnp.minimum(jnp.minimum(up, left), diag)
                    return (r, r)
                _, rest = lax.scan(col_step, first, (d_row[1:], prev_row[1:], prev_row[:-1]))
                row = jnp.concatenate([first[None], rest])
                return (row, row)
            _, rows = lax.scan(row_step, row0, D[1:])
            return jnp.concatenate([row0[None], rows], axis=0)

        def _backtrack(R, T1, T2):
            L = T1 + T2 - 1

            def step(carry, _):
                i, j, done = carry
                valid = jnp.logical_not(done)
                cd = jnp.where((i > 0) & (j > 0), R[jnp.maximum(i - 1, 0), jnp.maximum(j - 1, 0)], BIG)
                cu = jnp.where(i > 0, R[jnp.maximum(i - 1, 0), j], BIG)
                cl = jnp.where(j > 0, R[i, jnp.maximum(j - 1, 0)], BIG)
                choice = jnp.argmin(jnp.stack([cd, cu, cl]))
                ni = jnp.where(choice <= 1, i - 1, i)
                nj = jnp.where((choice == 0) | (choice == 2), j - 1, j)
                at_origin = (i == 0) & (j == 0)
                ni = jnp.where(at_origin, 0, ni)
                nj = jnp.where(at_origin, 0, nj)
                return ((ni, nj, done | at_origin), (i, j, valid))
            init = (jnp.int32(T1 - 1), jnp.int32(T2 - 1), jnp.bool_(False))
            _, (i_idx, j_idx, valid) = lax.scan(step, init, None, length=L)
            return (i_idx, j_idx, valid)

        def _align_one(small, large):
            T_small, d = small.shape
            T_large = large.shape[0]
            D = _pairwise_euclidean(small, large)
            R = _dtw_cost(D)
            i_idx, j_idx, valid = _backtrack(R, T_small, T_large)
            contrib = small[i_idx] * valid[:, None].astype(small.dtype)
            expanded = jnp.zeros((T_large, d), dtype=small.dtype).at[j_idx].add(contrib)
            return expanded
        key = jax.random.key(seed)
        k1, k2 = jax.random.split(key)
        teacher = jax.random.normal(k1, (16, 50, 128), dtype=jnp.float32)
        student = jax.random.normal(k2, (16, 75, 128), dtype=jnp.float32)
        return {'teacher_features': teacher, 'student_features': student}
    _L2_xattn_all = _L2_xattn_setup()
    _L2_xattn_in = {k: v for k, v in _L2_xattn_all.items() if k in ()}
    del _L2_xattn_all

    def _L2_ffn_setup():
        import jax, jax.numpy as jnp
        import numpy as np
        D_MODEL, D_FF, N_EXPERTS, TOP_K = (128, 512, 8, 2)
        key = jax.random.key(seed)
        k0, k1, k2, k3 = jax.random.split(key, 4)
        x = jax.random.normal(k0, (2, 256, D_MODEL), dtype=jnp.float32)
        Wg = jax.random.normal(k1, (D_MODEL, N_EXPERTS), dtype=jnp.float32) * 0.02
        W1 = jax.random.normal(k2, (N_EXPERTS, D_MODEL, D_FF), dtype=jnp.float32) * 0.02
        b1 = jnp.zeros((N_EXPERTS, D_FF), dtype=jnp.float32)
        W2 = jax.random.normal(k3, (N_EXPERTS, D_FF, D_MODEL), dtype=jnp.float32) * 0.02
        b2 = jnp.zeros((N_EXPERTS, D_MODEL), dtype=jnp.float32)
        return {'x': x, 'Wg': Wg, 'W1': W1, 'b1': b1, 'W2': W2, 'b2': b2}
    _L2_ffn_all = _L2_ffn_setup()
    _L2_ffn_in = {k: v for k, v in _L2_ffn_all.items() if k in ('Wg', 'W1', 'b1', 'W2', 'b2')}
    del _L2_ffn_all

    def _L3_xattn_setup():
        import jax, jax.numpy as jnp
        import numpy as np
        import math
        B, S, D, H = (2, 256, 128, 16)
        HD = D // H
        key = jax.random.key(seed)
        ks = jax.random.split(key, 12)
        s = 1.0 / math.sqrt(D)
        inp = {'query': jax.random.normal(ks[0], (B, S, D), jnp.float32), 'key': jax.random.normal(ks[1], (B, S, D), jnp.float32), 'value': jax.random.normal(ks[2], (B, S, D), jnp.float32), 'mask': jnp.tril(jnp.ones((S, S), jnp.int32))[None].repeat(B, axis=0), 'Wq': jax.random.normal(ks[3], (H, D, HD), jnp.float32) * s, 'bq': jax.random.normal(ks[4], (H, HD), jnp.float32) * s, 'Wk': jax.random.normal(ks[5], (H, D, HD), jnp.float32) * s, 'bk': jax.random.normal(ks[6], (H, HD), jnp.float32) * s, 'Wv': jax.random.normal(ks[7], (H, D, HD), jnp.float32) * s, 'bv': jax.random.normal(ks[8], (H, HD), jnp.float32) * s, 'Wo': jax.random.normal(ks[9], (D, D), jnp.float32) * s, 'bo': jax.random.normal(ks[10], (D,), jnp.float32) * s}
        return inp
    _L3_xattn_all = _L3_xattn_setup()
    _L3_xattn_in = {k: v for k, v in _L3_xattn_all.items() if k in ('Wq', 'bq', 'Wk', 'bk', 'Wv', 'bv', 'Wo', 'bo')}
    del _L3_xattn_all

    def _L3_ffn_setup():
        import jax, jax.numpy as jnp
        import numpy as np
        IN_F = 128
        OUT_F = 128
        B, S = (8, 512)

        def _pack_ternary(tern):
            enc = (tern + 1.0).astype(jnp.int32).reshape(-1)
            return (enc[0::4] | enc[1::4] << 2 | enc[2::4] << 4 | enc[3::4] << 6).astype(jnp.int32)
        key = jax.random.key(seed)
        kx, kw = jax.random.split(key)
        x = jax.random.normal(kx, (B, S, IN_F), dtype=jnp.float32)
        w = jax.random.normal(kw, (OUT_F, IN_F), dtype=jnp.float32) * 0.02
        scale = jnp.maximum(jnp.mean(jnp.abs(w)), 1e-05)
        wn = w / scale
        tern = jnp.sign(wn) * (jnp.abs(wn) > 0.5).astype(jnp.float32)
        packed = _pack_ternary(tern)
        bias = jnp.zeros((OUT_F,), dtype=jnp.float32)
        return {'x': x, 'packed_weight': packed, 'weight_scale': scale.reshape(1), 'bias': bias}
    _L3_ffn_all = _L3_ffn_setup()
    _L3_ffn_in = {k: v for k, v in _L3_ffn_all.items() if k in ('packed_weight', 'weight_scale', 'bias')}
    del _L3_ffn_all
    return {'x': x, 'ctx_1024': ctx_1024, 'mask_1x1xSxS2_bk0': mask_1x1xSxS2_bk0, 'mask_BxSxS2_ik0': mask_BxSxS2_ik0, 'L0_xattn_query_kernel': _L0_xattn_in['query_kernel'], 'L0_xattn_key_kernel': _L0_xattn_in['key_kernel'], 'L0_xattn_value_kernel': _L0_xattn_in['value_kernel'], 'L0_xattn_projection_kernel': _L0_xattn_in['projection_kernel'], 'L0_xattn_projection_bias': _L0_xattn_in['projection_bias'], 'L0_ffn_router_w': _L0_ffn_in['router_w'], 'L0_ffn_up_w': _L0_ffn_in['up_w'], 'L0_ffn_gate_w': _L0_ffn_in['gate_w'], 'L0_ffn_down_w': _L0_ffn_in['down_w'], 'L0_ffn_shared_up_w': _L0_ffn_in['shared_up_w'], 'L0_ffn_shared_gate_w': _L0_ffn_in['shared_gate_w'], 'L0_ffn_shared_down_w': _L0_ffn_in['shared_down_w'], 'L1_xattn_Wq': _L1_xattn_in['Wq'], 'L1_xattn_bq': _L1_xattn_in['bq'], 'L1_xattn_Wk': _L1_xattn_in['Wk'], 'L1_xattn_bk': _L1_xattn_in['bk'], 'L1_xattn_Wv': _L1_xattn_in['Wv'], 'L1_xattn_bv': _L1_xattn_in['bv'], 'L1_xattn_Wo': _L1_xattn_in['Wo'], 'L1_xattn_bo': _L1_xattn_in['bo'], 'L1_ffn_gate_w': _L1_ffn_in['gate_w'], 'L1_ffn_Wg': _L1_ffn_in['Wg'], 'L1_ffn_Wu': _L1_ffn_in['Wu'], 'L1_ffn_Wd': _L1_ffn_in['Wd'], 'L1_ffn_Ws_g': _L1_ffn_in['Ws_g'], 'L1_ffn_Ws_u': _L1_ffn_in['Ws_u'], 'L1_ffn_Ws_d': _L1_ffn_in['Ws_d'], 'L2_ffn_Wg': _L2_ffn_in['Wg'], 'L2_ffn_W1': _L2_ffn_in['W1'], 'L2_ffn_b1': _L2_ffn_in['b1'], 'L2_ffn_W2': _L2_ffn_in['W2'], 'L2_ffn_b2': _L2_ffn_in['b2'], 'L3_xattn_Wq': _L3_xattn_in['Wq'], 'L3_xattn_bq': _L3_xattn_in['bq'], 'L3_xattn_Wk': _L3_xattn_in['Wk'], 'L3_xattn_bk': _L3_xattn_in['bk'], 'L3_xattn_Wv': _L3_xattn_in['Wv'], 'L3_xattn_bv': _L3_xattn_in['bv'], 'L3_xattn_Wo': _L3_xattn_in['Wo'], 'L3_xattn_bo': _L3_xattn_in['bo'], 'L3_ffn_packed_weight': _L3_ffn_in['packed_weight'], 'L3_ffn_weight_scale': _L3_ffn_in['weight_scale'], 'L3_ffn_bias': _L3_ffn_in['bias']}

def reference(x, ctx_1024, mask_1x1xSxS2_bk0, mask_BxSxS2_ik0, L0_xattn_query_kernel, L0_xattn_key_kernel, L0_xattn_value_kernel, L0_xattn_projection_kernel, L0_xattn_projection_bias, L0_ffn_router_w, L0_ffn_up_w, L0_ffn_gate_w, L0_ffn_down_w, L0_ffn_shared_up_w, L0_ffn_shared_gate_w, L0_ffn_shared_down_w, L1_xattn_Wq, L1_xattn_bq, L1_xattn_Wk, L1_xattn_bk, L1_xattn_Wv, L1_xattn_bv, L1_xattn_Wo, L1_xattn_bo, L1_ffn_gate_w, L1_ffn_Wg, L1_ffn_Wu, L1_ffn_Wd, L1_ffn_Ws_g, L1_ffn_Ws_u, L1_ffn_Ws_d, L2_ffn_Wg, L2_ffn_W1, L2_ffn_b1, L2_ffn_W2, L2_ffn_b2, L3_xattn_Wq, L3_xattn_bq, L3_xattn_Wk, L3_xattn_bk, L3_xattn_Wv, L3_xattn_bv, L3_xattn_Wo, L3_xattn_bo, L3_ffn_packed_weight, L3_ffn_weight_scale, L3_ffn_bias):
    import jax
    import jax.numpy as jnp

    def _L0_xattn_ref(query, key, value, query_kernel, key_kernel, value_kernel, projection_kernel, projection_bias):
        import jax, jax.numpy as jnp
        import numpy as np
        B, N, M, D = (4, 256, 256, 128)
        H, HS, OUT = (16, 64, 128)
        q = jnp.einsum('bnd,hdo->bhno', query, query_kernel)
        k = jnp.einsum('bmd,hdo->bhmo', key, key_kernel)
        v = jnp.einsum('bmd,hdo->bhmo', value, value_kernel)
        q = q / jnp.sqrt(jnp.asarray(HS, q.dtype))
        logits = jnp.einsum('bhno,bhmo->bhnm', q, k)
        attn = jax.nn.softmax(logits, axis=-1)
        ctx = jnp.einsum('bhnm,bhmo->bhno', attn, v)
        out = jnp.einsum('bhno,hod->bnd', ctx, projection_kernel) + projection_bias
        return out

    def _L0_ffn_ref(x, router_w, up_w, gate_w, down_w, shared_up_w, shared_gate_w, shared_down_w):
        import jax, jax.numpy as jnp
        import numpy as np
        ALPHA = 2.0
        TOP_K = 2
        logits = jnp.einsum('bsd,de->bse', x, router_w)
        probs = jax.nn.softmax(logits, axis=-1)
        topk_vals, topk_idx = jax.lax.top_k(probs, TOP_K)
        top1_val = topk_vals[..., 0]
        top1_idx = topk_idx[..., 0]
        hid = jnp.einsum('bsd,edh->ebsh', x, up_w) * jax.nn.silu(jnp.einsum('bsd,edh->ebsh', x, gate_w))
        Er = up_w.shape[0]
        mask = (top1_idx[None, :, :] == jnp.arange(Er)[:, None, None]).astype(x.dtype)
        routed = jnp.einsum('ebsh,ehd,ebs->bsd', hid, down_w, mask)
        shid = jnp.einsum('bsd,dh->bsh', x, shared_up_w) * jax.nn.silu(jnp.einsum('bsd,dh->bsh', x, shared_gate_w))
        shared = jnp.einsum('bsh,hd->bsd', shid, shared_down_w)
        return ALPHA * top1_val[..., None] * routed + shared

    def _L1_xattn_ref(query, key, value, mask, Wq, bq, Wk, bk, Wv, bv, Wo, bo):
        import jax, jax.numpy as jnp
        import numpy as np
        B, L, D, H = (4, 256, 128, 16)
        HD = D // H

        def _rope_tables(seq_len, head_dim):
            inv_freq = 1.0 / 10000.0 ** (np.arange(0, head_dim, 2, dtype=np.float32) / head_dim)
            t = np.arange(seq_len, dtype=np.float32)
            freqs = np.outer(t, inv_freq)
            emb = np.concatenate([freqs, freqs], axis=-1)
            return (jnp.asarray(np.cos(emb)), jnp.asarray(np.sin(emb)))

        def _alibi_slopes(n):
            assert n & n - 1 == 0
            s = 2.0 ** (-2.0 ** (-(np.log2(n) - 3)) * np.arange(1, n + 1, dtype=np.float32))
            return jnp.asarray(s, dtype=jnp.float32)

        def _rotate_half(x):
            x1, x2 = jnp.split(x, 2, axis=-1)
            return jnp.concatenate([-x2, x1], axis=-1)
        Bq, Lq, _ = query.shape
        Lk = key.shape[1]
        scale = HD ** (-0.5)

        def proj(x, W, b, Lx):
            return (x @ W.T + b).reshape(Bq, Lx, H, HD).transpose(0, 2, 1, 3)
        Q = proj(query, Wq, bq, Lq)
        K = proj(key, Wk, bk, Lk)
        V = proj(value, Wv, bv, Lk)
        cos, sin = _rope_tables(Lq, HD)
        cos = cos[None, None]
        sin = sin[None, None]
        Q = Q * cos + _rotate_half(Q) * sin
        K = K * cos + _rotate_half(K) * sin
        scores = jnp.einsum('bhqd,bhkd->bhqk', Q, K) * scale
        dist = -jnp.abs(jnp.arange(Lq, dtype=jnp.float32)[:, None] - jnp.arange(Lk, dtype=jnp.float32)[None, :])
        scores = scores + _alibi_slopes(H)[None, :, None, None] * dist[None, None]
        scores = jnp.where(mask, scores, -jnp.inf)
        attn = jax.nn.softmax(scores, axis=-1)
        out = jnp.einsum('bhqk,bhkd->bhqd', attn, V)
        out = out.transpose(0, 2, 1, 3).reshape(Bq, Lq, D)
        return out @ Wo.T + bo

    def _L1_ffn_ref(hidden_states, gate_w, Wg, Wu, Wd, Ws_g, Ws_u, Ws_d):
        import jax, jax.numpy as jnp
        import numpy as np
        B, S, D = (4, 512, 128)
        E, F_EXP = (16, 256)
        F_C = 2.0
        F_SH = 256
        b, s, d = hidden_states.shape
        e = gate_w.shape[0]
        cap = int(s * F_C / e)
        logits = jnp.einsum('bsd,ed->bse', hidden_states, gate_w)
        scores = jax.nn.softmax(logits, axis=-1).transpose(0, 2, 1)
        topk_w, topk_idx = jax.lax.top_k(scores, cap)
        x_tok = jnp.take_along_axis(hidden_states[:, None, :, :], topk_idx[..., None], axis=2)
        g = jnp.einsum('becd,efd->becf', x_tok, Wg)
        u = jnp.einsum('becd,efd->becf', x_tok, Wu)
        h = jax.nn.gelu(g, approximate=False) * u
        eo = jnp.einsum('becf,edf->becd', h, Wd) * topk_w[..., None]
        offs = (jnp.arange(b) * s)[:, None, None]
        flat_idx = (topk_idx + offs).reshape(-1)
        flat = jnp.zeros((b * s, d), hidden_states.dtype)
        flat = flat.at[flat_idx].add(eo.reshape(-1, d))
        out = flat.reshape(b, s, d)
        gs = jnp.einsum('bsd,fd->bsf', hidden_states, Ws_g)
        us = jnp.einsum('bsd,fd->bsf', hidden_states, Ws_u)
        shared = jnp.einsum('bsf,df->bsd', jax.nn.gelu(gs, approximate=False) * us, Ws_d)
        return out + shared

    def _L2_xattn_ref(teacher_features, student_features):
        import jax, jax.numpy as jnp
        import numpy as np
        from jax import lax
        BIG = jnp.float32(1e+30)

        def _pairwise_euclidean(a, b):
            aa = jnp.sum(a * a, axis=-1)[:, None]
            bb = jnp.sum(b * b, axis=-1)[None, :]
            ab = a @ b.T
            return jnp.sqrt(jnp.maximum(aa + bb - 2.0 * ab, 0.0))

        def _dtw_cost(D):
            row0 = jnp.cumsum(D[0])

            def row_step(prev_row, d_row):
                first = d_row[0] + prev_row[0]

                def col_step(left, inp):
                    d_ij, up, diag = inp
                    r = d_ij + jnp.minimum(jnp.minimum(up, left), diag)
                    return (r, r)
                _, rest = lax.scan(col_step, first, (d_row[1:], prev_row[1:], prev_row[:-1]))
                row = jnp.concatenate([first[None], rest])
                return (row, row)
            _, rows = lax.scan(row_step, row0, D[1:])
            return jnp.concatenate([row0[None], rows], axis=0)

        def _backtrack(R, T1, T2):
            L = T1 + T2 - 1

            def step(carry, _):
                i, j, done = carry
                valid = jnp.logical_not(done)
                cd = jnp.where((i > 0) & (j > 0), R[jnp.maximum(i - 1, 0), jnp.maximum(j - 1, 0)], BIG)
                cu = jnp.where(i > 0, R[jnp.maximum(i - 1, 0), j], BIG)
                cl = jnp.where(j > 0, R[i, jnp.maximum(j - 1, 0)], BIG)
                choice = jnp.argmin(jnp.stack([cd, cu, cl]))
                ni = jnp.where(choice <= 1, i - 1, i)
                nj = jnp.where((choice == 0) | (choice == 2), j - 1, j)
                at_origin = (i == 0) & (j == 0)
                ni = jnp.where(at_origin, 0, ni)
                nj = jnp.where(at_origin, 0, nj)
                return ((ni, nj, done | at_origin), (i, j, valid))
            init = (jnp.int32(T1 - 1), jnp.int32(T2 - 1), jnp.bool_(False))
            _, (i_idx, j_idx, valid) = lax.scan(step, init, None, length=L)
            return (i_idx, j_idx, valid)

        def _align_one(small, large):
            T_small, d = small.shape
            T_large = large.shape[0]
            D = _pairwise_euclidean(small, large)
            R = _dtw_cost(D)
            i_idx, j_idx, valid = _backtrack(R, T_small, T_large)
            contrib = small[i_idx] * valid[:, None].astype(small.dtype)
            expanded = jnp.zeros((T_large, d), dtype=small.dtype).at[j_idx].add(contrib)
            return expanded
        return jax.vmap(_align_one)(teacher_features, student_features)

    def _L2_ffn_ref(x, Wg, W1, b1, W2, b2):
        import jax, jax.numpy as jnp
        import numpy as np
        D_MODEL, D_FF, N_EXPERTS, TOP_K = (128, 512, 8, 2)
        B = x.shape[:-1]
        xs = x.reshape(-1, x.shape[-1])
        T = xs.shape[0]
        gate_logits = xs @ Wg
        weights, sel = jax.lax.top_k(gate_logits, TOP_K)
        weights = jax.nn.softmax(weights.astype(jnp.float32), axis=1).astype(x.dtype)
        h = jax.nn.relu(jnp.einsum('td,edf->etf', xs, W1) + b1[:, None, :])
        out_e = jnp.einsum('etf,efd->etd', h, W2) + b2[:, None, :]
        tok = jnp.arange(T)
        picked = out_e[sel, tok[:, None]]
        out = jnp.einsum('tk,tkd->td', weights, picked)
        return out.reshape(*B, x.shape[-1])

    def _L3_xattn_ref(query, key, value, mask, Wq, bq, Wk, bk, Wv, bv, Wo, bo):
        import jax, jax.numpy as jnp
        import numpy as np
        import math
        B, S, D, H = (2, 256, 128, 16)
        HD = D // H
        q = jnp.einsum('bsd,hdk->bhsk', query, Wq) + bq[None, :, None, :]
        k = jnp.einsum('bsd,hdk->bhsk', key, Wk) + bk[None, :, None, :]
        v = jnp.einsum('bsd,hdk->bhsk', value, Wv) + bv[None, :, None, :]
        scores = jnp.einsum('bhsk,bhtk->bhst', q, k) / jnp.sqrt(jnp.asarray(HD, q.dtype))
        scores = jnp.where(mask[:, None, :, :] == 0, -jnp.inf, scores)
        attn = jax.nn.softmax(scores, axis=-1)
        ctx = jnp.einsum('bhst,bhtk->bhsk', attn, v)
        x = ctx.transpose(0, 2, 1, 3).reshape(query.shape[0], query.shape[1], D)
        return x @ Wo + bo

    def _L3_ffn_ref(x, packed_weight, weight_scale, bias):
        import jax, jax.numpy as jnp
        import numpy as np
        IN_F = 128
        OUT_F = 128
        B, S = (8, 512)

        def _pack_ternary(tern):
            enc = (tern + 1.0).astype(jnp.int32).reshape(-1)
            return (enc[0::4] | enc[1::4] << 2 | enc[2::4] << 4 | enc[3::4] << 6).astype(jnp.int32)
        n = OUT_F * IN_F
        shifts = jnp.array([0, 2, 4, 6], dtype=jnp.int32)
        enc = (packed_weight[None, :] >> shifts[:, None] & 3).reshape(-1)[:n]
        w = (enc.astype(jnp.float32) - 1.0).reshape(OUT_F, IN_F) * weight_scale
        act_scale = 127.0 / jnp.maximum(jnp.max(jnp.abs(x), axis=-1, keepdims=True), 1e-05)
        x_dq = jnp.clip(jnp.round(x * act_scale), -128.0, 127.0) / act_scale
        return jnp.einsum('bsi,oi->bso', x_dq, w) + bias
    x = x + _L0_xattn_ref(_layernorm(x, axis=-1), ctx_1024, ctx_1024, L0_xattn_query_kernel, L0_xattn_key_kernel, L0_xattn_value_kernel, L0_xattn_projection_kernel, L0_xattn_projection_bias)
    x = x + _L0_ffn_ref(_layernorm(x, axis=-1), L0_ffn_router_w, L0_ffn_up_w, L0_ffn_gate_w, L0_ffn_down_w, L0_ffn_shared_up_w, L0_ffn_shared_gate_w, L0_ffn_shared_down_w)
    x = x + _L1_xattn_ref(_layernorm(x, axis=-1), ctx_1024, ctx_1024, mask_1x1xSxS2_bk0, L1_xattn_Wq, L1_xattn_bq, L1_xattn_Wk, L1_xattn_bk, L1_xattn_Wv, L1_xattn_bv, L1_xattn_Wo, L1_xattn_bo)
    x = x + _L1_ffn_ref(_layernorm(x, axis=-1), L1_ffn_gate_w, L1_ffn_Wg, L1_ffn_Wu, L1_ffn_Wd, L1_ffn_Ws_g, L1_ffn_Ws_u, L1_ffn_Ws_d)
    x = x + _L2_xattn_ref(ctx_1024, _layernorm(x, axis=-1))
    x = x + _L2_ffn_ref(_layernorm(x, axis=-1), L2_ffn_Wg, L2_ffn_W1, L2_ffn_b1, L2_ffn_W2, L2_ffn_b2)
    x = x + _L3_xattn_ref(_layernorm(x, axis=-1), ctx_1024, ctx_1024, mask_BxSxS2_ik0, L3_xattn_Wq, L3_xattn_bq, L3_xattn_Wk, L3_xattn_bk, L3_xattn_Wv, L3_xattn_bv, L3_xattn_Wo, L3_xattn_bo)
    x = x + _L3_ffn_ref(_layernorm(x, axis=-1), L3_ffn_packed_weight, L3_ffn_weight_scale, L3_ffn_bias)
    return x

_drawn_inputs = setup_inputs


def setup_inputs(seed=0):
    import zlib

    import numpy as np

    out = dict(_drawn_inputs(seed))
    spreads = {'L0_xattn_projection_bias': (0.0, 0.1),
     'L1_xattn_bq': (0.0, 0.277),
     'L1_xattn_bk': (0.0, 0.747),
     'L1_xattn_bv': (0.0, 0.1),
     'L1_xattn_bo': (0.0, 0.1),
     'L2_ffn_b1': (0.0, 2.0),
     'L2_ffn_b2': (0.0, 0.714),
     'L3_ffn_bias': (0.0, 0.534)}
    factors = {'L0_xattn_query_kernel': 8.0,
     'L0_xattn_key_kernel': 8.0,
     'L1_ffn_gate_w': 8.0,
     'L1_ffn_Wg': 8.0,
     'L1_ffn_Wu': 8.0,
     'L1_ffn_Wd': 8.0,
     'L1_ffn_Ws_g': 8.0,
     'L1_ffn_Ws_u': 8.0,
     'L1_ffn_Ws_d': 7.795,
     'L3_xattn_bq': 14.359,
     'L3_xattn_bk': 64.0,
     'L2_ffn_Wg': 2.68,
     'L2_ffn_W1': 7.77,
     'L2_ffn_W2': 2.695,
     'L3_xattn_bv': 3.729,
     'L3_xattn_bo': 3.714}
    for name, (base, spread) in spreads.items():
        noise = np.random.default_rng([zlib.crc32(name.encode()), seed]).standard_normal(out[name].shape)
        drawn = base * np.exp(spread * noise) if base else spread * noise
        out[name] = jnp.asarray(drawn.astype(out[name].dtype))
    for name, factor in factors.items():
        out[name] = (out[name] * factor).astype(out[name].dtype)
    return out
```

```python
from contextlib import ExitStack

import concourse.bass as bass
from concourse import mybir

F32 = mybir.dt.float32
BF16 = mybir.dt.bfloat16
U8 = mybir.dt.uint8
U32 = mybir.dt.uint32
I32 = mybir.dt.int32
ALU = mybir.AluOpType
ACT = mybir.ActivationFunctionType
AX = mybir.AxisListType

P = 128
B, S, D = 4, 256, 128
T = S // P
EPS = 1e-5
NEG = -1e30
BIG = 1e30

H = 16
HS0 = 64
HS = 8
C0 = H * HS0 // P
NG = 4

E0, F0 = 8, 512
E1, F1, CAP = 16, 256, 32
E2, F2 = 8, 512
SLOPES = [2.0 ** (-0.5 * (h + 1)) for h in range(H)]

K = 16
W = S // K
LAG = 4
STEPS = S + LAG * (K - 1)
RING = 4 * LAG



def build(nc, x, ctxm, ctxT, mask1, mask3, w, out):
    LN_A, LN_B, XT_B = 5, 3, 2
    XD_A, XD_B = 5, 3
    with ExitStack() as ctx:
        def sb(name, shape, dt=F32):
            return ctx.enter_context(nc.sbuf_tensor(name, shape, dt))

        def sem(name):
            return ctx.enter_context(nc.semaphore(name))

        bank = [ctx.enter_context(nc.psum_tensor(f"bank{i}", [P, 512], F32)) for i in range(8)]
        bS, bT, bO, bLN, bY = bank[0:2], bank[2:4], bank[4:6], bank[6], bank[7]

        X = sb("X", [P, B * T * D])
        CT = sb("CT", [P, B * S])
        XNT = sb("XNT", [P, (B + 1) * S])
        xb = sb("xb", [P, T * D])
        xn = sb("xn", [P, T * D])
        xnT = sb("xnT", [P, S])
        ctb = sb("ctb", [P, S])
        ident = sb("ident", [P, P])
        identb = sb("identb", [P, P], BF16)
        ones = sb("ones", [P, 256])
        rows = sb("rows", [1, 5 * P])
        dmask = sb("dmask", [P, T * S])
        mneg = sb("mneg", [P, T * S])
        mload = dmask[:, :].bitcast(I32)
        m8 = sb("m8", [P, T * S], U8)
        cosT = sb("cosT", [P, S])
        sinT = sb("sinT", [P, S])
        qb1 = sb("qb1", [P, 4 * NG])
        qb3 = sb("qb3", [P, 2 * NG])
        wqk1 = sb("wqk1", [P, 4 * NG * P])
        wvo1 = sb("wvo1", [P, 2 * P])
        rt0 = sb("rt0", [P, E0])
        rt1 = sb("rt1", [P, E1])
        rt2 = sb("rt2", [P, E2])
        b1t = sb("b1t", [P, E2 * 4])
        b2t = sb("b2t", [E2, D])
        iota8 = sb("iota8", [P, 8])
        iota32 = sb("iota32", [P, CAP])
        inj = sb("inj", [P, 1])

        WA = 4 * 1024 + 3 * E0 * F0 + 3 * (E1 + 1) * F1
        arena = sb("arena", [P, WA])
        at = [0]

        def take(n):
            at[0] += n
            assert at[0] <= WA
            return arena[:, at[0] - n:at[0]]

        w0 = [take(1024) for _ in range(4)]
        f0g, f0u, f0d = take(E0 * F0), take(E0 * F0), take(E0 * F0)
        f1g, f1u, f1d = (take((E1 + 1) * F1) for _ in range(3))
        at[0] = 0
        dnat = take(S * W)
        f2d = dnat
        dskew = take(STEPS * W)
        f2u = dskew[:, 0:E2 * F2]
        edge = take(STEPS * W).bitcast(BF16)
        stay = take(STEPS * (W + 1)).bitcast(BF16)
        onc = take(STEPS * W // 2).bitcast(BF16)
        onu = take(S * W // 2).bitcast(BF16)
        onT = take(T * B * S)
        cnat = take(B * T * D)
        wqk3 = take(2 * NG * P)
        wvo3 = take(2 * P)

        work = sb("work", [P, 8192])
        qT, kT, V, cx = (work[:, 2048 * i:2048 * (i + 1)] for i in range(4))
        probs = sb("probs", [P, 2, 512])
        probsT = sb("probsT", [P, 2, 512])
        logit = sb("logit", [P, 2, 512])
        cxT = kT
        hid = qT
        sil = probs
        oneh, wone = kT[:, 0:1024], kT[:, 1024:2048]
        woneT = V[:, 0:1024]
        xgT, eout = V[:, 1024:1536], V[:, 1536:2048]
        stt = sb("stt", [P, T * 6])
        mv = sb("mv", [P, T * 2])
        ve = sb("ve", [P, 8])
        lnv = sb("lnv", [P, 2])
        y0 = sb("y0", [P, 2])
        rstd = sb("rstd", [P, 2])
        nmx = sb("nmx", [P, H * T])
        nmz = sb("nmz", [P, H * T])
        sums = sb("sums", [P, H * T])
        rsum = sb("rsum", [P, H * T])
        lg = sb("lg", [P, T * 16])
        v8 = sb("v8", [P, T * 8])
        ix = sb("ix", [P, T * 8], U32)
        ixf = sb("ixf", [P, T * 8])
        sm = sb("sm", [P, 8])
        coef = sb("coef", [P, T * 16])
        norms = sb("norms", [P, S + W])
        best = sb("best", [P, W])
        pv = sb("pv", [P, 3 * LAG * 2 * (2 * W + 2)], BF16)
        qiT = sb("qiT", [P, S], BF16)
        sel = cx[0:E1, 0:4 * S]
        top = sb("top", [16, 8 * 4])
        slot = sb("slot", [P, T * 16])
        coefT = sb("coefT", [8, S])
        tern = sb("tern", [P, D])
        ternT = sb("ternT", [P, D], BF16)
        pk = sb("pk", [P, D], I32)
        wscale = sb("wscale", [P, 1])
        fb3 = sb("fb3", [P, D])
        qi = sb("qi", [P, T * D], BF16)

        names = """
            ld_first ld_l0 ld_f0 ld_l1 ld_f1 ld_late ld_f2d ld_f2u
            consts ident_zero stored x_back
            x_done ctb_ready var_ready y0_ready xn_ready xnT_full xnT_ready
            p0_full p0_act p0_dve y0_out y1_out y3_out
            p1_full p1_dve p1_act o1_full o1_act p3_full p3_dve p3_act o3_full o3_act
            f0_logit f0_nmax f0_prob f0_gu f0_silu f0_hid f0_down f0_acc
            f1_logit f1_exp f1_score f1_byexp f1_slot f1_slotT f1_oneh f1_wone
            f1_sh_gu f1_sh_gelu f1_sh_hid f1_gath f1_xg f1_gu f1_gelu f1_hid f1_wT f1_wTc f1_down f1_eout f1_y
            f2_logit f2_exp f2_coef f2_cT f2_cTc f2_up f2_hidA f2_hidD f2_down f2_acc f2_y
            mask_loaded mask_used x_out f2_diff sq_ready norms_full norms_ready d_full d_lin d_sq d_root d_done
            skew_set stay_set onu_set pv_set cost_set skewed forward moves_ready backward on_kept unskewed
            identb_ready onT_full onT_ready expanded tern_ready ternT_full ternT_ready f3_q f3_qT f3_qTc f3_y
        """.split()
        for a in ("a0", "a1", "a3"):
            names += [f"{a}_{n}" for n in "scores logit nmax exp pt ptA ptD pv norm".split()]
        sm_ = {n: sem(n) for n in names}
        dve_chain, act_chain, pool_chain = sem("dve_chain"), sem("act_chain"), sem("pool_chain")
        block = ctx.enter_context(nc.Block())

        class Count:

            def __init__(self, eng, b, loop):
                self.eng, self.b, self.loop = eng, b, loop

            def wait(self, name, per, n):
                base = BASE[self.loop].get(name, 0)
                self.eng.wait_ge(sm_[name], self.b * per + (base + n))

        class Chain:

            def __init__(self, eng, s):
                self.eng, self.s, self.n = eng, s, 0

            def restart(self):
                self.eng.sem_clear(self.s)
                self.n = 0

            def __call__(self, ins):
                self.n += 1
                ins.then_inc(self.s, 1)
                self.eng.wait_ge(self.s, self.n)

        BASE = {"A": {}, "B": {n: B * LN_A for n in ("var_ready", "y0_ready", "xn_ready", "xnT_full", "xnT_ready")}
                | {"x_done": B * XD_A, "ctb_ready": B}}

        def v3(ap, c):
            return ap.rearrange("p (a c) -> p a c", c=c)

        def ln_dve(dve, q, link, loop, s):
            per = LN_A if loop == "A" else LN_B
            for t in range(T):
                last = dve.bn_stats(stt[:, 6 * t:6 * t + 6], xb[:, t * D:(t + 1) * D])
            link(last)
            for t in range(T):
                last = dve.bn_aggr(mv[:, 2 * t:2 * t + 2], stt[:, 6 * t:6 * t + 6])
            link(last)
            dve.tensor_scalar(ve[:, 0:2], mv[:, 1:4:2], EPS, None, ALU.add).then_inc(sm_["var_ready"], 1)
            q.wait("var_ready", per, s + 1)
            q.wait("y0_ready", per, s + 1)
            link(dve.tensor_tensor(ve[:, 2:4], y0[:, :], y0[:, :], ALU.mult))
            link(dve.scalar_tensor_tensor(out=ve[:, 4:6], in0=ve[:, 2:4], scalar=-0.5, in1=ve[:, 0:2],
                                          op0=ALU.mult, op1=ALU.mult))
            link(dve.scalar_tensor_tensor(out=rstd[:, :], in0=ve[:, 4:6], scalar=1.5, in1=y0[:, :],
                                          op0=ALU.add, op1=ALU.mult))
            for t in range(T):
                last = dve.tensor_scalar(xn[:, t * D:(t + 1) * D], xb[:, t * D:(t + 1) * D],
                                         mv[:, 2 * t:2 * t + 1], rstd[:, t:t + 1], ALU.subtract, ALU.mult)
            last.then_inc(sm_["xn_ready"], 1)

        def ln_act_rstd(act, q, link, loop, s):
            per = LN_A if loop == "A" else LN_B
            q.wait("var_ready", per, s + 1)
            link(act.activation(lnv[:, :], ve[:, 0:2], ACT.Ln))
            act.activation(y0[:, :], lnv[:, :], ACT.Exp, scale=-0.5).then_inc(sm_["y0_ready"], 1)

        def ln_pe(pe, q, loop, s):
            q.wait("xn_ready", LN_A if loop == "A" else LN_B, s + 1)
            for t in range(T):
                last = pe.transpose(bLN[:, t * P:(t + 1) * P], xn[:, t * D:(t + 1) * D], ident[:, :])
            last.then_inc(sm_["xnT_full"], 1)

        def ln_act_copy(act, q, loop, s):
            q.wait("xnT_full", LN_A if loop == "A" else XT_B, s + 1)
            act.copy(xnT[:, :], bLN[:, 0:S]).then_inc(sm_["xnT_ready"], 1)

        def pt_ready(q, a, hs, g):
            if hs == HS0:
                q.wait(a + ("_ptD" if g % 2 else "_ptA"), H // 2, g // 2 + 1)
            else:
                q.wait(a + "_ptA", H, g + 1)

        def att_pe(pe, q, a, hs):
            def head(tile, h, lo, n):
                if hs == HS0:
                    r, c = (h % 2) * HS0, (h // 2) * S
                else:
                    r, c = (h % 4) * 32, (h // 4) * S
                return tile[r:r + hs, c + lo:c + lo + n]

            for h in range(H + 2):
                if h < H:
                    if h >= 2:
                        q.wait(a + ("_exp" if hs == HS0 else "_logit"), H, h - 1)
                    for n in range(T):
                        last = pe.matmul(bS[h % 2][:, n * S:(n + 1) * S], head(qT, h, n * P, P),
                                         head(kT, h, 0, S), start=True, stop=True)
                    last.then_inc(sm_[a + "_scores"], 1)
                if 1 <= h <= H:
                    g = h - 1
                    q.wait(a + "_exp", H, g + 1)
                    if g >= 2:
                        pt_ready(q, a, hs, g - 2)
                    for m in range(T):
                        for n in range(T):
                            last = pe.transpose(bT[g % 2][:, (m * T + n) * P:(m * T + n + 1) * P],
                                                probs[:, g % 2, n * S + m * P:n * S + (m + 1) * P], ident[:, :])
                    last.then_inc(sm_[a + "_pt"], 1)
                if h >= 2:
                    g = h - 2
                    pt_ready(q, a, hs, g)
                    if hs == HS0:
                        if g % 4 == 0 and g >= 8:
                            q.wait(a + "_norm", H // 4, g // 4 - 1)
                        ob, o, st = bO[(g // 4) % 2], (g % 4) * hs, S
                    else:
                        ob, o, st = bO[0], g * hs, P
                    for n in range(T):
                        for m in range(T):
                            vo = m * H * hs + g * hs
                            last = pe.matmul(ob[:, n * st + o:n * st + o + hs],
                                             probsT[:, g % 2, (m * T + n) * P:(m * T + n + 1) * P],
                                             V[:, vo:vo + hs], start=(m == 0), stop=(m == T - 1))
                    last.then_inc(sm_[a + "_pv"], 1)

        def att_act(act, q, a, hs, scales):
            for h in range(H + 1):
                if h < H:
                    q.wait(a + "_nmax", H, h + 1)
                    if h >= 2:
                        q.wait(a + "_pt", H, h - 1)
                    for n in range(T):
                        src = bS[h % 2][:, n * S:(n + 1) * S] if hs == HS0 else logit[:, h % 2, n * S:(n + 1) * S]
                        last = act.activation(probs[:, h % 2, n * S:(n + 1) * S], src, ACT.Exp,
                                              bias=nmx[:, T * h + n:T * h + n + 1], scale=scales[h],
                                              accum_out=sums[:, T * h + n:T * h + n + 1])
                    last.then_inc(sm_[a + "_exp"], 1)
                if h >= 1 and (hs == HS or h % 2 == 1):
                    g = h - 1
                    q.wait(a + "_pt", H, g + 1)
                    if g >= 2:
                        q.wait(a + "_pv", H, g - 1)
                    act.copy(probsT[:, g % 2, :], bT[g % 2][:, :]).then_inc(sm_[a + "_ptA"], 1)

        def att_dve(dve, q, link, a, hs, scale, slopes, bias):
            for h in range(H + 2):
                if h < H:
                    q.wait(a + "_scores", H, h + 1)
                    nm = nmx[:, T * h:T * h + T]
                    if hs == HS0:
                        dve.tensor_reduce(nm, v3(bS[h % 2][:, :], S), AX.X, ALU.max,
                                          negate=True).then_inc(sm_[a + "_nmax"], 1)
                    else:
                        if h >= 2:
                            q.wait(a + "_exp", H, h - 1)
                        dve.scalar_tensor_tensor(out=logit[:, h % 2, :], in0=bS[h % 2][:, :],
                                                 scalar=scale / slopes[h], in1=bias[:, :],
                                                 op0=ALU.mult, op1=ALU.add).then_inc(sm_[a + "_logit"], 1)
                        q.wait(a + "_logit", H, h + 1)
                        if slopes[h] == 1.0:
                            dve.tensor_reduce(nm, v3(logit[:, h % 2, :], S), AX.X, ALU.max,
                                              negate=True).then_inc(sm_[a + "_nmax"], 1)
                        else:
                            z = nmz[:, T * h:T * h + T]
                            link(dve.tensor_reduce(z, v3(logit[:, h % 2, :], S), AX.X, ALU.max, negate=True))
                            dve.tensor_scalar(nm, z, slopes[h], None, ALU.mult).then_inc(sm_[a + "_nmax"], 1)
                if hs == HS0 and 1 <= h <= H and h % 2 == 0:
                    g = h - 1
                    q.wait(a + "_pt", H, g + 1)
                    if g >= 2:
                        q.wait(a + "_pv", H, g - 1)
                    dve.tensor_copy(probsT[:, g % 2, :], bT[g % 2][:, :]).then_inc(sm_[a + "_ptD"], 1)
                if hs == HS0 and h >= 2 and (h - 2) % 4 == 3:
                    g = (h - 2) // 4
                    q.wait(a + "_pv", H, h - 1)
                    att_norm(dve, link, a, 4 * g, 4, hs, bO[g % 2], S)
            if hs == HS:
                q.wait(a + "_pv", H, H)
                att_norm(dve, link, a, 0, H, hs, bO[0], P)

        def att_norm(dve, link, a, h0, nh, hs, ob, st):
            link(dve.reciprocal(rsum[:, T * h0:T * (h0 + nh)], sums[:, T * h0:T * (h0 + nh)]))
            src = ob[:, 0:T * st].rearrange("p (n c) -> p n c", n=T)[:, :, 0:nh * hs] \
                .rearrange("p n (h o) -> p n h o", o=hs)
            dst = cx[:, 0:T * H * hs].rearrange("p (n h o) -> p n h o", n=T, o=hs)[:, :, h0:h0 + nh, :]
            r = rsum[:, T * h0:T * (h0 + nh)].rearrange("p (h n) -> p n h", n=T)
            for n in range(T):
                last = dve.tensor_tensor(dst[:, n], src[:, n],
                                         r[:, n].unsqueeze(2).to_broadcast([P, nh, hs]), ALU.mult)
            last.then_inc(sm_[a + "_norm"], 1)

        def l0_pe(pe, q):
            banks = [*bS, *bT]
            q.wait("ctb_ready", 1, 1)
            q.wait("x_done", XD_A, 1)
            pe.wait_ge(sm_["ld_l0"], 16 * 4)

            def room(f):
                if f >= 4:
                    q.wait("p0_dve" if (f - 4) % 2 else "p0_act", 8, (f - 4) // 2 + 1)

            def heads(f, wt, src):
                room(f)
                for c in range(2):
                    o = ((f % 4) * 2 + c) * P
                    last = pe.matmul(banks[f % 4][:, c * S:(c + 1) * S], wt[:, o:o + P], src[:, :],
                                     start=True, stop=True)
                last.then_inc(sm_["p0_full"], 1)

            for f in range(4):
                heads(f, w0[1], ctb)
            for f in range(4, 8):
                room(f)
                t, j = (f - 4) // 2, f % 2
                pe.matmul(banks[f % 4][:, :], ctb[:, t * P:(t + 1) * P], w0[2][:, j * 512:(j + 1) * 512],
                          start=True, stop=True).then_inc(sm_["p0_full"], 1)
            ln_pe(pe, q, "A", 0)
            q.wait("xnT_ready", LN_A, 1)
            for f in range(8, 12):
                heads(f, w0[0], xnT)
            q.wait("p0_act", 8, 6)
            q.wait("p0_dve", 8, 6)
            att_pe(pe, q, "a0", HS0)
            q.wait("a0_norm", H // 4, H // 4)
            for f in range(12, 16):
                for c in range(2):
                    for t in range(T):
                        o = t * 1024 + ((f - 12) * 2 + c) * P
                        last = pe.transpose(banks[f % 4][:, c * S + t * P:c * S + (t + 1) * P],
                                            cx[:, o:o + P], ident[:, :])
                last.then_inc(sm_["p0_full"], 1)
            q.wait("p0_act", 8, 8)
            q.wait("p0_dve", 8, 8)
            for t in range(T):
                y = bY[:, t * D:(t + 1) * D]
                for c in range(C0):
                    pe.matmul(y, cxT[:, c * S + t * P:c * S + (t + 1) * P], w0[3][:, c * P:(c + 1) * P],
                              start=(c == 0), stop=False)
                last = pe.matmul(y, ones[0:1, 0:P], rows[0:1, 0:P], start=False, stop=True)
            last.then_inc(sm_["y0_out"], 1)

        def l0_drain(q, f, copy, scaled):
            q.wait("p0_full", 16, f + 1)
            src = [*bS, *bT][f % 4][:, :]
            o = (f % 4) * 512
            if f < 4:
                return copy(kT[:, o:o + 512], src)
            if f < 8:
                return copy(V[:, o:o + 512], src)
            if f < 12:
                return scaled(qT[:, o:o + 512], src)
            return copy(cxT[:, o:o + 512], src)

        def l0_act(act, q, link):
            ln_act_rstd(act, q, link, "A", 0)

            def drain(f):
                l0_drain(q, f, act.copy, lambda o, i: act.mul(o, i, HS0 ** -0.5)).then_inc(sm_["p0_act"], 1)

            for f in (0, 2, 4, 6):
                drain(f)
            ln_act_copy(act, q, "A", 0)
            for f in (8, 10):
                drain(f)
            att_act(act, q, "a0", HS0, [1.0] * H)
            for f in (12, 14):
                drain(f)

        def l0_dve(dve, q, link):
            ln_dve(dve, q, link, "A", 0)

            def drain(f):
                l0_drain(q, f, dve.tensor_copy,
                         lambda o, i: dve.tensor_scalar(o, i, HS0 ** -0.5, None, ALU.mult)) \
                    .then_inc(sm_["p0_dve"], 1)

            for f in (1, 3, 5, 7, 9, 11):
                drain(f)
            att_dve(dve, q, link, "a0", HS0, None, None, None)
            for f in (13, 15):
                drain(f)
            q.wait("y0_out", 1, 1)
            dve.tensor_tensor(xb[:, :], xb[:, :], bY[:, 0:T * D], ALU.add).then_inc(sm_["x_done"], 1)

        def f0_pe(pe, q):
            ln_pe(pe, q, "A", 1)
            q.wait("xnT_ready", LN_A, 2)
            pe.wait_ge(sm_["ld_first"], 16 * N_FIRST)
            for t in range(T):
                last = pe.matmul(bLN[:, 256 + t * 8:264 + t * 8], xnT[:, t * P:(t + 1) * P], rt0[:, :],
                                 start=True, stop=True)
            last.then_inc(sm_["f0_logit"], 1)
            pe.wait_ge(sm_["ld_f0"], 16 * 6)

            def down(e):
                q.wait("f0_hid", 2 * E0, 2 * e + 2)
                if e >= 2:
                    q.wait("f0_acc", E0 - 1, e - 1)
                for t in range(T):
                    for c in range(4):
                        last = pe.matmul(bO[e % 2][:, t * D:(t + 1) * D],
                                         hid[:, (e % 2) * 1024 + c * S + t * P:(e % 2) * 1024 + c * S + (t + 1) * P],
                                         f0d[:, (e * 4 + c) * D:(e * 4 + c + 1) * D], start=(c == 0), stop=(c == 3))
                last.then_inc(sm_["f0_down"], 1)

            for e in range(E0):
                for j in range(2):
                    n = 2 * e + j
                    if n >= 2:
                        q.wait("f0_hid", 2 * E0, n - 1)
                    for wt, bk in ((f0g, bS), (f0u, bT)):
                        for c in range(2):
                            o = e * F0 + (2 * j + c) * P
                            last = pe.matmul(bk[n % 2][:, c * S:(c + 1) * S], wt[:, o:o + P], xnT[:, :],
                                             start=True, stop=True)
                    last.then_inc(sm_["f0_gu"], 1)
                if e:
                    down(e - 1)
            down(E0 - 1)

        def f0_act(act, q, link):
            ln_act_rstd(act, q, link, "A", 1)
            ln_act_copy(act, q, "A", 1)
            q.wait("f0_nmax", 1, 1)
            for t in range(T):
                last = act.activation(v8[:, 8 * t:8 * t + 8], lg[:, 8 * t:8 * t + 8], ACT.Exp,
                                      bias=nmz[:, t:t + 1], accum_out=sm[:, t:t + 1])
            last.then_inc(sm_["f0_prob"], 1)
            for n in range(2 * E0):
                q.wait("f0_gu", 2 * E0, n + 1)
                if n >= 2:
                    q.wait("f0_hid", 2 * E0, n - 1)
                act.activation(sil[:, n % 2, :], bS[n % 2][:, :], ACT.Silu).then_inc(sm_["f0_silu"], 1)

        def top_index(dve, link, ne):
            for t in range(T):
                last = dve.max(v8[:, 8 * t:8 * t + 8], lg[:, ne * t:ne * t + ne])
            link(last)
            for t in range(T):
                last = dve.max_index(ix[:, 8 * t:8 * t + 8], v8[:, 8 * t:8 * t + 8], lg[:, ne * t:ne * t + ne])
            link(last)
            link(dve.tensor_copy(ixf[:, :], ix[:, :]))

        def f0_dve(dve, q, link):
            ln_dve(dve, q, link, "A", 1)
            q.wait("f0_logit", 1, 1)
            link(dve.tensor_copy(lg[:, 0:T * 8], bLN[:, 256:256 + T * 8]))
            top_index(dve, link, E0)
            dve.tensor_scalar(nmz[:, 0:T], v8[:, 0:T * 8:8], -1.0, None, ALU.mult).then_inc(sm_["f0_nmax"], 1)
            q.wait("f0_prob", 1, 1)
            link(dve.reciprocal(sm[:, 2:4], sm[:, 0:2]))
            link(dve.tensor_scalar(sm[:, 4:6], sm[:, 2:4], 2.0, None, ALU.mult))
            for t in range(T):
                last = dve.tensor_scalar(coef[:, 8 * t:8 * t + 8], iota8[:, :], ixf[:, 8 * t:8 * t + 1],
                                         sm[:, 4 + t:5 + t], ALU.is_equal, ALU.mult)
            link(last)
            link(dve.memset(coef[:, 7:16:8], 1.0))
            for n in range(2 * E0 + 2):
                if n < 2 * E0:
                    e, j = n // 2, n % 2
                    q.wait("f0_silu", 2 * E0, n + 1)
                    if e >= 2:
                        q.wait("f0_down", E0, e - 1)
                    o = (e % 2) * 1024 + j * 512
                    dve.tensor_tensor(hid[:, o:o + 512], sil[:, n % 2, :], bT[n % 2][:, :],
                                      ALU.mult).then_inc(sm_["f0_hid"], 1)
                if n >= 2 and n % 2 == 1:
                    e = (n - 2) // 2
                    q.wait("f0_down", E0, e + 1)
                    if e:
                        q.wait("f0_acc", E0 - 1, e)
                    for t in range(T):
                        last = dve.scalar_tensor_tensor(
                            out=xb[:, t * D:(t + 1) * D], in0=bO[e % 2][:, t * D:(t + 1) * D],
                            scalar=coef[:, 8 * t + e:8 * t + e + 1], in1=xb[:, t * D:(t + 1) * D],
                            op0=ALU.mult, op1=ALU.add)
                    last.then_inc(sm_["f0_acc" if e < E0 - 1 else "x_done"], 1)

        def proj(pe, bk, wt, o, src):
            for c in range(2):
                last = pe.matmul(bk[:, c * S:(c + 1) * S], wt[:, o + c * P:o + (c + 1) * P], src[:, :],
                                 start=True, stop=True)
            return last

        def values(pe, bk, wv, brow):
            for t in range(T):
                pe.matmul(bk[:, t * D:(t + 1) * D], ctb[:, t * P:(t + 1) * P], wv, start=True, stop=False)
                last = pe.matmul(bk[:, t * D:(t + 1) * D], ones[0:1, 0:P], rows[0:1, brow * P:(brow + 1) * P],
                                 start=False, stop=True)
            return last

        def attn_out(pe, q, k, wo, brow, name_y):
            q.wait(f"a{k}_norm", 1, 1)
            for t in range(T):
                last = pe.transpose(bLN[:, 256 + t * P:256 + (t + 1) * P], cx[:, t * P:(t + 1) * P], ident[:, :])
            last.then_inc(sm_[f"o{k}_full"], 1)
            q.wait(f"o{k}_act", 1, 1)
            for t in range(T):
                y = bY[:, t * D:(t + 1) * D]
                pe.matmul(y, cx[:, 1024 + t * P:1024 + (t + 1) * P], wo, start=True, stop=False)
                last = pe.matmul(y, ones[0:1, 0:P], rows[0:1, brow * P:(brow + 1) * P], start=False, stop=True)
            last.then_inc(sm_[name_y], 1)

        def attn_out_act(act, q, k):
            q.wait(f"o{k}_full", 1, 1)
            act.copy(cx[:, 1024:1280], bLN[:, 256:512]).then_inc(sm_[f"o{k}_act"], 1)

        def l1_pe(pe, q):
            q.wait("x_done", XD_A, 3)
            pe.wait_ge(sm_["ld_l1"], 16 * 2)

            def pairs(i, wt, src):
                for sw in range(2):
                    last = proj(pe, (bS if i % 2 == 0 else bT)[sw], wqk1, (wt + sw) * NG * P + (i % 2) * 2 * P, src)
                last.then_inc(sm_["p1_full"], 1)

            pairs(0, 2, ctb)
            pairs(1, 2, ctb)
            values(pe, bO[0], wvo1[:, 0:P], 1).then_inc(sm_["p1_full"], 1)
            ln_pe(pe, q, "A", 2)
            q.wait("xnT_ready", LN_A, 3)
            for i in range(2):
                q.wait("p1_dve", 4, i + 1)
                pairs(i, 0, xnT)
            q.wait("p1_dve", 4, 4)
            q.wait("p1_act", 1, 1)
            att_pe(pe, q, "a1", HS)
            attn_out(pe, q, 1, wvo1[:, P:2 * P], 2, "y1_out")

        def l1_act(act, q, link):
            ln_act_rstd(act, q, link, "A", 2)
            q.wait("p1_full", 5, 3)
            act.copy(V[:, 0:T * D], bO[0][:, 0:T * D]).then_inc(sm_["p1_act"], 1)
            ln_act_copy(act, q, "A", 2)
            att_act(act, q, "a1", HS, SLOPES)
            attn_out_act(act, q, 1)

        def l1_dve(dve, q, link):
            ln_dve(dve, q, link, "A", 2)

            def rope(dst, qb, i, full):
                q.wait("p1_full", 5, full)
                bk = bS if i % 2 == 0 else bT
                tmp = [logit[:, 0, :], logit[:, 1, :]] if i == 0 else [cx[:, 0:512], cx[:, 512:1024]]
                for sw, tab in ((0, cosT), (1, sinT)):
                    for c in range(2):
                        g = 2 * i + c
                        last = dve.scalar_tensor_tensor(
                            out=tmp[sw][:, c * S:(c + 1) * S], in0=bk[sw][:, c * S:(c + 1) * S],
                            scalar=qb1[:, (qb + sw) * NG + g:(qb + sw) * NG + g + 1], in1=tab[:, :],
                            op0=ALU.add, op1=ALU.mult)
                link(last)
                dve.tensor_tensor(dst[:, i * 512:(i + 1) * 512], tmp[0], tmp[1],
                                  ALU.add).then_inc(sm_["p1_dve"], 1)

            rope(kT, 2, 0, 1)
            rope(kT, 2, 1, 2)
            rope(qT, 0, 0, 4)
            rope(qT, 0, 1, 5)
            att_dve(dve, q, link, "a1", HS, HS ** -0.5, SLOPES, dmask)
            q.wait("y1_out", 1, 1)
            dve.tensor_tensor(xb[:, :], xb[:, :], bY[:, 0:T * D], ALU.add).then_inc(sm_["x_done"], 1)

        NE = E1 * CAP

        def f1_pe(pe, q):
            ln_pe(pe, q, "A", 3)
            q.wait("xnT_ready", LN_A, 4)
            for t in range(T):
                last = pe.matmul(bLN[:, 256 + t * E1:256 + (t + 1) * E1], xnT[:, t * P:(t + 1) * P], rt1[:, :],
                                 start=True, stop=True)
            last.then_inc(sm_["f1_logit"], 1)
            pe.wait_ge(sm_["ld_f1"], 16 * 3)
            for wt, bk in ((f1g, bT[0]), (f1u, bT[1])):
                for j in range(2):
                    o = E1 * F1 + j * P
                    last = pe.matmul(bk[:, j * S:(j + 1) * S], wt[:, o:o + P], xnT[:, :], start=True, stop=True)
            last.then_inc(sm_["f1_sh_gu"], 1)
            q.wait("f1_score", 1, 1)
            for t in range(T):
                last = pe.transpose(bY[0:E1, t * P:(t + 1) * P], coef[:, t * E1:(t + 1) * E1], ident[:, :])
            last.then_inc(sm_["f1_byexp"], 1)
            q.wait("f1_slot", 1, 1)
            for t in range(T):
                last = pe.matmul(bLN[:, 256 + t * E1:256 + (t + 1) * E1], sel[:, S + t * P:S + (t + 1) * P],
                                 ident[0:E1, 0:E1], start=True, stop=True)
            last.then_inc(sm_["f1_slotT"], 1)
            q.wait("f1_oneh", 1, 1)
            for t in range(T):
                last = pe.matmul(bS[0][:, :], xn[:, t * D:(t + 1) * D], oneh[:, t * NE:(t + 1) * NE],
                                 start=(t == 0), stop=(t == T - 1))
            last.then_inc(sm_["f1_gath"], 1)
            q.wait("f1_sh_hid", 1, 1)
            q.wait("f1_wone", 1, 1)
            for g in range(4):
                for t in range(T):
                    last = pe.transpose(bT[g // 2][:, (g % 2) * S + t * P:(g % 2) * S + (t + 1) * P],
                                        wone[:, t * NE + g * P:t * NE + (g + 1) * P], ident[:, :])
            last.then_inc(sm_["f1_wT"], 1)
            q.wait("f1_xg", 1, 1)
            for j in range(2):
                for wt, bk in ((f1g, bS), (f1u, bO)):
                    for e in range(E1):
                        o = e * F1 + j * P
                        last = pe.matmul(bk[j][:, e * CAP:(e + 1) * CAP], wt[:, o:o + P],
                                         xgT[:, e * CAP:(e + 1) * CAP], start=True, stop=True)
                last.then_inc(sm_["f1_gu"], 1)
            q.wait("f1_hid", 2, 2)
            for e in range(E1):
                r = 32 * (e % 4)
                for j in range(2):
                    o = 512 + j * 512 + e * CAP
                    last = pe.matmul(bLN[r:r + CAP, (e // 4) * D:(e // 4 + 1) * D], hid[:, o:o + CAP],
                                     f1d[:, (e * 2 + j) * D:(e * 2 + j + 1) * D], start=(j == 0), stop=(j == 1))
            last.then_inc(sm_["f1_down"], 1)
            q.wait("f1_eout", 1, 1)
            q.wait("f1_wTc", 1, 1)
            for t in range(T):
                y = bY[:, t * D:(t + 1) * D]
                for j in range(2):
                    pe.matmul(y, hid[:, j * S + t * P:j * S + (t + 1) * P],
                              f1d[:, (2 * E1 + j) * D:(2 * E1 + j + 1) * D], start=(j == 0), stop=False)
                for g in range(4):
                    last = pe.matmul(y, woneT[:, g * S + t * P:g * S + (t + 1) * P], eout[:, g * D:(g + 1) * D],
                                     start=False, stop=(g == 3))
            last.then_inc(sm_["f1_y"], 1)

        def f1_act(act, q, link):
            ln_act_rstd(act, q, link, "A", 3)
            ln_act_copy(act, q, "A", 3)
            q.wait("f1_logit", 2, 2)
            for t in range(T):
                last = act.activation(lg[:, t * E1:(t + 1) * E1], bLN[:, 256 + t * E1:256 + (t + 1) * E1], ACT.Exp,
                                      bias=nmz[:, t:t + 1], accum_out=sm[:, t:t + 1])
            last.then_inc(sm_["f1_exp"], 1)
            q.wait("f1_sh_gu", 1, 1)
            act.activation(sil[:, 0, :], bT[0][:, :], ACT.Gelu).then_inc(sm_["f1_sh_gelu"], 1)
            q.wait("f1_gath", 1, 1)
            act.copy(xgT, bS[0][:, :]).then_inc(sm_["f1_xg"], 1)
            q.wait("f1_wT", 1, 1)
            for i in range(2):
                last = act.copy(woneT[:, i * 512:(i + 1) * 512], bT[i][:, :])
            last.then_inc(sm_["f1_wTc"], 1)
            for j in range(2):
                q.wait("f1_gu", 2, j + 1)
                if j == 0:
                    q.wait("f1_sh_hid", 1, 1)
                act.activation(sil[:, j, :], bS[j][:, :], ACT.Gelu).then_inc(sm_["f1_gelu"], 1)
            q.wait("f1_down", 1, 1)
            act.copy(eout, bLN[:, :]).then_inc(sm_["f1_eout"], 1)

        def f1_dve(dve, q, link):
            ln_dve(dve, q, link, "A", 3)
            q.wait("f1_logit", 2, 1)
            dve.tensor_reduce(nmz[:, 0:T], v3(bLN[:, 256:256 + T * E1], E1), AX.X, ALU.max,
                              negate=True).then_inc(sm_["f1_logit"], 1)
            q.wait("f1_exp", 1, 1)
            link(dve.reciprocal(sm[:, 2:4], sm[:, 0:2]))
            for t in range(T):
                last = dve.tensor_scalar(coef[:, t * E1:(t + 1) * E1], lg[:, t * E1:(t + 1) * E1],
                                         sm[:, 2 + t:3 + t], None, ALU.mult)
            last.then_inc(sm_["f1_score"], 1)
            q.wait("f1_sh_gelu", 1, 1)
            dve.tensor_tensor(hid[:, 0:512], sil[:, 0, :], bT[1][:, :], ALU.mult).then_inc(sm_["f1_sh_hid"], 1)
            q.wait("f1_byexp", 1, 1)
            link(dve.tensor_copy(sel[:, 0:S], bY[0:E1, 0:S]))
            for r in range(CAP // 8):
                cur, nxt = sel[:, (r % 2) * S:(r % 2 + 1) * S], sel[:, ((r + 1) % 2) * S:((r + 1) % 2 + 1) * S]
                link(dve.max(top[:, 8 * r:8 * r + 8], cur))
                link(dve.match_replace(nxt, top[:, 8 * r:8 * r + 8], cur, -1.0))
            link(dve.tensor_scalar(sel[:, 2 * S:3 * S], sel[:, 0:S], 0.0, None, ALU.is_lt))
            link(dve.tensor_tensor_scan(sel[:, 3 * S:4 * S], ones[0:E1, 0:S], sel[:, 2 * S:3 * S], 0.0,
                                        ALU.mult, ALU.add))
            dve.tensor_tensor(sel[:, S:2 * S], sel[:, 2 * S:3 * S], sel[:, 3 * S:4 * S],
                              ALU.mult).then_inc(sm_["f1_slot"], 1)
            q.wait("f1_slotT", 1, 1)
            link(dve.tensor_copy(slot[:, :], bLN[:, 256:256 + T * E1]))
            o3, w3 = v3(oneh, CAP), v3(wone, CAP)
            dve.tensor_tensor(o3, slot[:, :].unsqueeze(2).to_broadcast([P, T * E1, CAP]),
                              iota32[:, :].unsqueeze(1).to_broadcast([P, T * E1, CAP]),
                              ALU.is_equal).then_inc(sm_["f1_oneh"], 1)
            q.wait("f1_oneh", 1, 1)
            dve.tensor_tensor(w3, o3, coef[:, 0:T * E1].unsqueeze(2).to_broadcast([P, T * E1, CAP]),
                              ALU.mult).then_inc(sm_["f1_wone"], 1)
            for j in range(2):
                q.wait("f1_gelu", 2, j + 1)
                dve.tensor_tensor(hid[:, 512 * (j + 1):512 * (j + 2)], sil[:, j, :], bO[j][:, :],
                                  ALU.mult).then_inc(sm_["f1_hid"], 1)
            q.wait("f1_y", 1, 1)
            dve.tensor_tensor(xb[:, :], xb[:, :], bY[:, 0:T * D], ALU.add).then_inc(sm_["x_done"], 1)

        banks4 = [*bS, *bT]
        sqc, sqx = work[:, 0:B * S], work[:, 1024:1024 + (B + 1) * S]
        dlin = [work[:, 2304 + i * 512:2816 + i * 512] for i in range(2)]
        dsq = [work[:, 3328 + i * 512:3840 + i * 512] for i in range(2)]
        root = [work[:, 4352 + i * 512:4864 + i * 512] for i in range(2)]
        dtmp = work[:, 5376:5888]
        NROUND = W // 2
        NGRP = STEPS // LAG
        BW = W + 1
        SW = 2 * W + 2
        PW = 2 * W + 2
        PR = 3 * LAG
        cost = work[:, 0:(STEPS + 1) * BW]
        chs = work[:, 6144:6144 + 3 * 4 * LAG * W]
        chb = work[:, 7168:7168 + 2 * 4 * LAG * W].bitcast(BF16)
        cost3 = cost.rearrange("p (s c) -> p s c", c=BW)
        edge4 = edge.rearrange("p (s c q) -> p s c q", c=W, q=2)
        stay3 = stay.rearrange("p (s c) -> p s c", c=SW)
        onc3 = onc.rearrange("p (s c) -> p s c", c=W)

        def dist_pe(pe):
            pe.wait_ge(sm_["sq_ready"], 2)
            for b in range(B):
                last = pe.matmul(bY[32 * b:32 * b + 32, 0:S], ones[:, 0:32], sqc[:, b * S:(b + 1) * S],
                                 start=True, stop=True)
            for b in range(B):
                for c in range(W):
                    o = b * S + c
                    last = pe.matmul(bY[32 * b:32 * b + 32, S + c:S + c + 1], sqx[:, o:o + 31 * W + 1:W],
                                     ones[:, 0:1], start=True, stop=True)
            last.then_inc(sm_["norms_full"], 1)
            for r in range(NROUND):
                if r >= 4:
                    pe.wait_ge(sm_["d_lin"], r - 3)
                for b in range(B):
                    for c in range(2):
                        o = b * S + 2 * r + c
                        last = pe.matmul(banks4[r % 4][32 * b:32 * b + 32, c * S:(c + 1) * S],
                                         XNT[:, o:o + 31 * W + 1:W], CT[:, b * S:(b + 1) * S],
                                         start=True, stop=True)
                last.then_inc(sm_["d_full"], 1)

        def dist_dve(dve, link):
            dve.wait_ge(sm_["norms_full"], 1)
            link(dve.tensor_copy(norms[:, :], bY[:, 0:S + W]))
            dve.sem_inc(sm_["norms_ready"], 1)
            dn = dnat.rearrange("p (i c) -> p c i", c=W)
            for r in range(NROUND + 1):
                if r < NROUND:
                    dve.wait_ge(sm_["d_full"], r + 1)
                    for c in range(2):
                        last = dve.scalar_tensor_tensor(out=dlin[r % 2][:, c * S:(c + 1) * S],
                                                        in0=banks4[r % 4][:, c * S:(c + 1) * S], scalar=-2.0,
                                                        in1=norms[:, 0:S], op0=ALU.mult, op1=ALU.add)
                    last.then_inc(sm_["d_lin"], 1)
                if r:
                    p = r - 1
                    dve.wait_ge(sm_["d_root"], p + 1)
                    link(dve.reciprocal(dtmp, root[p % 2]))
                    link(dve.tensor_tensor(dtmp, dtmp, dsq[p % 2], ALU.mult))
                    link(dve.tensor_tensor(dtmp, dtmp, root[p % 2], ALU.add))
                    dve.tensor_scalar(dn[:, 2 * p:2 * p + 2, :], dtmp.rearrange("p (c i) -> p c i", c=2), 0.5,
                                      None, ALU.mult).then_inc(sm_["d_done"], 1)
                    dve.wait_ge(sm_["d_done"], p + 1)

        def dist_pool(pool):
            pool.memset(dskew, BIG).then_inc(sm_["skew_set"], 1)
            pool.memset(stay, 1.0).then_inc(sm_["stay_set"], 1)
            pool.memset(onu, 0.0).then_inc(sm_["onu_set"], 1)
            pool.memset(pv[:, :], 0.0).then_inc(sm_["pv_set"], 1)
            pool.wait_ge(sm_["norms_ready"], 1)
            for r in range(NROUND):
                pool.wait_ge(sm_["d_lin"], r + 1)
                if r >= 2:
                    pool.wait_ge(sm_["d_done"], r - 1)
                for c in range(2):
                    w_ = S + 2 * r + c
                    last = pool.tensor_scalar(dsq[r % 2][:, c * S:(c + 1) * S], dlin[r % 2][:, c * S:(c + 1) * S],
                                              norms[:, w_:w_ + 1], 1e-30, ALU.add, ALU.max)
                last.then_inc(sm_["d_sq"], 1)
            pool.wait_ge(sm_["d_done"], NROUND)
            pool.memset(cost3[:, 0:1, :], BIG).then_inc(sm_["cost_set"], 1)
            pool.memset(cost3[:, 1:1 + LAG, 0:1], BIG).then_inc(sm_["cost_set"], 1)
            pool.wait_ge(sm_["cost_set"], 2)
            for b in range(B):
                pool.memset(cost[32 * b:32 * b + 1, 0:1], 0.0).then_inc(sm_["cost_set"], 1)

        def dist_act(act):
            act.activation(sqx, XNT[:, :], ACT.Square).then_inc(sm_["sq_ready"], 1)
            act.activation(sqc, CT[:, :], ACT.Square).then_inc(sm_["sq_ready"], 1)
            for r in range(NROUND):
                act.wait_ge(sm_["d_sq"], r + 1)
                act.activation(root[r % 2], dsq[r % 2], ACT.Sqrt).then_inc(sm_["d_root"], 1)

        def forward_dve(dve, link):
            dve.wait_ge(sm_["skewed"], 16 * K)
            dve.wait_ge(sm_["cost_set"], 2 + B)
            for g in range(NGRP):
                for s in range(g * LAG, (g + 1) * LAG):
                    link(dve.tensor_tensor(best[:, :], cost3[:, s, 1:BW], cost3[:, s, 0:W], ALU.min))
                    link(dve.tensor_tensor_scan(cost3[:, s + 1, 1:BW], best[:, :], dskew[:, s * W:(s + 1) * W],
                                                cost3[:, s + 1, 0:1], ALU.min, ALU.add))
                if g < NGRP - 1:
                    a = g * LAG + 1
                    dve.stream_shuffle(cost3[:, a + LAG:a + 2 * LAG, 0], cost3[:, a:a + LAG, W],
                                       [31, *range(31)]).then_inc(sm_["forward"], 1)
                    dve.wait_ge(sm_["forward"], g + 1)
                else:
                    dve.sem_inc(sm_["forward"], 1)

        CH = 4 * LAG

        def moves_pool(pool):
            n = 0
            for lo in range(0, STEPS, CH):
                r = min(CH, STEPS - lo)
                pool.wait_ge(sm_["forward"], (lo + r) // LAG)
                if lo == 0:
                    pool.wait_ge(sm_["stay_set"], 1)
                up, diag = cost3[:, lo:lo + r, 1:BW], cost3[:, lo:lo + r, 0:W]
                left = cost3[:, lo + 1:lo + 1 + r, 0:W]
                v4 = chs[:, 0:3 * r * W].rearrange("p (n s c) -> p n s c", n=3, c=W)
                pool.tensor_tensor(v4[:, 0], up, left, ALU.subtract)
                pool.tensor_tensor(v4[:, 1], diag, up, ALU.subtract)
                pool.tensor_tensor(v4[:, 2], diag, left, ALU.subtract).then_inc(pool_chain, 1)
                pool.wait_ge(pool_chain, 5 * n + 1)
                f3, d3 = chb[:, 0:3 * r * W], chs[:, 0:3 * r * W]
                pool.tensor_scalar(f3, d3, 0.0, None, ALU.is_le).then_inc(pool_chain, 1)
                pool.wait_ge(pool_chain, 5 * n + 2)
                m, g1, g2 = (chb[:, i * r * W:(i + 1) * r * W].rearrange("p (s c) -> p s c", c=W) for i in range(3))
                by_diag, by_up = edge4[:, lo:lo + r, ::-1, 1], edge4[:, lo:lo + r, ::-1, 0]
                pool.tensor_tensor(by_diag, g1, g2, ALU.mult).then_inc(pool_chain, 1)
                pool.wait_ge(pool_chain, 5 * n + 3)
                other = chb[:, 3 * r * W:4 * r * W].rearrange("p (s c) -> p s c", c=W)
                pool.tensor_scalar(other, by_diag, -1.0, 1.0, ALU.mult, ALU.add).then_inc(pool_chain, 1)
                pool.wait_ge(pool_chain, 5 * n + 4)
                pool.tensor_tensor(by_up, m, other, ALU.mult).then_inc(pool_chain, 1)
                pool.wait_ge(pool_chain, 5 * n + 5)
                pool.tensor_tensor(stay3[:, lo:lo + r, SW - 2:0:-2], other, by_up,
                                   ALU.subtract).then_inc(sm_["moves_ready"], 1)
                n += 1
                pool.wait_ge(sm_["moves_ready"], n)

        def backward_dve(dve, link):
            dve.wait_ge(sm_["moves_ready"], -(-STEPS // CH))
            dve.wait_ge(sm_["pv_set"], 1)
            n = STEPS - LAG
            link(dve.stream_shuffle(stay3[:, 0:n, 0], stay3[:, LAG:STEPS, SW - 2], [*range(1, 32), 31]))
            link(dve.memset(stay3[:, n:STEPS, 0:1], 0.0))
            link(dve.tensor_copy(stay3[:, STEPS - 1, 0:1], inj[:, :]))
            pv4 = pv[:, :].rearrange("p (s q c) -> p s q c", q=2, c=PW)
            link(dve.tensor_copy(pv4[:, (STEPS - 1) % PR, 0, 0:1], inj[:, :]))
            for i, g in enumerate(reversed(range(NGRP))):
                if i >= 3:
                    dve.wait_ge(sm_["on_kept"], i - 2)
                for s in reversed(range(g * LAG, (g + 1) * LAG)):
                    r, nx = s % PR, (s + 1) % PR
                    link(dve.tensor_tensor_scan(pv4[:, r, 0, 1:2 * W + 1], stay3[:, s, 0:2 * W],
                                                pv4[:, nx, 1, 0:2 * W], pv4[:, r, 0, 0:1], ALU.mult, ALU.add))
                    link(dve.tensor_tensor(pv4[:, r, 1, 1:2 * W + 1].rearrange("p (c q) -> p c q", q=2),
                                           edge4[:, s], pv4[:, r, 0, 2:2 * W + 2:2].unsqueeze(2)
                                           .to_broadcast([P, W, 2]), ALU.mult))
                if g:
                    a, z = (g * LAG) % PR, ((g - 1) * LAG) % PR
                    dve.stream_shuffle(pv4[:, z:z + LAG, :, 0], pv4[:, a:a + LAG, :, 2 * W],
                                       [*range(1, 32), 31]).then_inc(sm_["backward"], 1)
                    dve.wait_ge(sm_["backward"], i + 1)
                else:
                    dve.sem_inc(sm_["backward"], 1)

        def backward_act(act):
            pv4 = pv[:, :].rearrange("p (s q c) -> p s q c", q=2, c=PW)
            for i, g in enumerate(reversed(range(NGRP))):
                act.wait_ge(sm_["backward"], i + 1)
                a = (g * LAG) % PR
                act.copy(onc3[:, g * LAG:(g + 1) * LAG, :],
                         pv4[:, a:a + LAG, 0, 2:2 * W + 2:2]).then_inc(sm_["on_kept"], 1)

        def expand_pe(pe):
            pe.wait_ge(sm_["unskewed"], 16 * K)
            pe.wait_ge(sm_["identb_ready"], 1)
            for n in range(4):
                for c in range(W // 2):
                    o = (n // 2) * P * W + W - 1 - ((n % 2) * (W // 2) + c)
                    last = pe.transpose(banks4[n][:, :].bitcast(BF16)[:, c * P:(c + 1) * P],
                                        onu[:, o:o + (P - 1) * W + 1:W], identb[:, :])
                last.then_inc(sm_["onT_full"], 1)
            pe.wait_ge(sm_["onT_ready"], 4)
            pe.wait_ge(sm_["ld_late"], 16 * N_LATE)
            for b in range(B):
                for jt in range(T):
                    for h in range(T):
                        o = (h * B + b) * S + jt * P
                        last = pe.matmul(bO[b // 2][:, ((b % 2) * T + jt) * D:((b % 2) * T + jt + 1) * D],
                                         onT[:, o:o + P], cnat[:, (b * T + h) * D:(b * T + h + 1) * D],
                                         start=(h == 0), stop=(h == T - 1))
            last.then_inc(sm_["expanded"], 1)

        def expand_dve(dve, link):
            for n in range(4):
                dve.wait_ge(sm_["onT_full"], n + 1)
                src = banks4[n][:, :].bitcast(BF16).rearrange("p (c b k) -> p c b k", b=B, k=32)
                h = n // 2
                dst = onT[:, h * B * S:(h + 1) * B * S].rearrange("p (b k c) -> p b k c", b=B, c=W)
                for b in range(B):
                    last = dve.tensor_copy(dst[:, b, :, (n % 2) * (W // 2):(n % 2 + 1) * (W // 2)],
                                           src[:, :, b, 0:K].rearrange("p c k -> p k c"))
                last.then_inc(sm_["onT_ready"], 1)
            dve.wait_ge(sm_["expanded"], 1)
            for i in range(2):
                v = X[:, i * 512:(i + 1) * 512]
                last = dve.tensor_tensor(v, v, bO[i][:, :], ALU.add)
            link(last)

        def f2_pe(pe, q):
            ln_pe(pe, q, "B", 0)
            q.wait("xnT_ready", XT_B, 1)
            for t in range(T):
                last = pe.matmul(bLN[:, 256 + t * 8:264 + t * 8], xnT[:, t * P:(t + 1) * P], rt2[:, :],
                                 start=True, stop=True)
            last.then_inc(sm_["f2_logit"], 1)
            pe.wait_ge(sm_["ld_f2d"], 16)
            pe.wait_ge(sm_["ld_f2u"], 16)

            def down(e):
                q.wait("f2_hidA", E2, e + 1)
                q.wait("f2_hidD", E2, e + 1)
                if e >= 2:
                    q.wait("f2_acc", E2, e - 1)
                for t in range(T):
                    for c in range(4):
                        o = (e % 2) * 1024 + c * S + t * P
                        last = pe.matmul(bO[e % 2][:, t * D:(t + 1) * D], hid[:, o:o + P],
                                         f2d[:, (e * 4 + c) * D:(e * 4 + c + 1) * D], start=(c == 0), stop=(c == 3))
                last.then_inc(sm_["f2_down"], 1)

            for e in range(E2):
                for j in range(2):
                    n = 2 * e + j
                    if n >= 4:
                        q.wait("f2_hidD" if j else "f2_hidA", E2, e - 1)
                    for c in range(2):
                        o = e * F2 + (2 * j + c) * P
                        last = pe.matmul(banks4[n % 4][:, c * S:(c + 1) * S], f2u[:, o:o + P], xnT[:, :],
                                         start=True, stop=True)
                    last.then_inc(sm_["f2_up"], 1)
                if e == 1:
                    q.wait("f2_coef", 1, 1)
                    for t in range(T):
                        last = pe.transpose(bLN[0:E2, t * P:(t + 1) * P], coef[:, 8 * t:8 * t + 8], ident[:, :])
                    last.then_inc(sm_["f2_cT"], 1)
                if e:
                    down(e - 1)
            down(E2 - 1)
            q.wait("f2_cTc", 1, 1)
            for t in range(T):
                last = pe.matmul(bY[:, t * D:(t + 1) * D], coefT[:, t * P:(t + 1) * P], b2t[:, :],
                                 start=True, stop=True)
            last.then_inc(sm_["f2_y"], 1)

        def f2_act(act, q, link):
            ln_act_rstd(act, q, link, "B", 0)
            ln_act_copy(act, q, "B", 0)
            q.wait("f2_diff", 1, 1)
            act.activation(sm[:, 2:4], sm[:, 0:2], ACT.Exp).then_inc(sm_["f2_exp"], 1)
            for e in range(E2):
                if e == 2:
                    q.wait("f2_cT", 1, 1)
                    act.copy(coefT[:, :], bLN[0:E2, 0:S]).then_inc(sm_["f2_cTc"], 1)
                q.wait("f2_up", 2 * E2, 2 * e + 1)
                if e >= 2:
                    q.wait("f2_down", E2, e - 1)
                for c in range(2):
                    o = (e % 2) * 1024 + c * S
                    last = act.activation(hid[:, o:o + S], banks4[(2 * e) % 4][:, c * S:(c + 1) * S], ACT.Relu,
                                          bias=b1t[:, e * 4 + c:e * 4 + c + 1])
                last.then_inc(sm_["f2_hidA"], 1)

        def f2_dve(dve, q, link):
            ln_dve(dve, q, link, "B", 0)
            q.wait("f2_logit", 1, 1)
            link(dve.tensor_copy(lg[:, 0:T * 8], bLN[:, 256:256 + T * 8]))
            top_index(dve, link, E2)
            dve.tensor_tensor(sm[:, 0:2], v8[:, 1:T * 8:8], v8[:, 0:T * 8:8],
                              ALU.subtract).then_inc(sm_["f2_diff"], 1)
            q.wait("f2_exp", 1, 1)
            link(dve.tensor_scalar(sm[:, 4:6], sm[:, 2:4], 1.0, None, ALU.add))
            link(dve.reciprocal(sm[:, 6:8], sm[:, 4:6]))
            link(dve.tensor_tensor(sm[:, 4:6], sm[:, 2:4], sm[:, 6:8], ALU.mult))
            for t in range(T):
                dve.tensor_scalar(coef[:, 8 * t:8 * t + 8], iota8[:, :], ixf[:, 8 * t:8 * t + 1],
                                  sm[:, 6 + t:7 + t], ALU.is_equal, ALU.mult)
                last = dve.tensor_scalar(coef[:, 16 + 8 * t:24 + 8 * t], iota8[:, :], ixf[:, 8 * t + 1:8 * t + 2],
                                         sm[:, 4 + t:5 + t], ALU.is_equal, ALU.mult)
            link(last)
            dve.tensor_tensor(coef[:, 0:16], coef[:, 0:16], coef[:, 16:32], ALU.add).then_inc(sm_["f2_coef"], 1)
            q.wait("f2_coef", 1, 1)
            for e in range(E2 + 2):
                if e < E2:
                    q.wait("f2_up", 2 * E2, 2 * e + 2)
                    if e >= 2:
                        q.wait("f2_down", E2, e - 1)
                    for c in range(2):
                        o = (e % 2) * 1024 + (2 + c) * S
                        last = dve.tensor_scalar(hid[:, o:o + S], banks4[(2 * e + 1) % 4][:, c * S:(c + 1) * S],
                                                 b1t[:, e * 4 + 2 + c:e * 4 + 3 + c], 0.0, ALU.add, ALU.max)
                    last.then_inc(sm_["f2_hidD"], 1)
                if 1 <= e <= E2:
                    p = e - 1
                    q.wait("f2_down", E2, p + 1)
                    if p:
                        q.wait("f2_acc", E2, p)
                    for t in range(T):
                        last = dve.scalar_tensor_tensor(
                            out=xb[:, t * D:(t + 1) * D], in0=bO[p % 2][:, t * D:(t + 1) * D],
                            scalar=coef[:, 8 * t + p:8 * t + p + 1], in1=xb[:, t * D:(t + 1) * D],
                            op0=ALU.mult, op1=ALU.add)
                    last.then_inc(sm_["f2_acc"], 1)
            q.wait("f2_acc", E2, E2)
            q.wait("f2_y", 1, 1)
            dve.tensor_tensor(xb[:, :], xb[:, :], bY[:, 0:T * D], ALU.add).then_inc(sm_["x_done"], 1)

        def l3_pe(pe, q):
            q.wait("ctb_ready", 1, 1)
            q.wait("x_done", XD_B, 2)
            proj(pe, bS[0], wqk3, NG * P, ctb)
            proj(pe, bT[0], wqk3, NG * P + 2 * P, ctb)
            values(pe, bO[0], wvo3[:, 0:P], 3).then_inc(sm_["p3_full"], 1)
            ln_pe(pe, q, "B", 1)
            q.wait("xnT_ready", XT_B, 2)
            proj(pe, bS[1], wqk3, 0, xnT)
            proj(pe, bT[1], wqk3, 2 * P, xnT).then_inc(sm_["p3_full"], 1)
            q.wait("p3_act", 1, 1)
            q.wait("p3_dve", 1, 1)
            att_pe(pe, q, "a3", HS)
            attn_out(pe, q, 3, wvo3[:, P:2 * P], 4, "y3_out")

        def l3_act(act, q, link):
            ln_act_rstd(act, q, link, "B", 1)
            q.wait("p3_full", 2, 1)
            for g in range(NG):
                act.activation(kT[:, g * S:(g + 1) * S], (bS, bT)[g // 2][0][:, (g % 2) * S:(g % 2 + 1) * S],
                               ACT.Identity, bias=qb3[:, NG + g:NG + g + 1])
            act.copy(V[:, 0:T * D], bO[0][:, 0:T * D]).then_inc(sm_["p3_act"], 1)
            ln_act_copy(act, q, "B", 1)
            att_act(act, q, "a3", HS, [1.0] * H)
            attn_out_act(act, q, 3)

        def l3_dve(dve, q, link):
            ln_dve(dve, q, link, "B", 1)
            q.wait("mask_loaded", 16, 16)
            dve.tensor_scalar(mneg[:, :], mload, 0.0, NEG, ALU.is_equal, ALU.mult).then_inc(sm_["mask_used"], 1)
            q.wait("p3_full", 2, 2)
            for g in range(NG):
                last = dve.tensor_scalar(qT[:, g * S:(g + 1) * S],
                                         (bS, bT)[g // 2][1][:, (g % 2) * S:(g % 2 + 1) * S],
                                         qb3[:, g:g + 1], None, ALU.add)
            last.then_inc(sm_["p3_dve"], 1)
            q.wait("p3_dve", 1, 1)
            att_dve(dve, q, link, "a3", HS, HS ** -0.5, [1.0] * H, mneg)
            q.wait("y3_out", 1, 1)
            dve.tensor_tensor(xb[:, :], xb[:, :], bY[:, 0:T * D], ALU.add).then_inc(sm_["x_done"], 1)

        def tern_dve(dve, link):
            dve.wait_ge(sm_["ld_first"], 16 * N_FIRST)
            for s in range(4):
                p = pk[32 * s:32 * s + 32, :]
                last = dve.tensor_scalar(p, p, 2 * s, 3, ALU.logical_shift_right, ALU.bitwise_and)
            link(last)
            dve.tensor_scalar(tern[:, :], pk[:, :], 1.0, None, ALU.subtract).then_inc(sm_["tern_ready"], 1)
            dve.wait_ge(sm_["ternT_full"], 1)
            dve.tensor_copy(ternT[:, :], bY[:, 0:D]).then_inc(sm_["ternT_ready"], 1)

        def tern_pe(pe):
            pe.wait_ge(sm_["tern_ready"], 1)
            pe.transpose(bY[:, 0:D], tern[:, :], ident[:, :]).then_inc(sm_["ternT_full"], 1)
            pe.wait_ge(sm_["ternT_ready"], 1)

        def f3_pe(pe, q):
            q.wait("f3_q", 1, 1)
            qp = bLN[:, :].bitcast(BF16)
            for t in range(T):
                last = pe.transpose(qp[:, t * P:(t + 1) * P], qi[:, t * D:(t + 1) * D], identb[:, :])
            last.then_inc(sm_["f3_qT"], 1)
            q.wait("f3_qTc", 1, 1)
            for t in range(T):
                last = pe.matmul(bY[:, t * D:(t + 1) * D], qiT[:, t * P:(t + 1) * P], ternT[:, :],
                                 start=True, stop=True)
            last.then_inc(sm_["f3_y"], 1)

        def f3_act(act, q, link):
            ln_act_rstd(act, q, link, "B", 2)
            q.wait("f3_qT", 1, 1)
            act.copy(qiT[:, :], bLN[:, :].bitcast(BF16)[:, 0:S]).then_inc(sm_["f3_qTc"], 1)

        ROUND = 1.5 * 2.0 ** 23

        def f3_dve(dve, q, link, b):
            ln_dve(dve, q, link, "B", 2)
            q.wait("xn_ready", LN_B, 3)
            link(dve.tensor_reduce(sm[:, 0:2], v3(xn[:, :], D), AX.X, ALU.max, apply_absolute_value=True))
            link(dve.tensor_scalar(sm[:, 2:4], sm[:, 0:2], 1e-5, None, ALU.max))
            link(dve.reciprocal(sm[:, 4:6], sm[:, 2:4]))
            link(dve.tensor_scalar(sm[:, 0:2], sm[:, 4:6], 127.0, None, ALU.mult))
            for t in range(T):
                last = dve.tensor_scalar(cx[:, t * D:(t + 1) * D], xn[:, t * D:(t + 1) * D], sm[:, t:t + 1],
                                         ROUND, ALU.mult, ALU.add)
            link(last)
            link(dve.tensor_scalar(cx[:, 512:512 + T * D], cx[:, 0:T * D], ROUND, 127.0, ALU.subtract, ALU.min))
            dve.tensor_scalar(qi[:, :], cx[:, 512:512 + T * D], -128.0, None, ALU.max).then_inc(sm_["f3_q"], 1)
            link(dve.tensor_scalar(sm[:, 4:6], sm[:, 2:4], wscale[:, 0:1], 1.0 / 127.0, ALU.mult, ALU.mult))
            q.wait("f3_y", 1, 1)
            for t in range(T):
                last = dve.scalar_tensor_tensor(out=cx[:, 1024 + t * D:1024 + (t + 1) * D],
                                                in0=bY[:, t * D:(t + 1) * D], scalar=sm[:, 4 + t:5 + t],
                                                in1=fb3[:, :], op0=ALU.mult, op1=ALU.add)
            link(last)
            dve.tensor_tensor(X[:, bass.ds(b * T * D, T * D)], xb[:, :], cx[:, 1024:1024 + T * D],
                              ALU.add).then_inc(sm_["x_out"], 1)
            q.wait("x_out", 1, 1)

        def each_batch(f, eng, chain, loop):
            with eng.Fori(0, B) as b:
                if chain is not None:
                    chain.restart()
                f(Count(eng, b, loop), b)

        @block.sync
        def _(sp):
            def load(name, *pairs):
                for o, i in pairs:
                    sp.dma_start(o, i).then_inc(sm_[name], 16)

            load("ld_first", *[(X[:, b * T * D:(b + 1) * T * D].rearrange("p (t d) -> p t d", t=T),
                                x[b].rearrange("(t p) d -> p t d", p=P)) for b in range(B)],
                 (CT[:, :], ctxT), (rows[:, :], w["rows"]), (cosT[:, :], w["cosT"]), (sinT[:, :], w["sinT"]),
                 (dmask[:, :], w["dist"]), (m8[:, :].rearrange("p (t m) -> p t m", t=T),
                                            mask1.rearrange("(t p) m -> p t m", p=P)),
                 (iota8[:, :], w["iota8"]), (iota32[:, :], w["iota32"]), (inj[:, :], w["inj"]),
                 (rt0[:, :], w["rt0"]), (rt1[:, :], w["rt1"]), (qb1[:, :], w["qb1"]),
                 (rt2[:, :], w["rt2"]), (qb3[:, :], w["qb3"]), (b1t[:, :], w["b1_2"]), (b2t[:, :], w["b2_2"]),
                 (wscale[:, :], w["wscale"].to_broadcast([P, 1])), (fb3[:, :], w["fb3"].to_broadcast([P, D])),
                 *[(pk[32 * s:32 * s + 32, :], w["packed"]) for s in range(4)])
            load("ld_l0", (w0[1], w["wk0"]), (w0[2], w["wv0"]), (w0[0], w["wq0"]), (w0[3], w["wo0"]))
            ne = E0 - 1
            load("ld_f0",
                 (v3(f0g[:, 0:ne * F0], F0), w["gate0"].rearrange("e d h -> d e h")),
                 (v3(f0u[:, 0:ne * F0], F0), w["up0"].rearrange("e d h -> d e h")),
                 (v3(f0d[:, 0:ne * F0], D), w["down0"].rearrange("e (c p) d -> p (e c) d", p=P)),
                 (f0g[:, ne * F0:], w["sgate0"]), (f0u[:, ne * F0:], w["sup0"]),
                 (v3(f0d[:, ne * F0:], D), w["sdown0"].rearrange("(c p) d -> p c d", p=P)))
            load("ld_l1", (wqk1[:, :], w["wqk1"]), (wvo1[:, :], w["wvo1"]))
            load("ld_f1", (f1g, w["g1"]), (f1u, w["u1"]), (f1d, w["d1"]))
            sp.wait_ge(sm_["x_back"], B)
            load("ld_late", (cnat.rearrange("p (n d) -> p n d", d=D), ctxm.rearrange("b (t p) d -> p (b t) d", p=P)),
                 (wqk3, w["wqk3"]), (wvo3, w["wvo3"]))
            sp.wait_ge(sm_["d_done"], NROUND)
            sp.wait_ge(sm_["skew_set"], 1)
            for k in range(K):
                sp.dma_start(dskew[k:P:32, LAG * k * W:(LAG * k + S) * W], dnat[k:P:32, :]) \
                    .then_inc(sm_["skewed"], 16)
            sp.wait_ge(sm_["skewed"], 16 * K)
            load("ld_f2d", (v3(f2d, D), w["w2_2"].rearrange("e (c p) d -> p (e c) d", p=P)))
            sp.wait_ge(sm_["forward"], NGRP)
            load("ld_f2u", (v3(f2u, F2), w["w1_2"].rearrange("e d h -> d e h")))
            sp.wait_ge(sm_["on_kept"], NGRP)
            sp.wait_ge(sm_["onu_set"], 1)
            for k in range(K):
                sp.dma_start(onu[k:P:32, :], onc[k:P:32, LAG * k * W:(LAG * k + S) * W]) \
                    .then_inc(sm_["unskewed"], 16)

            def batch(q, b):
                q.wait("x_done", XD_B, 1)
                sp.dma_start(v3(mload, S), mask3[bass.ds(b, 1)].rearrange("a (t p) m -> p (a t) m", p=P)) \
                    .then_inc(sm_["mask_loaded"], 16)
                q.wait("x_out", 1, 1)
                sp.dma_start(out[bass.ds(b, 1)].rearrange("a (t p) d -> p (a t) d", p=P),
                             v3(X[:, bass.ds(b * T * D, T * D)], D)).then_inc(sm_["stored"], 16)

            each_batch(batch, sp, None, "B")
            sp.wait_ge(sm_["stored"], 16 * B)

        @block.gpsimd
        def _(pool):
            pool.memset(ident[:, :], 0.0).then_inc(sm_["ident_zero"], 1)
            pool.memset(ones[:, :], 1.0).then_inc(sm_["consts"], 1)
            pool.memset(XNT[:, B * S:], 0.0).then_inc(sm_["consts"], 1)
            pool.wait_ge(sm_["ident_zero"], 1)
            pool.affine_select(out=ident[:, :], in_=ident[:, :], compare_op=ALU.not_equal, fill=1.0, base=0,
                               pattern=[[-1, P]], channel_multiplier=1).then_inc(sm_["consts"], 1)
            pool.wait_ge(sm_["consts"], 3)
            pool.tensor_copy(identb[:, :], ident[:, :]).then_inc(sm_["identb_ready"], 1)
            pool.wait_ge(sm_["ld_first"], 16 * N_FIRST)

            def batch(q, b):
                q.wait("x_done", XD_A if q.loop == "A" else XD_B, 1)
                pool.tensor_copy(ctb[:, :], CT[:, bass.ds(b * S, S)]).then_inc(sm_["ctb_ready"], 1)

            each_batch(batch, pool, None, "A")
            pool.wait_ge(sm_["x_back"], B)
            dist_pool(pool)
            moves_pool(pool)
            each_batch(batch, pool, None, "B")

        @block.tensor
        def _(pe):
            pe.wait_ge(sm_["consts"], 3)
            tern_pe(pe)

            def batch_a(q, b):
                l0_pe(pe, q)
                f0_pe(pe, q)
                l1_pe(pe, q)
                f1_pe(pe, q)
                ln_pe(pe, q, "A", 4)

            each_batch(batch_a, pe, None, "A")
            dist_pe(pe)
            expand_pe(pe)

            def batch_b(q, b):
                f2_pe(pe, q)
                l3_pe(pe, q)
                f3_pe(pe, q)

            each_batch(batch_b, pe, None, "B")

        @block.scalar
        def _(act):
            link = Chain(act, act_chain)

            def batch_a(q, b):
                l0_act(act, q, link)
                f0_act(act, q, link)
                l1_act(act, q, link)
                f1_act(act, q, link)
                ln_act_rstd(act, q, link, "A", 4)
                q.wait("xnT_full", LN_A, 5)
                act.copy(XNT[:, bass.ds(b * S, S)], bLN[:, 0:S]).then_inc(sm_["xnT_ready"], 1)
                q.wait("xnT_ready", LN_A, 5)

            each_batch(batch_a, act, link, "A")
            act.wait_ge(sm_["x_back"], B)
            dist_act(act)
            backward_act(act)

            def batch_b(q, b):
                f2_act(act, q, link)
                l3_act(act, q, link)
                f3_act(act, q, link)

            each_batch(batch_b, act, link, "B")

        @block.vector
        def _(dve):
            link = Chain(dve, dve_chain)
            dve.wait_ge(sm_["ld_first"], 16 * N_FIRST)
            dve.wait_ge(sm_["consts"], 3)
            tern_dve(dve, link)
            link(dve.tensor_scalar(mneg[:, :], m8[:, :], 0.0, NEG, ALU.is_equal, ALU.mult))
            link(dve.tensor_tensor(dmask[:, :], dmask[:, :], mneg[:, :], ALU.add))

            def batch_a(q, b):
                dve.tensor_copy(xb[:, :], X[:, bass.ds(b * T * D, T * D)]).then_inc(sm_["x_done"], 1)
                q.wait("x_done", XD_A, 1)
                l0_dve(dve, q, link)
                q.wait("x_done", XD_A, 2)
                f0_dve(dve, q, link)
                q.wait("x_done", XD_A, 3)
                l1_dve(dve, q, link)
                q.wait("x_done", XD_A, 4)
                f1_dve(dve, q, link)
                q.wait("x_done", XD_A, 5)
                ln_dve(dve, q, link, "A", 4)
                dve.tensor_scalar(X[:, bass.ds(b * T * D, T * D)], xb[:, :], 1.0, None,
                                  ALU.mult).then_inc(sm_["x_back"], 1)
                q.wait("x_back", 1, 1)

            each_batch(batch_a, dve, link, "A")
            link.restart()
            dist_dve(dve, link)
            forward_dve(dve, link)
            backward_dve(dve, link)
            expand_dve(dve, link)

            def batch_b(q, b):
                dve.tensor_copy(xb[:, :], X[:, bass.ds(b * T * D, T * D)]).then_inc(sm_["x_done"], 1)
                q.wait("x_done", XD_B, 1)
                f2_dve(dve, q, link)
                q.wait("x_done", XD_B, 2)
                l3_dve(dve, q, link)
                q.wait("x_done", XD_B, 3)
                f3_dve(dve, q, link, b)

            each_batch(batch_b, dve, link, "B")


N_FIRST = 26
N_LATE = 3


def kernel(**inputs):
    import numpy as np
    import concourse.bacc as bacc
    from concourse.bass_utils import run_bass_kernel_spmd

    g = {k: np.asarray(v) for k, v in inputs.items()}

    def heads8(wt):
        o = np.zeros((wt.shape[0], NG, 4, 32), np.float32)
        o[..., :HS] = wt.reshape(wt.shape[0], NG, 4, HS)
        return o.reshape(wt.shape[0], NG * P)

    def bias8(b):
        return np.ascontiguousarray(heads8(b.reshape(1, P)).reshape(NG, P).T)

    def cat(*a):
        return np.concatenate(a, axis=1)

    swap = (np.arange(P) // HS) * HS + (np.arange(P) + HS // 2) % HS
    inv = 1.0 / 10000.0 ** (np.arange(0, HS, 2, dtype=np.float32) / HS)
    fr = np.outer(np.arange(S, dtype=np.float32), inv)
    emb = np.concatenate([fr, fr], axis=-1)
    sign = np.where(np.arange(HS) < HS // 2, -1.0, 1.0).astype(np.float32)
    cosT, sinT = np.zeros((4, 32, S), np.float32), np.zeros((4, 32, S), np.float32)
    cosT[:, :HS] = np.cos(emb).T
    sinT[:, :HS] = (np.sin(emb) * sign).T
    pos = np.arange(S, dtype=np.float32)
    dist = -np.abs(pos[:, None] - pos[None, :]).reshape(T, P, S)
    q1, k1 = g["L1_xattn_Wq"].T, g["L1_xattn_Wk"].T
    bq1, bk1 = g["L1_xattn_bq"], g["L1_xattn_bk"]
    q3 = g["L3_xattn_Wq"].transpose(1, 0, 2).reshape(D, P)
    k3 = g["L3_xattn_Wk"].transpose(1, 0, 2).reshape(D, P)

    def up1(routed, shared):
        return cat(routed.transpose(2, 0, 1).reshape(D, E1 * F1), shared.T)

    def down1(routed, shared):
        a = np.concatenate([routed, shared[None]], axis=0).transpose(0, 2, 1).reshape(E1 + 1, 2, P, D)
        return a.transpose(2, 0, 1, 3).reshape(P, -1)

    consts = {
        "rows": np.concatenate([g["L0_xattn_projection_bias"], g["L1_xattn_bv"], g["L1_xattn_bo"],
                                g["L3_xattn_bv"].reshape(-1), g["L3_xattn_bo"]])[None],
        "cosT": cosT.reshape(P, S), "sinT": sinT.reshape(P, S),
        "dist": dist.transpose(1, 0, 2).reshape(P, T * S),
        "iota8": np.tile(np.arange(8, dtype=np.float32), (P, 1)),
        "iota32": np.tile(np.arange(1, CAP + 1, dtype=np.float32), (P, 1)),
        "inj": (np.arange(P) % 32 == K - 1).astype(np.float32)[:, None],
        "rt0": g["L0_ffn_router_w"], "rt1": g["L1_ffn_gate_w"].T, "rt2": g["L2_ffn_Wg"],
        "qb1": cat(bias8(bq1), bias8(bq1[swap]), bias8(bk1), bias8(bk1[swap])),
        "qb3": cat(bias8(g["L3_xattn_bq"].reshape(-1)), bias8(g["L3_xattn_bk"].reshape(-1))),
        "wq0": g["L0_xattn_query_kernel"].transpose(1, 0, 2).reshape(D, H * HS0),
        "wk0": g["L0_xattn_key_kernel"].transpose(1, 0, 2).reshape(D, H * HS0),
        "wv0": g["L0_xattn_value_kernel"].transpose(1, 0, 2).reshape(D, H * HS0),
        "wo0": g["L0_xattn_projection_kernel"].reshape(C0, P, D).transpose(1, 0, 2).reshape(P, C0 * D),
        "gate0": g["L0_ffn_gate_w"], "up0": g["L0_ffn_up_w"], "down0": g["L0_ffn_down_w"],
        "sgate0": g["L0_ffn_shared_gate_w"], "sup0": g["L0_ffn_shared_up_w"], "sdown0": g["L0_ffn_shared_down_w"],
        "wqk1": cat(heads8(q1), heads8(q1[:, swap]), heads8(k1), heads8(k1[:, swap])),
        "wvo1": cat(g["L1_xattn_Wv"].T, g["L1_xattn_Wo"].T),
        "g1": up1(g["L1_ffn_Wg"], g["L1_ffn_Ws_g"]), "u1": up1(g["L1_ffn_Wu"], g["L1_ffn_Ws_u"]),
        "d1": down1(g["L1_ffn_Wd"], g["L1_ffn_Ws_d"]),
        "wqk3": cat(heads8(q3), heads8(k3)),
        "wvo3": cat(g["L3_xattn_Wv"].transpose(1, 0, 2).reshape(D, P), g["L3_xattn_Wo"]),
        "w1_2": g["L2_ffn_W1"], "w2_2": g["L2_ffn_W2"],
        "b1_2": g["L2_ffn_b1"].reshape(E2 * 4, P).T, "b2_2": g["L2_ffn_b2"],
        "packed": g["L3_ffn_packed_weight"].reshape(32, P), "wscale": g["L3_ffn_weight_scale"].reshape(1, 1), "fb3": g["L3_ffn_bias"].reshape(1, D),
    }
    nc = bacc.Bacc("TRN2", target_bir_lowering=False, num_devices=1)
    arrays = {}

    def dram(name, a):
        a = np.ascontiguousarray(a)
        arrays[name] = a
        return nc.dram_tensor(name, a.shape, mybir.dt.from_np(a.dtype), kind="ExternalInput").ap()

    xd = dram("x", g["x"])
    cm = dram("ctx", g["ctx_1024"])
    ct = dram("ctxT", g["ctx_1024"].transpose(2, 0, 1).reshape(D, B * S))
    m1 = dram("mask1", g["mask_1x1xSxS2_bk0"].reshape(S, S))
    m3 = dram("mask3", g["mask_BxSxS2_ik0"])
    w = {k: dram("w_" + k, a) for k, a in consts.items()}
    o = nc.dram_tensor("out", (B, S, D), F32, kind="ExternalOutput").ap()
    build(nc, xd, cm, ct, m1, m3, w, o)
    r = run_bass_kernel_spmd(nc, [arrays], core_ids=[0])
    return r.results[0]["out"]
```

```python
from contextlib import ExitStack

import concourse.bass as bass
from concourse import mybir

F32 = mybir.dt.float32
BF16 = mybir.dt.bfloat16
U8 = mybir.dt.uint8
U32 = mybir.dt.uint32
I32 = mybir.dt.int32
ALU = mybir.AluOpType
ACT = mybir.ActivationFunctionType
AX = mybir.AxisListType

P = 128
B, S, D = 4, 256, 128
T = S // P
EPS = 1e-5
NEG = -1e30
BIG = 1e30

H = 16
HS0 = 64
HS = 8
C0 = H * HS0 // P
NQ = 4

E0, F0 = 8, 512
E1, F1, CAP = 16, 256, 32
E2, F2 = 8, 512
SLOPES = [2.0 ** (-0.5 * (h + 1)) for h in range(H)]

K = 16
W = S // K
LAG = 4
STEPS = S + LAG * (K - 1)
RING = 4 * LAG



def build(nc, x, ctxm, ctxT, mask1, mask3, w, out):
    LN_A, LN_B, XT_B = 5, 3, 2
    XD_A, XD_B = 5, 3
    with ExitStack() as ctx:
        def sb(name, shape, dt=F32):
            return ctx.enter_context(nc.sbuf_tensor(name, shape, dt))

        def sem(name):
            return ctx.enter_context(nc.semaphore(name))

        bank = [ctx.enter_context(nc.psum_tensor(f"bank{i}", [P, 512], F32)) for i in range(8)]
        bS, bT, bO, bLN, bY = bank[0:2], bank[2:4], bank[4:6], bank[6], bank[7]

        X = sb("X", [P, B * T * D])
        CT = sb("CT", [P, B * S])
        XNT = sb("XNT", [P, (B + 1) * S])
        xb = sb("xb", [P, T * D])
        xn = sb("xn", [P, T * D])
        xnT = sb("xnT", [P, S])
        ctb = sb("ctb", [P, S])
        ident = sb("ident", [P, P])
        identb = sb("identb", [P, P], BF16)
        ones = sb("ones", [P, 256])
        rows = sb("rows", [1, 5 * P])
        dmask = sb("dmask", [P, T * S])
        mneg = sb("mneg", [P, T * S])
        mload = dmask[:, :].bitcast(I32)
        m8 = sb("m8", [P, T * S], U8)
        cosT = sb("cosT", [P, S])
        sinT = sb("sinT", [P, S])
        qb1 = sb("qb1", [P, 4])
        qb3 = sb("qb3", [P, 2])
        wqk1 = sb("wqk1", [P, 4 * P])
        wvo1 = sb("wvo1", [P, 2 * P])
        rt0 = sb("rt0", [P, E0])
        rt1 = sb("rt1", [P, E1])
        rt2 = sb("rt2", [P, E2])
        b1t = sb("b1t", [P, E2 * 4])
        b2t = sb("b2t", [E2, D])
        iota8 = sb("iota8", [P, 8])
        hmask = sb("hmask", [P, H + 2])
        iota32 = sb("iota32", [P, CAP])
        inj = sb("inj", [P, 1])

        WA = 4 * 1024 + 3 * E0 * F0 + 3 * (E1 + 1) * F1
        arena = sb("arena", [P, WA])
        at = [0]

        def take(n):
            at[0] += n
            assert at[0] <= WA
            return arena[:, at[0] - n:at[0]]

        w0 = [take(1024) for _ in range(4)]
        f0g, f0u, f0d = take(E0 * F0), take(E0 * F0), take(E0 * F0)
        f1g, f1u, f1d = (take((E1 + 1) * F1) for _ in range(3))
        at[0] = 0
        dnat = take(S * W)
        f2d = dnat
        dskew = take(STEPS * W)
        f2u = dskew[:, 0:E2 * F2]
        edge = take(STEPS * W).bitcast(BF16)
        stay = take(STEPS * (W + 1)).bitcast(BF16)
        onc = take(STEPS * W // 2).bitcast(BF16)
        onu = take(S * W // 2).bitcast(BF16)
        onT = take(T * B * S)
        cnat = take(B * T * D)
        wqk3 = take(2 * P)
        wvo3 = take(2 * P)

        work = sb("work", [P, 8192])
        qT, kT, V, cx = (work[:, 2048 * i:2048 * (i + 1)] for i in range(4))
        probs = sb("probs", [P, 2, 512])
        probsT = sb("probsT", [P, 2, 512])
        logit = sb("logit", [P, 2, 512])
        q_even, q_odd = qT, cx
        cxT = qT
        qz = qT[:, 512:512 + NQ * S]
        hid = qT
        sil = probs
        oneh, wone = kT[:, 0:1024], kT[:, 1024:2048]
        woneT = V[:, 0:1024]
        xgT, eout = V[:, 1024:1536], V[:, 1536:2048]
        stt = sb("stt", [P, T * 6])
        mv = sb("mv", [P, T * 2])
        ve = sb("ve", [P, 8])
        lnv = sb("lnv", [P, 2])
        y0 = sb("y0", [P, 2])
        rstd = sb("rstd", [P, 2])
        nmx = sb("nmx", [P, H * T])
        nmz = sb("nmz", [P, H * T])
        sums = sb("sums", [P, H * T])
        rsum = sb("rsum", [P, 512])
        rinv = sb("rinv", [P, 512])
        lg = sb("lg", [P, T * 16])
        v8 = sb("v8", [P, T * 8])
        ix = sb("ix", [P, T * 8], U32)
        ixf = sb("ixf", [P, T * 8])
        sm = sb("sm", [P, 8])
        coef = sb("coef", [P, T * 16])
        norms = sb("norms", [P, S + W])
        best = sb("best", [P, W])
        pv = sb("pv", [P, 3 * LAG * 2 * (2 * W + 2)], BF16)
        qiT = sb("qiT", [P, S], BF16)
        sel = cx[0:E1, 0:4 * S]
        top = sb("top", [16, 8 * 4])
        slot = sb("slot", [P, T * 16])
        coefT = sb("coefT", [8, S])
        tern = sb("tern", [P, D])
        ternT = sb("ternT", [P, D], BF16)
        pk = sb("pk", [P, D], I32)
        wscale = sb("wscale", [P, 1])
        fb3 = sb("fb3", [P, D])
        qi = sb("qi", [P, T * D], BF16)

        names = """
            ld_first ld_l0 ld_f0 ld_l1 ld_f1 ld_late ld_f2d ld_f2u
            consts ident_zero stored x_back
            x_done ctb_ready var_ready y0_ready xn_ready xnT_full xnT_ready
            p0_full p0_act p0_dve y0_out y1_out y3_out v_zero
            p1_full p1_dve p1_act p3_full p3_dve p3_act
            f0_logit f0_nmax f0_prob f0_gu f0_silu f0_hid f0_down f0_acc
            f1_logit f1_exp f1_score f1_byexp f1_slot f1_slotT f1_oneh f1_wone
            f1_sh_gu f1_sh_gelu f1_sh_hid f1_gath f1_xg f1_gu f1_gelu f1_hid f1_wT f1_wTc f1_down f1_eout f1_y
            f2_logit f2_exp f2_coef f2_cT f2_cTc f2_up f2_hidA f2_hidD f2_down f2_acc f2_y
            mask_loaded mask_used x_out f2_diff sq_ready norms_full norms_ready d_full d_lin d_sq d_root d_done
            skew_set stay_set onu_set pv_set cost_set skewed forward moves_ready backward on_kept unskewed
            identb_ready onT_full onT_ready expanded tern_ready ternT_full ternT_ready f3_q f3_qT f3_qTc f3_y
        """.split()
        for a in ("a0", "a1", "a3"):
            names += [f"{a}_{n}" for n in "q scores logit nmax exp pt ptA ptD pv rsum rfull rinv norm".split()]
        sm_ = {n: sem(n) for n in names}
        dve_chain, act_chain, pool_chain = sem("dve_chain"), sem("act_chain"), sem("pool_chain")
        block = ctx.enter_context(nc.Block())

        class Count:

            def __init__(self, eng, b, loop):
                self.eng, self.b, self.loop = eng, b, loop

            def wait(self, name, per, n):
                base = BASE[self.loop].get(name, 0)
                self.eng.wait_ge(sm_[name], self.b * per + (base + n))

        class Chain:

            def __init__(self, eng, s):
                self.eng, self.s, self.n = eng, s, 0

            def restart(self):
                self.eng.sem_clear(self.s)
                self.n = 0

            def __call__(self, ins):
                self.n += 1
                ins.then_inc(self.s, 1)
                self.eng.wait_ge(self.s, self.n)

        BASE = {"A": {}, "B": {n: B * LN_A for n in ("var_ready", "y0_ready", "xn_ready", "xnT_full", "xnT_ready")}
                | {"x_done": B * XD_A, "ctb_ready": B, "v_zero": B}}

        def v3(ap, c):
            return ap.rearrange("p (a c) -> p a c", c=c)

        def ln_dve(dve, q, link, loop, s):
            per = LN_A if loop == "A" else LN_B
            for t in range(T):
                last = dve.bn_stats(stt[:, 6 * t:6 * t + 6], xb[:, t * D:(t + 1) * D])
            link(last)
            for t in range(T):
                last = dve.bn_aggr(mv[:, 2 * t:2 * t + 2], stt[:, 6 * t:6 * t + 6])
            link(last)
            dve.tensor_scalar(ve[:, 0:2], mv[:, 1:4:2], EPS, None, ALU.add).then_inc(sm_["var_ready"], 1)
            q.wait("var_ready", per, s + 1)
            q.wait("y0_ready", per, s + 1)
            link(dve.tensor_tensor(ve[:, 2:4], y0[:, :], y0[:, :], ALU.mult))
            link(dve.scalar_tensor_tensor(out=ve[:, 4:6], in0=ve[:, 2:4], scalar=-0.5, in1=ve[:, 0:2],
                                          op0=ALU.mult, op1=ALU.mult))
            link(dve.scalar_tensor_tensor(out=rstd[:, :], in0=ve[:, 4:6], scalar=1.5, in1=y0[:, :],
                                          op0=ALU.add, op1=ALU.mult))
            for t in range(T):
                last = dve.tensor_scalar(xn[:, t * D:(t + 1) * D], xb[:, t * D:(t + 1) * D],
                                         mv[:, 2 * t:2 * t + 1], rstd[:, t:t + 1], ALU.subtract, ALU.mult)
            last.then_inc(sm_["xn_ready"], 1)

        def ln_act_rstd(act, q, link, loop, s):
            per = LN_A if loop == "A" else LN_B
            q.wait("var_ready", per, s + 1)
            link(act.activation(lnv[:, :], ve[:, 0:2], ACT.Ln))
            act.activation(y0[:, :], lnv[:, :], ACT.Exp, scale=-0.5).then_inc(sm_["y0_ready"], 1)

        def ln_pe(pe, q, loop, s):
            q.wait("xn_ready", LN_A if loop == "A" else LN_B, s + 1)
            for t in range(T):
                last = pe.transpose(bLN[:, t * P:(t + 1) * P], xn[:, t * D:(t + 1) * D], ident[:, :])
            last.then_inc(sm_["xnT_full"], 1)

        def ln_act_copy(act, q, loop, s):
            q.wait("xnT_full", LN_A if loop == "A" else XT_B, s + 1)
            act.copy(xnT[:, :], bLN[:, 0:S]).then_inc(sm_["xnT_ready"], 1)

        def pt_ready(q, a, hs, g):
            if hs == HS0:
                q.wait(a + ("_ptD" if g % 2 else "_ptA"), H // 2, g // 2 + 1)
            else:
                q.wait(a + "_ptA", H, g + 1)

        def att_pe(pe, q, a, hs):
            for h in range(H + 3):
                if h < H:
                    if hs == HS:
                        q.wait(a + "_q", H, h + 1)
                    if h >= 2:
                        q.wait(a + ("_exp" if hs == HS0 else "_logit"), H, h - 1)
                    if hs == HS0:
                        qh, o, k = (q_odd if h % 2 else q_even), (h // 2) * S, kT[:, (h // 2) * S:(h // 2 + 1) * S]
                    else:
                        qh, o, k = qz, (h % NQ) * S, kT[:, 0:S]
                    for n in range(T):
                        last = pe.matmul(bS[h % 2][:, n * S:(n + 1) * S], qh[:, o + n * P:o + (n + 1) * P], k,
                                         start=True, stop=True)
                    last.then_inc(sm_[a + "_scores"], 1)
                if 2 <= h < H + 2:
                    g = h - 2
                    q.wait(a + "_exp", H, g + 1)
                    if g >= 2:
                        pt_ready(q, a, hs, g - 2)
                    for m in range(T):
                        for n in range(T):
                            last = pe.transpose(bT[g % 2][:, (m * T + n) * P:(m * T + n + 1) * P],
                                                probs[:, g % 2, n * S + m * P:n * S + (m + 1) * P], ident[:, :])
                    last.then_inc(sm_[a + "_pt"], 1)
                if h >= 3:
                    g = h - 3
                    pt_ready(q, a, hs, g)
                    if hs == HS0:
                        if g % 4 == 0 and g >= 8:
                            q.wait(a + "_norm", H // 4, g // 4 - 1)
                        r, m_ = (g % 2) * HS0, HS0
                        o = bO[(g // 4) % 2][r:r + m_, (g // 2 % 2) * S:(g // 2 % 2 + 1) * S]
                        first, final = True, True
                    else:
                        r, m_ = (g // 4) * 32, 32
                        o = bO[0][r:r + m_, 0:S]
                        first, final = g % 4 == 0, g % 4 == 3
                    for m in range(T):
                        vo = m * H * m_ + g * m_
                        last = pe.matmul(o, V[:, vo:vo + m_], probsT[:, g % 2, m * S:(m + 1) * S],
                                         start=first and m == 0, stop=final and m == T - 1)
                    last.then_inc(sm_[a + "_pv"], 1)
                    if hs == HS0 and g % 4 == 3:
                        q.wait(a + "_rsum", H // 4, g // 4 + 1)
                        if g >= 7:
                            q.wait(a + "_rinv", H // 4, g // 4)
                        for j in range(2):
                            last = spread(pe, bLN[:, j * S:(j + 1) * S], j * P, S)
                        last.then_inc(sm_[a + "_rfull"], 1)
            if hs == HS:
                q.wait(a + "_rsum", 1, 1)
                spread(pe, bLN[:, 0:S], 0, P).then_inc(sm_[a + "_rfull"], 1)

        def spread(pe, o, lo, step):
            for t in range(T):
                last = pe.matmul(o[:, t * P:(t + 1) * P], rsum[:, t * step + lo:t * step + lo + P], ident[:, :],
                                 start=True, stop=True)
            return last

        def att_act(act, q, a, hs, scales):
            for h in range(H + 4):
                if hs == HS0 and h % 4 == 3 and h >= 7:
                    g = (h - 7) // 4
                    q.wait(a + "_rfull", H // 4, g + 1)
                    if g:
                        q.wait(a + "_norm", H // 4, g)
                    act.copy(rinv[:, :], bLN[:, :]).then_inc(sm_[a + "_rinv"], 1)
                if 2 <= h < H + 2 and (hs == HS or h % 2 == 0):
                    g = h - 2
                    q.wait(a + "_pt", H, g + 1)
                    if g >= 2:
                        q.wait(a + "_pv", H, g - 1)
                    act.copy(probsT[:, g % 2, :], bT[g % 2][:, :]).then_inc(sm_[a + "_ptA"], 1)
                if h < H:
                    q.wait(a + "_nmax", H, h + 1)
                    if h >= 2:
                        q.wait(a + "_pt", H, h - 1)
                    for n in range(T):
                        src = bS[h % 2][:, n * S:(n + 1) * S] if hs == HS0 else logit[:, h % 2, n * S:(n + 1) * S]
                        last = act.activation(probs[:, h % 2, n * S:(n + 1) * S], src, ACT.Exp,
                                              bias=nmx[:, T * h + n:T * h + n + 1], scale=scales[h],
                                              accum_out=sums[:, T * h + n:T * h + n + 1])
                    last.then_inc(sm_[a + "_exp"], 1)
            if hs == HS:
                q.wait(a + "_rfull", 1, 1)
                act.copy(rinv[:, 0:S], bLN[:, 0:S]).then_inc(sm_[a + "_rinv"], 1)

        def att_dve(dve, q, link, a, hs, scale, slopes, bias):
            def inverse(h0, nh):
                q.wait(a + "_exp", H, h0 + nh)
                if h0:
                    q.wait(a + "_rfull", H // 4, h0 // 4)
                dst = rsum[:, 0:T * nh * hs].rearrange("p (t h o) -> p t h o", h=nh, o=hs)
                src = sums[:, T * h0:T * (h0 + nh)].rearrange("p (h t) -> p t h", t=T)
                dve.reciprocal(dst, src.unsqueeze(3).to_broadcast([P, T, nh, hs])).then_inc(sm_[a + "_rsum"], 1)

            for h in range(H + 4):
                if h < H:
                    q.wait(a + "_scores", H, h + 1)
                    nm = nmx[:, T * h:T * h + T]
                    if hs == HS0:
                        dve.tensor_reduce(nm, v3(bS[h % 2][:, :], S), AX.X, ALU.max,
                                          negate=True).then_inc(sm_[a + "_nmax"], 1)
                    else:
                        if h >= 2:
                            q.wait(a + "_exp", H, h - 1)
                        dve.scalar_tensor_tensor(out=logit[:, h % 2, :], in0=bS[h % 2][:, :],
                                                 scalar=scale / slopes[h], in1=bias[:, :],
                                                 op0=ALU.mult, op1=ALU.add).then_inc(sm_[a + "_logit"], 1)
                        q.wait(a + "_logit", H, h + 1)
                        if slopes[h] == 1.0:
                            dve.tensor_reduce(nm, v3(logit[:, h % 2, :], S), AX.X, ALU.max,
                                              negate=True).then_inc(sm_[a + "_nmax"], 1)
                        else:
                            z = nmz[:, T * h:T * h + T]
                            link(dve.tensor_reduce(z, v3(logit[:, h % 2, :], S), AX.X, ALU.max, negate=True))
                            dve.tensor_scalar(nm, z, slopes[h], None, ALU.mult).then_inc(sm_[a + "_nmax"], 1)
                if hs == HS0 and 2 <= h < H + 2 and h % 2 == 1:
                    g = h - 2
                    q.wait(a + "_pt", H, g + 1)
                    if g >= 2:
                        q.wait(a + "_pv", H, g - 1)
                    dve.tensor_copy(probsT[:, g % 2, :], bT[g % 2][:, :]).then_inc(sm_[a + "_ptD"], 1)
                if hs == HS0 and h % 4 == 1 and h >= 5:
                    inverse(h - 5, 4)
                if hs == HS0 and h % 4 == 3 and h >= 7:
                    g = (h - 7) // 4
                    q.wait(a + "_pv", H, 4 * g + 4)
                    q.wait(a + "_rinv", H // 4, g + 1)
                    dve.tensor_tensor(cxT[:, 512 * g:512 * (g + 1)], bO[g % 2][:, :], rinv[:, :],
                                      ALU.mult).then_inc(sm_[a + "_norm"], 1)
            if hs == HS:
                inverse(0, H)
                q.wait(a + "_pv", H, H)
                q.wait(a + "_rinv", 1, 1)
                dve.tensor_tensor(cx[:, 0:S], bO[0][:, 0:S], rinv[:, 0:S], ALU.mult).then_inc(sm_[a + "_norm"], 1)

        def att_pool(pool, q, a, ready, per):
            q.wait(ready, per, per)
            for h in range(H):
                if h >= NQ:
                    q.wait(a + "_scores", H, h - NQ + 1)
                o = (h % NQ) * S
                pool.tensor_tensor(qz[:, o:o + S], qT[:, 0:S], hmask[:, h:h + 1].to_broadcast([P, S]),
                                   ALU.mult).then_inc(sm_[a + "_q"], 1)

        def l0_pe(pe, q):
            banks = [*bS, *bT]
            q.wait("ctb_ready", 1, 1)
            q.wait("x_done", XD_A, 1)
            pe.wait_ge(sm_["ld_l0"], 16 * 4)

            def room(f):
                if f >= 4:
                    q.wait("p0_dve" if (f - 4) % 2 else "p0_act", 6, (f - 4) // 2 + 1)

            def heads(f, wt, src):
                room(f)
                for c in range(2):
                    o = ((f % 4) * 2 + c) * P
                    last = pe.matmul(banks[f % 4][:, c * S:(c + 1) * S], wt[:, o:o + P], src[:, :],
                                     start=True, stop=True)
                last.then_inc(sm_["p0_full"], 1)

            for f in range(4):
                heads(f, w0[1], ctb)
            for f in range(4, 8):
                room(f)
                t, j = (f - 4) // 2, f % 2
                pe.matmul(banks[f % 4][:, :], ctb[:, t * P:(t + 1) * P], w0[2][:, j * 512:(j + 1) * 512],
                          start=True, stop=True).then_inc(sm_["p0_full"], 1)
            ln_pe(pe, q, "A", 0)
            q.wait("xnT_ready", LN_A, 1)
            for f in range(8, 12):
                heads(f, w0[0], xnT)
            q.wait("p0_act", 6, 6)
            q.wait("p0_dve", 6, 6)
            att_pe(pe, q, "a0", HS0)
            q.wait("a0_norm", H // 4, H // 4)
            for t in range(T):
                y = bY[:, t * D:(t + 1) * D]
                for c in range(C0):
                    pe.matmul(y, cxT[:, c * S + t * P:c * S + (t + 1) * P], w0[3][:, c * P:(c + 1) * P],
                              start=(c == 0), stop=False)
                last = pe.matmul(y, ones[0:1, 0:P], rows[0:1, 0:P], start=False, stop=True)
            last.then_inc(sm_["y0_out"], 1)

        def l0_drain(q, f, copy, scaled):
            q.wait("p0_full", 12, f + 1)
            src = [*bS, *bT][f % 4][:, :]
            o = (f % 4) * 512
            if f < 4:
                return copy(kT[:, o:o + 512], src)
            if f < 8:
                return copy(V[:, o:o + 512], src)
            scaled(q_even[:, o:o + 512], src, hmask[:, H:H + 1])
            return scaled(q_odd[:, o:o + 512], src, hmask[:, H + 1:H + 2])

        def l0_act(act, q, link):
            ln_act_rstd(act, q, link, "A", 0)

            def drain(f):
                l0_drain(q, f, act.copy, lambda o, i, m: act.mul(o, i, m)).then_inc(sm_["p0_act"], 1)

            for f in (0, 2, 4, 6):
                drain(f)
            ln_act_copy(act, q, "A", 0)
            for f in (8, 10):
                drain(f)
            att_act(act, q, "a0", HS0, [1.0] * H)

        def l0_dve(dve, q, link):
            ln_dve(dve, q, link, "A", 0)

            def drain(f):
                l0_drain(q, f, dve.tensor_copy,
                         lambda o, i, m: dve.tensor_scalar(o, i, m, None, ALU.mult)) \
                    .then_inc(sm_["p0_dve"], 1)

            for f in (1, 3, 5, 7, 9, 11):
                drain(f)
            att_dve(dve, q, link, "a0", HS0, None, None, None)
            q.wait("y0_out", 1, 1)
            dve.tensor_tensor(xb[:, :], xb[:, :], bY[:, 0:T * D], ALU.add).then_inc(sm_["x_done"], 1)

        def f0_pe(pe, q):
            ln_pe(pe, q, "A", 1)
            q.wait("xnT_ready", LN_A, 2)
            pe.wait_ge(sm_["ld_first"], 16 * N_FIRST)
            for t in range(T):
                last = pe.matmul(bLN[:, 256 + t * 8:264 + t * 8], xnT[:, t * P:(t + 1) * P], rt0[:, :],
                                 start=True, stop=True)
            last.then_inc(sm_["f0_logit"], 1)
            pe.wait_ge(sm_["ld_f0"], 16 * 6)

            def down(e):
                q.wait("f0_hid", 2 * E0, 2 * e + 2)
                if e >= 2:
                    q.wait("f0_acc", E0 - 1, e - 1)
                for t in range(T):
                    for c in range(4):
                        last = pe.matmul(bO[e % 2][:, t * D:(t + 1) * D],
                                         hid[:, (e % 2) * 1024 + c * S + t * P:(e % 2) * 1024 + c * S + (t + 1) * P],
                                         f0d[:, (e * 4 + c) * D:(e * 4 + c + 1) * D], start=(c == 0), stop=(c == 3))
                last.then_inc(sm_["f0_down"], 1)

            for e in range(E0):
                for j in range(2):
                    n = 2 * e + j
                    if n >= 2:
                        q.wait("f0_hid", 2 * E0, n - 1)
                    for wt, bk in ((f0g, bS), (f0u, bT)):
                        for c in range(2):
                            o = e * F0 + (2 * j + c) * P
                            last = pe.matmul(bk[n % 2][:, c * S:(c + 1) * S], wt[:, o:o + P], xnT[:, :],
                                             start=True, stop=True)
                    last.then_inc(sm_["f0_gu"], 1)
                if e:
                    down(e - 1)
            down(E0 - 1)

        def f0_act(act, q, link):
            ln_act_rstd(act, q, link, "A", 1)
            ln_act_copy(act, q, "A", 1)
            q.wait("f0_nmax", 1, 1)
            for t in range(T):
                last = act.activation(v8[:, 8 * t:8 * t + 8], lg[:, 8 * t:8 * t + 8], ACT.Exp,
                                      bias=nmz[:, t:t + 1], accum_out=sm[:, t:t + 1])
            last.then_inc(sm_["f0_prob"], 1)
            for n in range(2 * E0):
                q.wait("f0_gu", 2 * E0, n + 1)
                if n >= 2:
                    q.wait("f0_hid", 2 * E0, n - 1)
                act.activation(sil[:, n % 2, :], bS[n % 2][:, :], ACT.Silu).then_inc(sm_["f0_silu"], 1)

        def top_index(dve, link, ne):
            for t in range(T):
                last = dve.max(v8[:, 8 * t:8 * t + 8], lg[:, ne * t:ne * t + ne])
            link(last)
            for t in range(T):
                last = dve.max_index(ix[:, 8 * t:8 * t + 8], v8[:, 8 * t:8 * t + 8], lg[:, ne * t:ne * t + ne])
            link(last)
            link(dve.tensor_copy(ixf[:, :], ix[:, :]))

        def f0_dve(dve, q, link):
            ln_dve(dve, q, link, "A", 1)
            q.wait("f0_logit", 1, 1)
            link(dve.tensor_copy(lg[:, 0:T * 8], bLN[:, 256:256 + T * 8]))
            top_index(dve, link, E0)
            dve.tensor_scalar(nmz[:, 0:T], v8[:, 0:T * 8:8], -1.0, None, ALU.mult).then_inc(sm_["f0_nmax"], 1)
            q.wait("f0_prob", 1, 1)
            link(dve.reciprocal(sm[:, 2:4], sm[:, 0:2]))
            link(dve.tensor_scalar(sm[:, 4:6], sm[:, 2:4], 2.0, None, ALU.mult))
            for t in range(T):
                last = dve.tensor_scalar(coef[:, 8 * t:8 * t + 8], iota8[:, :], ixf[:, 8 * t:8 * t + 1],
                                         sm[:, 4 + t:5 + t], ALU.is_equal, ALU.mult)
            link(last)
            link(dve.memset(coef[:, 7:16:8], 1.0))
            for n in range(2 * E0 + 2):
                if n < 2 * E0:
                    e, j = n // 2, n % 2
                    q.wait("f0_silu", 2 * E0, n + 1)
                    if e >= 2:
                        q.wait("f0_down", E0, e - 1)
                    o = (e % 2) * 1024 + j * 512
                    dve.tensor_tensor(hid[:, o:o + 512], sil[:, n % 2, :], bT[n % 2][:, :],
                                      ALU.mult).then_inc(sm_["f0_hid"], 1)
                if n >= 2 and n % 2 == 1:
                    e = (n - 2) // 2
                    q.wait("f0_down", E0, e + 1)
                    if e:
                        q.wait("f0_acc", E0 - 1, e)
                    for t in range(T):
                        last = dve.scalar_tensor_tensor(
                            out=xb[:, t * D:(t + 1) * D], in0=bO[e % 2][:, t * D:(t + 1) * D],
                            scalar=coef[:, 8 * t + e:8 * t + e + 1], in1=xb[:, t * D:(t + 1) * D],
                            op0=ALU.mult, op1=ALU.add)
                    last.then_inc(sm_["f0_acc" if e < E0 - 1 else "x_done"], 1)

        def proj(pe, o, wt, src):
            return pe.matmul(o, wt, src[:, :], start=True, stop=True)

        def values(pe, bk, wv, brow):
            for t in range(T):
                pe.matmul(bk[:, t * D:(t + 1) * D], ctb[:, t * P:(t + 1) * P], wv, start=True, stop=False)
                last = pe.matmul(bk[:, t * D:(t + 1) * D], ones[0:1, 0:P], rows[0:1, brow * P:(brow + 1) * P],
                                 start=False, stop=True)
            return last

        def values_act(act, q):
            q.wait("v_zero", 1, 1)
            for t in range(T):
                vt = V[:, t * 512:(t + 1) * 512].rearrange("p (i x e) -> p i x e", i=4, e=HS)[:, :, 0:16:5, :]
                last = act.copy(vt, bO[0][:, t * D:(t + 1) * D].rearrange("p (i j e) -> p i j e", i=4, e=HS))
            return last

        def attn_out(pe, q, k, wo, brow, name_y):
            q.wait(f"a{k}_norm", 1, 1)
            for t in range(T):
                y = bY[:, t * D:(t + 1) * D]
                pe.matmul(y, cx[:, t * P:(t + 1) * P], wo, start=True, stop=False)
                last = pe.matmul(y, ones[0:1, 0:P], rows[0:1, brow * P:(brow + 1) * P], start=False, stop=True)
            last.then_inc(sm_[name_y], 1)

        def l1_pe(pe, q):
            q.wait("x_done", XD_A, 3)
            pe.wait_ge(sm_["ld_l1"], 16 * 2)

            def pair(bk, wt, src):
                for sw in range(2):
                    last = proj(pe, bk[:, sw * S:(sw + 1) * S], wqk1[:, (wt + sw) * P:(wt + sw + 1) * P], src)
                last.then_inc(sm_["p1_full"], 1)

            pair(bS[0], 2, ctb)
            values(pe, bO[0], wvo1[:, 0:P], 1).then_inc(sm_["p1_full"], 1)
            ln_pe(pe, q, "A", 2)
            q.wait("xnT_ready", LN_A, 3)
            pair(bS[1], 0, xnT)
            q.wait("p1_dve", 2, 2)
            q.wait("p1_act", 1, 1)
            att_pe(pe, q, "a1", HS)
            attn_out(pe, q, 1, wvo1[:, P:2 * P], 2, "y1_out")

        def l1_act(act, q, link):
            ln_act_rstd(act, q, link, "A", 2)
            q.wait("p1_full", 3, 2)
            values_act(act, q).then_inc(sm_["p1_act"], 1)
            ln_act_copy(act, q, "A", 2)
            att_act(act, q, "a1", HS, SLOPES)

        def l1_dve(dve, q, link):
            ln_dve(dve, q, link, "A", 2)

            def rope(dst, bk, qb, full):
                q.wait("p1_full", 3, full)
                for sw, tab in ((0, cosT), (1, sinT)):
                    last = dve.scalar_tensor_tensor(
                        out=logit[:, 0, sw * S:(sw + 1) * S], in0=bk[:, sw * S:(sw + 1) * S],
                        scalar=qb1[:, qb + sw:qb + sw + 1], in1=tab[:, :], op0=ALU.add, op1=ALU.mult)
                link(last)
                dve.tensor_tensor(dst[:, 0:S], logit[:, 0, 0:S], logit[:, 0, S:2 * S],
                                  ALU.add).then_inc(sm_["p1_dve"], 1)

            rope(kT, bS[0], 2, 1)
            q.wait("p1_dve", 2, 1)
            rope(qT, bS[1], 0, 3)
            att_dve(dve, q, link, "a1", HS, HS ** -0.5, SLOPES, dmask)
            q.wait("y1_out", 1, 1)
            dve.tensor_tensor(xb[:, :], xb[:, :], bY[:, 0:T * D], ALU.add).then_inc(sm_["x_done"], 1)

        NE = E1 * CAP

        def f1_pe(pe, q):
            ln_pe(pe, q, "A", 3)
            q.wait("xnT_ready", LN_A, 4)
            for t in range(T):
                last = pe.matmul(bLN[:, 256 + t * E1:256 + (t + 1) * E1], xnT[:, t * P:(t + 1) * P], rt1[:, :],
                                 start=True, stop=True)
            last.then_inc(sm_["f1_logit"], 1)
            pe.wait_ge(sm_["ld_f1"], 16 * 3)
            for wt, bk in ((f1g, bT[0]), (f1u, bT[1])):
                for j in range(2):
                    o = E1 * F1 + j * P
                    last = pe.matmul(bk[:, j * S:(j + 1) * S], wt[:, o:o + P], xnT[:, :], start=True, stop=True)
            last.then_inc(sm_["f1_sh_gu"], 1)
            q.wait("f1_score", 1, 1)
            for t in range(T):
                last = pe.transpose(bY[0:E1, t * P:(t + 1) * P], coef[:, t * E1:(t + 1) * E1], ident[:, :])
            last.then_inc(sm_["f1_byexp"], 1)
            q.wait("f1_slot", 1, 1)
            for t in range(T):
                last = pe.matmul(bLN[:, 256 + t * E1:256 + (t + 1) * E1], sel[:, S + t * P:S + (t + 1) * P],
                                 ident[0:E1, 0:E1], start=True, stop=True)
            last.then_inc(sm_["f1_slotT"], 1)
            q.wait("f1_oneh", 1, 1)
            for t in range(T):
                last = pe.matmul(bS[0][:, :], xn[:, t * D:(t + 1) * D], oneh[:, t * NE:(t + 1) * NE],
                                 start=(t == 0), stop=(t == T - 1))
            last.then_inc(sm_["f1_gath"], 1)
            q.wait("f1_sh_hid", 1, 1)
            q.wait("f1_wone", 1, 1)
            for g in range(4):
                for t in range(T):
                    last = pe.transpose(bT[g // 2][:, (g % 2) * S + t * P:(g % 2) * S + (t + 1) * P],
                                        wone[:, t * NE + g * P:t * NE + (g + 1) * P], ident[:, :])
            last.then_inc(sm_["f1_wT"], 1)
            q.wait("f1_xg", 1, 1)
            for j in range(2):
                for wt, bk in ((f1g, bS), (f1u, bO)):
                    for e in range(E1):
                        o = e * F1 + j * P
                        last = pe.matmul(bk[j][:, e * CAP:(e + 1) * CAP], wt[:, o:o + P],
                                         xgT[:, e * CAP:(e + 1) * CAP], start=True, stop=True)
                last.then_inc(sm_["f1_gu"], 1)
            q.wait("f1_hid", 2, 2)
            for e in range(E1):
                r = 32 * (e % 4)
                for j in range(2):
                    o = 512 + j * 512 + e * CAP
                    last = pe.matmul(bLN[r:r + CAP, (e // 4) * D:(e // 4 + 1) * D], hid[:, o:o + CAP],
                                     f1d[:, (e * 2 + j) * D:(e * 2 + j + 1) * D], start=(j == 0), stop=(j == 1))
            last.then_inc(sm_["f1_down"], 1)
            q.wait("f1_eout", 1, 1)
            q.wait("f1_wTc", 1, 1)
            for t in range(T):
                y = bY[:, t * D:(t + 1) * D]
                for j in range(2):
                    pe.matmul(y, hid[:, j * S + t * P:j * S + (t + 1) * P],
                              f1d[:, (2 * E1 + j) * D:(2 * E1 + j + 1) * D], start=(j == 0), stop=False)
                for g in range(4):
                    last = pe.matmul(y, woneT[:, g * S + t * P:g * S + (t + 1) * P], eout[:, g * D:(g + 1) * D],
                                     start=False, stop=(g == 3))
            last.then_inc(sm_["f1_y"], 1)

        def f1_act(act, q, link):
            ln_act_rstd(act, q, link, "A", 3)
            ln_act_copy(act, q, "A", 3)
            q.wait("f1_logit", 2, 2)
            for t in range(T):
                last = act.activation(lg[:, t * E1:(t + 1) * E1], bLN[:, 256 + t * E1:256 + (t + 1) * E1], ACT.Exp,
                                      bias=nmz[:, t:t + 1], accum_out=sm[:, t:t + 1])
            last.then_inc(sm_["f1_exp"], 1)
            q.wait("f1_sh_gu", 1, 1)
            act.activation(sil[:, 0, :], bT[0][:, :], ACT.Gelu).then_inc(sm_["f1_sh_gelu"], 1)
            q.wait("f1_gath", 1, 1)
            act.copy(xgT, bS[0][:, :]).then_inc(sm_["f1_xg"], 1)
            q.wait("f1_wT", 1, 1)
            for i in range(2):
                last = act.copy(woneT[:, i * 512:(i + 1) * 512], bT[i][:, :])
            last.then_inc(sm_["f1_wTc"], 1)
            for j in range(2):
                q.wait("f1_gu", 2, j + 1)
                if j == 0:
                    q.wait("f1_sh_hid", 1, 1)
                act.activation(sil[:, j, :], bS[j][:, :], ACT.Gelu).then_inc(sm_["f1_gelu"], 1)
            q.wait("f1_down", 1, 1)
            act.copy(eout, bLN[:, :]).then_inc(sm_["f1_eout"], 1)

        def f1_dve(dve, q, link):
            ln_dve(dve, q, link, "A", 3)
            q.wait("f1_logit", 2, 1)
            dve.tensor_reduce(nmz[:, 0:T], v3(bLN[:, 256:256 + T * E1], E1), AX.X, ALU.max,
                              negate=True).then_inc(sm_["f1_logit"], 1)
            q.wait("f1_exp", 1, 1)
            link(dve.reciprocal(sm[:, 2:4], sm[:, 0:2]))
            for t in range(T):
                last = dve.tensor_scalar(coef[:, t * E1:(t + 1) * E1], lg[:, t * E1:(t + 1) * E1],
                                         sm[:, 2 + t:3 + t], None, ALU.mult)
            last.then_inc(sm_["f1_score"], 1)
            q.wait("f1_sh_gelu", 1, 1)
            dve.tensor_tensor(hid[:, 0:512], sil[:, 0, :], bT[1][:, :], ALU.mult).then_inc(sm_["f1_sh_hid"], 1)
            q.wait("f1_byexp", 1, 1)
            link(dve.tensor_copy(sel[:, 0:S], bY[0:E1, 0:S]))
            for r in range(CAP // 8):
                cur, nxt = sel[:, (r % 2) * S:(r % 2 + 1) * S], sel[:, ((r + 1) % 2) * S:((r + 1) % 2 + 1) * S]
                link(dve.max(top[:, 8 * r:8 * r + 8], cur))
                link(dve.match_replace(nxt, top[:, 8 * r:8 * r + 8], cur, -1.0))
            link(dve.tensor_scalar(sel[:, 2 * S:3 * S], sel[:, 0:S], 0.0, None, ALU.is_lt))
            link(dve.tensor_tensor_scan(sel[:, 3 * S:4 * S], ones[0:E1, 0:S], sel[:, 2 * S:3 * S], 0.0,
                                        ALU.mult, ALU.add))
            dve.tensor_tensor(sel[:, S:2 * S], sel[:, 2 * S:3 * S], sel[:, 3 * S:4 * S],
                              ALU.mult).then_inc(sm_["f1_slot"], 1)
            q.wait("f1_slotT", 1, 1)
            link(dve.tensor_copy(slot[:, :], bLN[:, 256:256 + T * E1]))
            o3, w3 = v3(oneh, CAP), v3(wone, CAP)
            dve.tensor_tensor(o3, slot[:, :].unsqueeze(2).to_broadcast([P, T * E1, CAP]),
                              iota32[:, :].unsqueeze(1).to_broadcast([P, T * E1, CAP]),
                              ALU.is_equal).then_inc(sm_["f1_oneh"], 1)
            q.wait("f1_oneh", 1, 1)
            dve.tensor_tensor(w3, o3, coef[:, 0:T * E1].unsqueeze(2).to_broadcast([P, T * E1, CAP]),
                              ALU.mult).then_inc(sm_["f1_wone"], 1)
            for j in range(2):
                q.wait("f1_gelu", 2, j + 1)
                dve.tensor_tensor(hid[:, 512 * (j + 1):512 * (j + 2)], sil[:, j, :], bO[j][:, :],
                                  ALU.mult).then_inc(sm_["f1_hid"], 1)
            q.wait("f1_y", 1, 1)
            dve.tensor_tensor(xb[:, :], xb[:, :], bY[:, 0:T * D], ALU.add).then_inc(sm_["x_done"], 1)

        banks4 = [*bS, *bT]
        sqc, sqx = work[:, 0:B * S], work[:, 1024:1024 + (B + 1) * S]
        dlin = [work[:, 2304 + i * 512:2816 + i * 512] for i in range(2)]
        dsq = [work[:, 3328 + i * 512:3840 + i * 512] for i in range(2)]
        root = [work[:, 4352 + i * 512:4864 + i * 512] for i in range(2)]
        dtmp = work[:, 5376:5888]
        NROUND = W // 2
        NGRP = STEPS // LAG
        BW = W + 1
        SW = 2 * W + 2
        PW = 2 * W + 2
        PR = 3 * LAG
        cost = work[:, 0:(STEPS + 1) * BW]
        chs = work[:, 6144:6144 + 3 * 4 * LAG * W]
        chb = work[:, 7168:7168 + 2 * 4 * LAG * W].bitcast(BF16)
        cost3 = cost.rearrange("p (s c) -> p s c", c=BW)
        edge4 = edge.rearrange("p (s c q) -> p s c q", c=W, q=2)
        stay3 = stay.rearrange("p (s c) -> p s c", c=SW)
        onc3 = onc.rearrange("p (s c) -> p s c", c=W)

        def dist_pe(pe):
            pe.wait_ge(sm_["sq_ready"], 2)
            for b in range(B):
                last = pe.matmul(bY[32 * b:32 * b + 32, 0:S], ones[:, 0:32], sqc[:, b * S:(b + 1) * S],
                                 start=True, stop=True)
            for b in range(B):
                for c in range(W):
                    o = b * S + c
                    last = pe.matmul(bY[32 * b:32 * b + 32, S + c:S + c + 1], sqx[:, o:o + 31 * W + 1:W],
                                     ones[:, 0:1], start=True, stop=True)
            last.then_inc(sm_["norms_full"], 1)
            for r in range(NROUND):
                if r >= 4:
                    pe.wait_ge(sm_["d_lin"], r - 3)
                for b in range(B):
                    for c in range(2):
                        o = b * S + 2 * r + c
                        last = pe.matmul(banks4[r % 4][32 * b:32 * b + 32, c * S:(c + 1) * S],
                                         XNT[:, o:o + 31 * W + 1:W], CT[:, b * S:(b + 1) * S],
                                         start=True, stop=True)
                last.then_inc(sm_["d_full"], 1)

        def dist_dve(dve, link):
            dve.wait_ge(sm_["norms_full"], 1)
            link(dve.tensor_copy(norms[:, :], bY[:, 0:S + W]))
            dve.sem_inc(sm_["norms_ready"], 1)
            dn = dnat.rearrange("p (i c) -> p c i", c=W)
            for r in range(NROUND + 1):
                if r < NROUND:
                    dve.wait_ge(sm_["d_full"], r + 1)
                    for c in range(2):
                        last = dve.scalar_tensor_tensor(out=dlin[r % 2][:, c * S:(c + 1) * S],
                                                        in0=banks4[r % 4][:, c * S:(c + 1) * S], scalar=-2.0,
                                                        in1=norms[:, 0:S], op0=ALU.mult, op1=ALU.add)
                    last.then_inc(sm_["d_lin"], 1)
                if r:
                    p = r - 1
                    dve.wait_ge(sm_["d_root"], p + 1)
                    link(dve.reciprocal(dtmp, root[p % 2]))
                    link(dve.tensor_tensor(dtmp, dtmp, dsq[p % 2], ALU.mult))
                    link(dve.tensor_tensor(dtmp, dtmp, root[p % 2], ALU.add))
                    dve.tensor_scalar(dn[:, 2 * p:2 * p + 2, :], dtmp.rearrange("p (c i) -> p c i", c=2), 0.5,
                                      None, ALU.mult).then_inc(sm_["d_done"], 1)
                    dve.wait_ge(sm_["d_done"], p + 1)

        def dist_pool(pool):
            pool.memset(dskew, BIG).then_inc(sm_["skew_set"], 1)
            pool.memset(stay, 1.0).then_inc(sm_["stay_set"], 1)
            pool.memset(onu, 0.0).then_inc(sm_["onu_set"], 1)
            pool.memset(pv[:, :], 0.0).then_inc(sm_["pv_set"], 1)
            pool.wait_ge(sm_["norms_ready"], 1)
            for r in range(NROUND):
                pool.wait_ge(sm_["d_lin"], r + 1)
                if r >= 2:
                    pool.wait_ge(sm_["d_done"], r - 1)
                for c in range(2):
                    w_ = S + 2 * r + c
                    last = pool.tensor_scalar(dsq[r % 2][:, c * S:(c + 1) * S], dlin[r % 2][:, c * S:(c + 1) * S],
                                              norms[:, w_:w_ + 1], 1e-30, ALU.add, ALU.max)
                last.then_inc(sm_["d_sq"], 1)
            pool.wait_ge(sm_["d_done"], NROUND)
            pool.memset(cost3[:, 0:1, :], BIG).then_inc(sm_["cost_set"], 1)
            pool.memset(cost3[:, 1:1 + LAG, 0:1], BIG).then_inc(sm_["cost_set"], 1)
            pool.wait_ge(sm_["cost_set"], 2)
            for b in range(B):
                pool.memset(cost[32 * b:32 * b + 1, 0:1], 0.0).then_inc(sm_["cost_set"], 1)

        def dist_act(act):
            act.activation(sqx, XNT[:, :], ACT.Square).then_inc(sm_["sq_ready"], 1)
            act.activation(sqc, CT[:, :], ACT.Square).then_inc(sm_["sq_ready"], 1)
            for r in range(NROUND):
                act.wait_ge(sm_["d_sq"], r + 1)
                act.activation(root[r % 2], dsq[r % 2], ACT.Sqrt).then_inc(sm_["d_root"], 1)

        def forward_dve(dve, link):
            dve.wait_ge(sm_["skewed"], 16 * K)
            dve.wait_ge(sm_["cost_set"], 2 + B)
            for g in range(NGRP):
                for s in range(g * LAG, (g + 1) * LAG):
                    link(dve.tensor_tensor(best[:, :], cost3[:, s, 1:BW], cost3[:, s, 0:W], ALU.min))
                    link(dve.tensor_tensor_scan(cost3[:, s + 1, 1:BW], best[:, :], dskew[:, s * W:(s + 1) * W],
                                                cost3[:, s + 1, 0:1], ALU.min, ALU.add))
                if g < NGRP - 1:
                    a = g * LAG + 1
                    dve.stream_shuffle(cost3[:, a + LAG:a + 2 * LAG, 0], cost3[:, a:a + LAG, W],
                                       [31, *range(31)]).then_inc(sm_["forward"], 1)
                    dve.wait_ge(sm_["forward"], g + 1)
                else:
                    dve.sem_inc(sm_["forward"], 1)

        CH = 4 * LAG

        def moves_pool(pool):
            n = 0
            for lo in range(0, STEPS, CH):
                r = min(CH, STEPS - lo)
                pool.wait_ge(sm_["forward"], (lo + r) // LAG)
                if lo == 0:
                    pool.wait_ge(sm_["stay_set"], 1)
                up, diag = cost3[:, lo:lo + r, 1:BW], cost3[:, lo:lo + r, 0:W]
                left = cost3[:, lo + 1:lo + 1 + r, 0:W]
                v4 = chs[:, 0:3 * r * W].rearrange("p (n s c) -> p n s c", n=3, c=W)
                pool.tensor_tensor(v4[:, 0], up, left, ALU.subtract)
                pool.tensor_tensor(v4[:, 1], diag, up, ALU.subtract)
                pool.tensor_tensor(v4[:, 2], diag, left, ALU.subtract).then_inc(pool_chain, 1)
                pool.wait_ge(pool_chain, 5 * n + 1)
                f3, d3 = chb[:, 0:3 * r * W], chs[:, 0:3 * r * W]
                pool.tensor_scalar(f3, d3, 0.0, None, ALU.is_le).then_inc(pool_chain, 1)
                pool.wait_ge(pool_chain, 5 * n + 2)
                m, g1, g2 = (chb[:, i * r * W:(i + 1) * r * W].rearrange("p (s c) -> p s c", c=W) for i in range(3))
                by_diag, by_up = edge4[:, lo:lo + r, ::-1, 1], edge4[:, lo:lo + r, ::-1, 0]
                pool.tensor_tensor(by_diag, g1, g2, ALU.mult).then_inc(pool_chain, 1)
                pool.wait_ge(pool_chain, 5 * n + 3)
                other = chb[:, 3 * r * W:4 * r * W].rearrange("p (s c) -> p s c", c=W)
                pool.tensor_scalar(other, by_diag, -1.0, 1.0, ALU.mult, ALU.add).then_inc(pool_chain, 1)
                pool.wait_ge(pool_chain, 5 * n + 4)
                pool.tensor_tensor(by_up, m, other, ALU.mult).then_inc(pool_chain, 1)
                pool.wait_ge(pool_chain, 5 * n + 5)
                pool.tensor_tensor(stay3[:, lo:lo + r, SW - 2:0:-2], other, by_up,
                                   ALU.subtract).then_inc(sm_["moves_ready"], 1)
                n += 1
                pool.wait_ge(sm_["moves_ready"], n)

        def backward_dve(dve, link):
            dve.wait_ge(sm_["moves_ready"], -(-STEPS // CH))
            dve.wait_ge(sm_["pv_set"], 1)
            n = STEPS - LAG
            link(dve.stream_shuffle(stay3[:, 0:n, 0], stay3[:, LAG:STEPS, SW - 2], [*range(1, 32), 31]))
            link(dve.memset(stay3[:, n:STEPS, 0:1], 0.0))
            link(dve.tensor_copy(stay3[:, STEPS - 1, 0:1], inj[:, :]))
            pv4 = pv[:, :].rearrange("p (s q c) -> p s q c", q=2, c=PW)
            link(dve.tensor_copy(pv4[:, (STEPS - 1) % PR, 0, 0:1], inj[:, :]))
            for i, g in enumerate(reversed(range(NGRP))):
                if i >= 3:
                    dve.wait_ge(sm_["on_kept"], i - 2)
                for s in reversed(range(g * LAG, (g + 1) * LAG)):
                    r, nx = s % PR, (s + 1) % PR
                    link(dve.tensor_tensor_scan(pv4[:, r, 0, 1:2 * W + 1], stay3[:, s, 0:2 * W],
                                                pv4[:, nx, 1, 0:2 * W], pv4[:, r, 0, 0:1], ALU.mult, ALU.add))
                    link(dve.tensor_tensor(pv4[:, r, 1, 1:2 * W + 1].rearrange("p (c q) -> p c q", q=2),
                                           edge4[:, s], pv4[:, r, 0, 2:2 * W + 2:2].unsqueeze(2)
                                           .to_broadcast([P, W, 2]), ALU.mult))
                if g:
                    a, z = (g * LAG) % PR, ((g - 1) * LAG) % PR
                    dve.stream_shuffle(pv4[:, z:z + LAG, :, 0], pv4[:, a:a + LAG, :, 2 * W],
                                       [*range(1, 32), 31]).then_inc(sm_["backward"], 1)
                    dve.wait_ge(sm_["backward"], i + 1)
                else:
                    dve.sem_inc(sm_["backward"], 1)

        def backward_act(act):
            pv4 = pv[:, :].rearrange("p (s q c) -> p s q c", q=2, c=PW)
            for i, g in enumerate(reversed(range(NGRP))):
                act.wait_ge(sm_["backward"], i + 1)
                a = (g * LAG) % PR
                act.copy(onc3[:, g * LAG:(g + 1) * LAG, :],
                         pv4[:, a:a + LAG, 0, 2:2 * W + 2:2]).then_inc(sm_["on_kept"], 1)

        def expand_pe(pe):
            pe.wait_ge(sm_["unskewed"], 16 * K)
            pe.wait_ge(sm_["identb_ready"], 1)
            for n in range(4):
                for c in range(W // 2):
                    o = (n // 2) * P * W + W - 1 - ((n % 2) * (W // 2) + c)
                    last = pe.transpose(banks4[n][:, :].bitcast(BF16)[:, c * P:(c + 1) * P],
                                        onu[:, o:o + (P - 1) * W + 1:W], identb[:, :])
                last.then_inc(sm_["onT_full"], 1)
            pe.wait_ge(sm_["onT_ready"], 4)
            pe.wait_ge(sm_["ld_late"], 16 * N_LATE)
            for b in range(B):
                for jt in range(T):
                    for h in range(T):
                        o = (h * B + b) * S + jt * P
                        last = pe.matmul(bO[b // 2][:, ((b % 2) * T + jt) * D:((b % 2) * T + jt + 1) * D],
                                         onT[:, o:o + P], cnat[:, (b * T + h) * D:(b * T + h + 1) * D],
                                         start=(h == 0), stop=(h == T - 1))
            last.then_inc(sm_["expanded"], 1)

        def expand_dve(dve, link):
            for n in range(4):
                dve.wait_ge(sm_["onT_full"], n + 1)
                src = banks4[n][:, :].bitcast(BF16).rearrange("p (c b k) -> p c b k", b=B, k=32)
                h = n // 2
                dst = onT[:, h * B * S:(h + 1) * B * S].rearrange("p (b k c) -> p b k c", b=B, c=W)
                for b in range(B):
                    last = dve.tensor_copy(dst[:, b, :, (n % 2) * (W // 2):(n % 2 + 1) * (W // 2)],
                                           src[:, :, b, 0:K].rearrange("p c k -> p k c"))
                last.then_inc(sm_["onT_ready"], 1)
            dve.wait_ge(sm_["expanded"], 1)
            for i in range(2):
                v = X[:, i * 512:(i + 1) * 512]
                last = dve.tensor_tensor(v, v, bO[i][:, :], ALU.add)
            link(last)

        def f2_pe(pe, q):
            ln_pe(pe, q, "B", 0)
            q.wait("xnT_ready", XT_B, 1)
            for t in range(T):
                last = pe.matmul(bLN[:, 256 + t * 8:264 + t * 8], xnT[:, t * P:(t + 1) * P], rt2[:, :],
                                 start=True, stop=True)
            last.then_inc(sm_["f2_logit"], 1)
            pe.wait_ge(sm_["ld_f2d"], 16)
            pe.wait_ge(sm_["ld_f2u"], 16)

            def down(e):
                q.wait("f2_hidA", E2, e + 1)
                q.wait("f2_hidD", E2, e + 1)
                if e >= 2:
                    q.wait("f2_acc", E2, e - 1)
                for t in range(T):
                    for c in range(4):
                        o = (e % 2) * 1024 + c * S + t * P
                        last = pe.matmul(bO[e % 2][:, t * D:(t + 1) * D], hid[:, o:o + P],
                                         f2d[:, (e * 4 + c) * D:(e * 4 + c + 1) * D], start=(c == 0), stop=(c == 3))
                last.then_inc(sm_["f2_down"], 1)

            for e in range(E2):
                for j in range(2):
                    n = 2 * e + j
                    if n >= 4:
                        q.wait("f2_hidD" if j else "f2_hidA", E2, e - 1)
                    for c in range(2):
                        o = e * F2 + (2 * j + c) * P
                        last = pe.matmul(banks4[n % 4][:, c * S:(c + 1) * S], f2u[:, o:o + P], xnT[:, :],
                                         start=True, stop=True)
                    last.then_inc(sm_["f2_up"], 1)
                if e == 1:
                    q.wait("f2_coef", 1, 1)
                    for t in range(T):
                        last = pe.transpose(bLN[0:E2, t * P:(t + 1) * P], coef[:, 8 * t:8 * t + 8], ident[:, :])
                    last.then_inc(sm_["f2_cT"], 1)
                if e:
                    down(e - 1)
            down(E2 - 1)
            q.wait("f2_cTc", 1, 1)
            for t in range(T):
                last = pe.matmul(bY[:, t * D:(t + 1) * D], coefT[:, t * P:(t + 1) * P], b2t[:, :],
                                 start=True, stop=True)
            last.then_inc(sm_["f2_y"], 1)

        def f2_act(act, q, link):
            ln_act_rstd(act, q, link, "B", 0)
            ln_act_copy(act, q, "B", 0)
            q.wait("f2_diff", 1, 1)
            act.activation(sm[:, 2:4], sm[:, 0:2], ACT.Exp).then_inc(sm_["f2_exp"], 1)
            for e in range(E2):
                if e == 2:
                    q.wait("f2_cT", 1, 1)
                    act.copy(coefT[:, :], bLN[0:E2, 0:S]).then_inc(sm_["f2_cTc"], 1)
                q.wait("f2_up", 2 * E2, 2 * e + 1)
                if e >= 2:
                    q.wait("f2_down", E2, e - 1)
                for c in range(2):
                    o = (e % 2) * 1024 + c * S
                    last = act.activation(hid[:, o:o + S], banks4[(2 * e) % 4][:, c * S:(c + 1) * S], ACT.Relu,
                                          bias=b1t[:, e * 4 + c:e * 4 + c + 1])
                last.then_inc(sm_["f2_hidA"], 1)

        def f2_dve(dve, q, link):
            ln_dve(dve, q, link, "B", 0)
            q.wait("f2_logit", 1, 1)
            link(dve.tensor_copy(lg[:, 0:T * 8], bLN[:, 256:256 + T * 8]))
            top_index(dve, link, E2)
            dve.tensor_tensor(sm[:, 0:2], v8[:, 1:T * 8:8], v8[:, 0:T * 8:8],
                              ALU.subtract).then_inc(sm_["f2_diff"], 1)
            q.wait("f2_exp", 1, 1)
            link(dve.tensor_scalar(sm[:, 4:6], sm[:, 2:4], 1.0, None, ALU.add))
            link(dve.reciprocal(sm[:, 6:8], sm[:, 4:6]))
            link(dve.tensor_tensor(sm[:, 4:6], sm[:, 2:4], sm[:, 6:8], ALU.mult))
            for t in range(T):
                dve.tensor_scalar(coef[:, 8 * t:8 * t + 8], iota8[:, :], ixf[:, 8 * t:8 * t + 1],
                                  sm[:, 6 + t:7 + t], ALU.is_equal, ALU.mult)
                last = dve.tensor_scalar(coef[:, 16 + 8 * t:24 + 8 * t], iota8[:, :], ixf[:, 8 * t + 1:8 * t + 2],
                                         sm[:, 4 + t:5 + t], ALU.is_equal, ALU.mult)
            link(last)
            dve.tensor_tensor(coef[:, 0:16], coef[:, 0:16], coef[:, 16:32], ALU.add).then_inc(sm_["f2_coef"], 1)
            q.wait("f2_coef", 1, 1)
            for e in range(E2 + 2):
                if e < E2:
                    q.wait("f2_up", 2 * E2, 2 * e + 2)
                    if e >= 2:
                        q.wait("f2_down", E2, e - 1)
                    for c in range(2):
                        o = (e % 2) * 1024 + (2 + c) * S
                        last = dve.tensor_scalar(hid[:, o:o + S], banks4[(2 * e + 1) % 4][:, c * S:(c + 1) * S],
                                                 b1t[:, e * 4 + 2 + c:e * 4 + 3 + c], 0.0, ALU.add, ALU.max)
                    last.then_inc(sm_["f2_hidD"], 1)
                if 1 <= e <= E2:
                    p = e - 1
                    q.wait("f2_down", E2, p + 1)
                    if p:
                        q.wait("f2_acc", E2, p)
                    for t in range(T):
                        last = dve.scalar_tensor_tensor(
                            out=xb[:, t * D:(t + 1) * D], in0=bO[p % 2][:, t * D:(t + 1) * D],
                            scalar=coef[:, 8 * t + p:8 * t + p + 1], in1=xb[:, t * D:(t + 1) * D],
                            op0=ALU.mult, op1=ALU.add)
                    last.then_inc(sm_["f2_acc"], 1)
            q.wait("f2_acc", E2, E2)
            q.wait("f2_y", 1, 1)
            dve.tensor_tensor(xb[:, :], xb[:, :], bY[:, 0:T * D], ALU.add).then_inc(sm_["x_done"], 1)

        def l3_pe(pe, q):
            q.wait("ctb_ready", 1, 1)
            q.wait("x_done", XD_B, 2)
            proj(pe, bS[0][:, 0:S], wqk3[:, P:2 * P], ctb)
            values(pe, bO[0], wvo3[:, 0:P], 3).then_inc(sm_["p3_full"], 1)
            ln_pe(pe, q, "B", 1)
            q.wait("xnT_ready", XT_B, 2)
            proj(pe, bS[1][:, 0:S], wqk3[:, 0:P], xnT).then_inc(sm_["p3_full"], 1)
            q.wait("p3_act", 1, 1)
            q.wait("p3_dve", 1, 1)
            att_pe(pe, q, "a3", HS)
            attn_out(pe, q, 3, wvo3[:, P:2 * P], 4, "y3_out")

        def l3_act(act, q, link):
            ln_act_rstd(act, q, link, "B", 1)
            q.wait("p3_full", 2, 1)
            act.activation(kT[:, 0:S], bS[0][:, 0:S], ACT.Identity, bias=qb3[:, 1:2])
            values_act(act, q).then_inc(sm_["p3_act"], 1)
            ln_act_copy(act, q, "B", 1)
            att_act(act, q, "a3", HS, [1.0] * H)

        def l3_dve(dve, q, link):
            ln_dve(dve, q, link, "B", 1)
            q.wait("mask_loaded", 16, 16)
            dve.tensor_scalar(mneg[:, :], mload, 0.0, NEG, ALU.is_equal, ALU.mult).then_inc(sm_["mask_used"], 1)
            q.wait("p3_full", 2, 2)
            dve.tensor_scalar(qT[:, 0:S], bS[1][:, 0:S], qb3[:, 0:1], None, ALU.add).then_inc(sm_["p3_dve"], 1)
            att_dve(dve, q, link, "a3", HS, HS ** -0.5, [1.0] * H, mneg)
            q.wait("y3_out", 1, 1)
            dve.tensor_tensor(xb[:, :], xb[:, :], bY[:, 0:T * D], ALU.add).then_inc(sm_["x_done"], 1)

        def tern_dve(dve, link):
            dve.wait_ge(sm_["ld_first"], 16 * N_FIRST)
            for s in range(4):
                p = pk[32 * s:32 * s + 32, :]
                last = dve.tensor_scalar(p, p, 2 * s, 3, ALU.logical_shift_right, ALU.bitwise_and)
            link(last)
            dve.tensor_scalar(tern[:, :], pk[:, :], 1.0, None, ALU.subtract).then_inc(sm_["tern_ready"], 1)
            dve.wait_ge(sm_["ternT_full"], 1)
            dve.tensor_copy(ternT[:, :], bY[:, 0:D]).then_inc(sm_["ternT_ready"], 1)

        def tern_pe(pe):
            pe.wait_ge(sm_["tern_ready"], 1)
            pe.transpose(bY[:, 0:D], tern[:, :], ident[:, :]).then_inc(sm_["ternT_full"], 1)
            pe.wait_ge(sm_["ternT_ready"], 1)

        def f3_pe(pe, q):
            q.wait("f3_q", 1, 1)
            qp = bLN[:, :].bitcast(BF16)
            for t in range(T):
                last = pe.transpose(qp[:, t * P:(t + 1) * P], qi[:, t * D:(t + 1) * D], identb[:, :])
            last.then_inc(sm_["f3_qT"], 1)
            q.wait("f3_qTc", 1, 1)
            for t in range(T):
                last = pe.matmul(bY[:, t * D:(t + 1) * D], qiT[:, t * P:(t + 1) * P], ternT[:, :],
                                 start=True, stop=True)
            last.then_inc(sm_["f3_y"], 1)

        def f3_act(act, q, link):
            ln_act_rstd(act, q, link, "B", 2)
            q.wait("f3_qT", 1, 1)
            act.copy(qiT[:, :], bLN[:, :].bitcast(BF16)[:, 0:S]).then_inc(sm_["f3_qTc"], 1)

        ROUND = 1.5 * 2.0 ** 23

        def f3_dve(dve, q, link, b):
            ln_dve(dve, q, link, "B", 2)
            q.wait("xn_ready", LN_B, 3)
            link(dve.tensor_reduce(sm[:, 0:2], v3(xn[:, :], D), AX.X, ALU.max, apply_absolute_value=True))
            link(dve.tensor_scalar(sm[:, 2:4], sm[:, 0:2], 1e-5, None, ALU.max))
            link(dve.reciprocal(sm[:, 4:6], sm[:, 2:4]))
            link(dve.tensor_scalar(sm[:, 0:2], sm[:, 4:6], 127.0, None, ALU.mult))
            for t in range(T):
                last = dve.tensor_scalar(cx[:, t * D:(t + 1) * D], xn[:, t * D:(t + 1) * D], sm[:, t:t + 1],
                                         ROUND, ALU.mult, ALU.add)
            link(last)
            link(dve.tensor_scalar(cx[:, 512:512 + T * D], cx[:, 0:T * D], ROUND, 127.0, ALU.subtract, ALU.min))
            dve.tensor_scalar(qi[:, :], cx[:, 512:512 + T * D], -128.0, None, ALU.max).then_inc(sm_["f3_q"], 1)
            link(dve.tensor_scalar(sm[:, 4:6], sm[:, 2:4], wscale[:, 0:1], 1.0 / 127.0, ALU.mult, ALU.mult))
            q.wait("f3_y", 1, 1)
            for t in range(T):
                last = dve.scalar_tensor_tensor(out=cx[:, 1024 + t * D:1024 + (t + 1) * D],
                                                in0=bY[:, t * D:(t + 1) * D], scalar=sm[:, 4 + t:5 + t],
                                                in1=fb3[:, :], op0=ALU.mult, op1=ALU.add)
            link(last)
            dve.tensor_tensor(X[:, bass.ds(b * T * D, T * D)], xb[:, :], cx[:, 1024:1024 + T * D],
                              ALU.add).then_inc(sm_["x_out"], 1)
            q.wait("x_out", 1, 1)

        def each_batch(f, eng, chain, loop):
            with eng.Fori(0, B) as b:
                if chain is not None:
                    chain.restart()
                f(Count(eng, b, loop), b)

        @block.sync
        def _(sp):
            def load(name, *pairs):
                for o, i in pairs:
                    sp.dma_start(o, i).then_inc(sm_[name], 16)

            load("ld_first", *[(X[:, b * T * D:(b + 1) * T * D].rearrange("p (t d) -> p t d", t=T),
                                x[b].rearrange("(t p) d -> p t d", p=P)) for b in range(B)],
                 (CT[:, :], ctxT), (rows[:, :], w["rows"]), (cosT[:, :], w["cosT"]), (sinT[:, :], w["sinT"]),
                 (dmask[:, :], w["dist"]), (m8[:, :].rearrange("p (t m) -> p t m", t=T),
                                            mask1.rearrange("(t p) m -> p t m", p=P)),
                 (iota8[:, :], w["iota8"]), (hmask[:, :], w["hmask"]), (iota32[:, :], w["iota32"]), (inj[:, :], w["inj"]),
                 (rt0[:, :], w["rt0"]), (rt1[:, :], w["rt1"]), (qb1[:, :], w["qb1"]),
                 (rt2[:, :], w["rt2"]), (qb3[:, :], w["qb3"]), (b1t[:, :], w["b1_2"]), (b2t[:, :], w["b2_2"]),
                 (wscale[:, :], w["wscale"].to_broadcast([P, 1])), (fb3[:, :], w["fb3"].to_broadcast([P, D])),
                 *[(pk[32 * s:32 * s + 32, :], w["packed"]) for s in range(4)])
            load("ld_l0", (w0[1], w["wk0"]), (w0[2], w["wv0"]), (w0[0], w["wq0"]), (w0[3], w["wo0"]))
            ne = E0 - 1
            load("ld_f0",
                 (v3(f0g[:, 0:ne * F0], F0), w["gate0"].rearrange("e d h -> d e h")),
                 (v3(f0u[:, 0:ne * F0], F0), w["up0"].rearrange("e d h -> d e h")),
                 (v3(f0d[:, 0:ne * F0], D), w["down0"].rearrange("e (c p) d -> p (e c) d", p=P)),
                 (f0g[:, ne * F0:], w["sgate0"]), (f0u[:, ne * F0:], w["sup0"]),
                 (v3(f0d[:, ne * F0:], D), w["sdown0"].rearrange("(c p) d -> p c d", p=P)))
            load("ld_l1", (wqk1[:, :], w["wqk1"]), (wvo1[:, :], w["wvo1"]))
            load("ld_f1", (f1g, w["g1"]), (f1u, w["u1"]), (f1d, w["d1"]))
            sp.wait_ge(sm_["x_back"], B)
            load("ld_late", (cnat.rearrange("p (n d) -> p n d", d=D), ctxm.rearrange("b (t p) d -> p (b t) d", p=P)),
                 (wqk3, w["wqk3"]), (wvo3, w["wvo3"]))
            sp.wait_ge(sm_["d_done"], NROUND)
            sp.wait_ge(sm_["skew_set"], 1)
            for k in range(K):
                sp.dma_start(dskew[k:P:32, LAG * k * W:(LAG * k + S) * W], dnat[k:P:32, :]) \
                    .then_inc(sm_["skewed"], 16)
            sp.wait_ge(sm_["skewed"], 16 * K)
            load("ld_f2d", (v3(f2d, D), w["w2_2"].rearrange("e (c p) d -> p (e c) d", p=P)))
            sp.wait_ge(sm_["forward"], NGRP)
            load("ld_f2u", (v3(f2u, F2), w["w1_2"].rearrange("e d h -> d e h")))
            sp.wait_ge(sm_["on_kept"], NGRP)
            sp.wait_ge(sm_["onu_set"], 1)
            for k in range(K):
                sp.dma_start(onu[k:P:32, :], onc[k:P:32, LAG * k * W:(LAG * k + S) * W]) \
                    .then_inc(sm_["unskewed"], 16)

            def batch(q, b):
                q.wait("x_done", XD_B, 1)
                sp.dma_start(v3(mload, S), mask3[bass.ds(b, 1)].rearrange("a (t p) m -> p (a t) m", p=P)) \
                    .then_inc(sm_["mask_loaded"], 16)
                q.wait("x_out", 1, 1)
                sp.dma_start(out[bass.ds(b, 1)].rearrange("a (t p) d -> p (a t) d", p=P),
                             v3(X[:, bass.ds(b * T * D, T * D)], D)).then_inc(sm_["stored"], 16)

            each_batch(batch, sp, None, "B")
            sp.wait_ge(sm_["stored"], 16 * B)

        @block.gpsimd
        def _(pool):
            pool.memset(ident[:, :], 0.0).then_inc(sm_["ident_zero"], 1)
            pool.memset(ones[:, :], 1.0).then_inc(sm_["consts"], 1)
            pool.memset(XNT[:, B * S:], 0.0).then_inc(sm_["consts"], 1)
            pool.wait_ge(sm_["ident_zero"], 1)
            pool.affine_select(out=ident[:, :], in_=ident[:, :], compare_op=ALU.not_equal, fill=1.0, base=0,
                               pattern=[[-1, P]], channel_multiplier=1).then_inc(sm_["consts"], 1)
            pool.wait_ge(sm_["consts"], 3)
            pool.tensor_copy(identb[:, :], ident[:, :]).then_inc(sm_["identb_ready"], 1)
            pool.wait_ge(sm_["ld_first"], 16 * N_FIRST)

            def batch(q, b):
                q.wait("x_done", XD_A if q.loop == "A" else XD_B, 1)
                pool.tensor_copy(ctb[:, :], CT[:, bass.ds(b * S, S)]).then_inc(sm_["ctb_ready"], 1)
                if q.loop == "A":
                    q.wait("x_done", XD_A, 2)
                zero = XNT[:, B * S:].unsqueeze(1).to_broadcast([P, 1024 // S, S])
                pool.tensor_tensor(v3(V[:, 0:1024], S), zero, zero, ALU.add).then_inc(sm_["v_zero"], 1)
                if q.loop == "A":
                    att_pool(pool, q, "a1", "p1_dve", 2)
                else:
                    att_pool(pool, q, "a3", "p3_dve", 1)

            each_batch(batch, pool, None, "A")
            pool.wait_ge(sm_["x_back"], B)
            dist_pool(pool)
            moves_pool(pool)
            each_batch(batch, pool, None, "B")

        @block.tensor
        def _(pe):
            pe.wait_ge(sm_["consts"], 3)
            tern_pe(pe)

            def batch_a(q, b):
                l0_pe(pe, q)
                f0_pe(pe, q)
                l1_pe(pe, q)
                f1_pe(pe, q)
                ln_pe(pe, q, "A", 4)

            each_batch(batch_a, pe, None, "A")
            dist_pe(pe)
            expand_pe(pe)

            def batch_b(q, b):
                f2_pe(pe, q)
                l3_pe(pe, q)
                f3_pe(pe, q)

            each_batch(batch_b, pe, None, "B")

        @block.scalar
        def _(act):
            link = Chain(act, act_chain)

            def batch_a(q, b):
                l0_act(act, q, link)
                f0_act(act, q, link)
                l1_act(act, q, link)
                f1_act(act, q, link)
                ln_act_rstd(act, q, link, "A", 4)
                q.wait("xnT_full", LN_A, 5)
                act.copy(XNT[:, bass.ds(b * S, S)], bLN[:, 0:S]).then_inc(sm_["xnT_ready"], 1)
                q.wait("xnT_ready", LN_A, 5)

            each_batch(batch_a, act, link, "A")
            act.wait_ge(sm_["x_back"], B)
            dist_act(act)
            backward_act(act)

            def batch_b(q, b):
                f2_act(act, q, link)
                l3_act(act, q, link)
                f3_act(act, q, link)

            each_batch(batch_b, act, link, "B")

        @block.vector
        def _(dve):
            link = Chain(dve, dve_chain)
            dve.wait_ge(sm_["ld_first"], 16 * N_FIRST)
            dve.wait_ge(sm_["consts"], 3)
            tern_dve(dve, link)
            link(dve.tensor_scalar(mneg[:, :], m8[:, :], 0.0, NEG, ALU.is_equal, ALU.mult))
            link(dve.tensor_tensor(dmask[:, :], dmask[:, :], mneg[:, :], ALU.add))

            def batch_a(q, b):
                dve.tensor_copy(xb[:, :], X[:, bass.ds(b * T * D, T * D)]).then_inc(sm_["x_done"], 1)
                q.wait("x_done", XD_A, 1)
                l0_dve(dve, q, link)
                q.wait("x_done", XD_A, 2)
                f0_dve(dve, q, link)
                q.wait("x_done", XD_A, 3)
                l1_dve(dve, q, link)
                q.wait("x_done", XD_A, 4)
                f1_dve(dve, q, link)
                q.wait("x_done", XD_A, 5)
                ln_dve(dve, q, link, "A", 4)
                dve.tensor_scalar(X[:, bass.ds(b * T * D, T * D)], xb[:, :], 1.0, None,
                                  ALU.mult).then_inc(sm_["x_back"], 1)
                q.wait("x_back", 1, 1)

            each_batch(batch_a, dve, link, "A")
            link.restart()
            dist_dve(dve, link)
            forward_dve(dve, link)
            backward_dve(dve, link)
            expand_dve(dve, link)

            def batch_b(q, b):
                dve.tensor_copy(xb[:, :], X[:, bass.ds(b * T * D, T * D)]).then_inc(sm_["x_done"], 1)
                q.wait("x_done", XD_B, 1)
                f2_dve(dve, q, link)
                q.wait("x_done", XD_B, 2)
                l3_dve(dve, q, link)
                q.wait("x_done", XD_B, 3)
                f3_dve(dve, q, link, b)

            each_batch(batch_b, dve, link, "B")


N_FIRST = 27
N_LATE = 3


def kernel(**inputs):
    import numpy as np
    import concourse.bacc as bacc
    from concourse.bass_utils import run_bass_kernel_spmd

    g = {k: np.asarray(v) for k, v in inputs.items()}

    def cat(*a):
        return np.concatenate(a, axis=1)

    swap = (np.arange(P) // HS) * HS + (np.arange(P) + HS // 2) % HS
    inv = 1.0 / 10000.0 ** (np.arange(0, HS, 2, dtype=np.float32) / HS)
    fr = np.outer(np.arange(S, dtype=np.float32), inv)
    emb = np.concatenate([fr, fr], axis=-1)
    sign = np.where(np.arange(HS) < HS // 2, -1.0, 1.0).astype(np.float32)
    cosT, sinT = np.tile(np.cos(emb).T, (H, 1)), np.tile((np.sin(emb) * sign).T, (H, 1))
    p = np.arange(P)[:, None]
    hmask = np.concatenate([p // HS == np.arange(H)[None], (p // HS0 == np.arange(2)[None]) * HS0 ** -0.5], axis=1)
    pos = np.arange(S, dtype=np.float32)
    dist = -np.abs(pos[:, None] - pos[None, :]).reshape(T, P, S)
    q1, k1 = g["L1_xattn_Wq"].T, g["L1_xattn_Wk"].T
    bq1, bk1 = g["L1_xattn_bq"], g["L1_xattn_bk"]
    q3 = g["L3_xattn_Wq"].transpose(1, 0, 2).reshape(D, P)
    k3 = g["L3_xattn_Wk"].transpose(1, 0, 2).reshape(D, P)

    def up1(routed, shared):
        return cat(routed.transpose(2, 0, 1).reshape(D, E1 * F1), shared.T)

    def down1(routed, shared):
        a = np.concatenate([routed, shared[None]], axis=0).transpose(0, 2, 1).reshape(E1 + 1, 2, P, D)
        return a.transpose(2, 0, 1, 3).reshape(P, -1)

    consts = {
        "rows": np.concatenate([g["L0_xattn_projection_bias"], g["L1_xattn_bv"], g["L1_xattn_bo"],
                                g["L3_xattn_bv"].reshape(-1), g["L3_xattn_bo"]])[None],
        "cosT": cosT, "sinT": sinT, "hmask": hmask.astype(np.float32),
        "dist": dist.transpose(1, 0, 2).reshape(P, T * S),
        "iota8": np.tile(np.arange(8, dtype=np.float32), (P, 1)),
        "iota32": np.tile(np.arange(1, CAP + 1, dtype=np.float32), (P, 1)),
        "inj": (np.arange(P) % 32 == K - 1).astype(np.float32)[:, None],
        "rt0": g["L0_ffn_router_w"], "rt1": g["L1_ffn_gate_w"].T, "rt2": g["L2_ffn_Wg"],
        "qb1": np.stack([bq1, bq1[swap], bk1, bk1[swap]], axis=1),
        "qb3": np.stack([g["L3_xattn_bq"].reshape(-1), g["L3_xattn_bk"].reshape(-1)], axis=1),
        "wq0": g["L0_xattn_query_kernel"].transpose(1, 0, 2).reshape(D, H * HS0),
        "wk0": g["L0_xattn_key_kernel"].transpose(1, 0, 2).reshape(D, H * HS0),
        "wv0": g["L0_xattn_value_kernel"].transpose(1, 0, 2).reshape(D, H * HS0),
        "wo0": g["L0_xattn_projection_kernel"].reshape(C0, P, D).transpose(1, 0, 2).reshape(P, C0 * D),
        "gate0": g["L0_ffn_gate_w"], "up0": g["L0_ffn_up_w"], "down0": g["L0_ffn_down_w"],
        "sgate0": g["L0_ffn_shared_gate_w"], "sup0": g["L0_ffn_shared_up_w"], "sdown0": g["L0_ffn_shared_down_w"],
        "wqk1": cat(q1, q1[:, swap], k1, k1[:, swap]),
        "wvo1": cat(g["L1_xattn_Wv"].T, g["L1_xattn_Wo"].T),
        "g1": up1(g["L1_ffn_Wg"], g["L1_ffn_Ws_g"]), "u1": up1(g["L1_ffn_Wu"], g["L1_ffn_Ws_u"]),
        "d1": down1(g["L1_ffn_Wd"], g["L1_ffn_Ws_d"]),
        "wqk3": cat(q3, k3),
        "wvo3": cat(g["L3_xattn_Wv"].transpose(1, 0, 2).reshape(D, P), g["L3_xattn_Wo"]),
        "w1_2": g["L2_ffn_W1"], "w2_2": g["L2_ffn_W2"],
        "b1_2": g["L2_ffn_b1"].reshape(E2 * 4, P).T, "b2_2": g["L2_ffn_b2"],
        "packed": g["L3_ffn_packed_weight"].reshape(32, P), "wscale": g["L3_ffn_weight_scale"].reshape(1, 1), "fb3": g["L3_ffn_bias"].reshape(1, D),
    }
    nc = bacc.Bacc("TRN2", target_bir_lowering=False, num_devices=1)
    arrays = {}

    def dram(name, a):
        a = np.ascontiguousarray(a)
        arrays[name] = a
        return nc.dram_tensor(name, a.shape, mybir.dt.from_np(a.dtype), kind="ExternalInput").ap()

    xd = dram("x", g["x"])
    cm = dram("ctx", g["ctx_1024"])
    ct = dram("ctxT", g["ctx_1024"].transpose(2, 0, 1).reshape(D, B * S))
    m1 = dram("mask1", g["mask_1x1xSxS2_bk0"].reshape(S, S))
    m3 = dram("mask3", g["mask_BxSxS2_ik0"])
    w = {k: dram("w_" + k, a) for k, a in consts.items()}
    o = nc.dram_tensor("out", (B, S, D), F32, kind="ExternalOutput").ap()
    build(nc, xd, cm, ct, m1, m3, w, o)
    r = run_bass_kernel_spmd(nc, [arrays], core_ids=[0])
    return r.results[0]["out"]
```

```python
from contextlib import ExitStack

import concourse.bass as bass
from concourse import mybir

F32 = mybir.dt.float32
BF16 = mybir.dt.bfloat16
U8 = mybir.dt.uint8
U32 = mybir.dt.uint32
I32 = mybir.dt.int32
ALU = mybir.AluOpType
ACT = mybir.ActivationFunctionType
AX = mybir.AxisListType

P = 128
B, S, D = 4, 256, 128
T = S // P
EPS = 1e-5
BIG = 1e30

H = 16
HS0 = 64
HS = 8
C0 = H * HS0 // P
NQ = 6

E0, F0 = 8, 512
E1, F1, CAP = 16, 256, 32
E2, F2 = 8, 512
SLOPES = [2.0 ** (-0.5 * (h + 1)) for h in range(H)]

K = 16
W = S // K
LAG = 2
STEPS = S + LAG * (K - 1)



def build(nc, x, ctxm, ctxT, mask1, mask3, w, out):
    LN_A, LN_B, XT_B = 5, 3, 2
    XD_A, XD_B = 5, 3
    with ExitStack() as ctx:
        def sb(name, shape, dt=F32):
            return ctx.enter_context(nc.sbuf_tensor(name, shape, dt))

        def sem(name):
            return ctx.enter_context(nc.semaphore(name))

        bank = [ctx.enter_context(nc.psum_tensor(f"bank{i}", [P, 512], F32)) for i in range(8)]
        bS, bT, bO, bLN, bY = bank[0:2], bank[2:4], bank[4:6], bank[6], bank[7]

        X = sb("X", [P, B * T * D])
        CT = sb("CT", [P, (B + 1) * S])
        XNT = sb("XNT", [P, (B + 1) * S])
        xb = sb("xb", [P, T * D])
        xn = sb("xn", [P, T * D])
        xnT = sb("xnT", [P, S])
        ctb = sb("ctb", [P, S])
        ident = sb("ident", [P, P])
        identb = sb("identb", [P, P], BF16)
        ones = sb("ones", [P, 256])
        rows = sb("rows", [1, 5 * P])
        dmask = sb("dmask", [P, T * S])
        mbig = sb("mbig", [P, T * S])
        mload = dmask[:, :].bitcast(I32)
        m8 = sb("m8", [P, T * S], U8)
        cosT = sb("cosT", [P, S])
        sinT = sb("sinT", [P, S])
        qb1 = sb("qb1", [P, 4])
        qb3 = sb("qb3", [P, 2])
        wqk1 = sb("wqk1", [P, 4 * P])
        wvo1 = sb("wvo1", [P, 3 * P])
        rt0 = sb("rt0", [P, E0])
        rt1 = sb("rt1", [P, E1])
        rt2 = sb("rt2", [P, E2])
        b1t = sb("b1t", [P, E2 * 4])
        b2t = sb("b2t", [E2, D])
        iota8 = sb("iota8", [P, 8])
        hmask = sb("hmask", [P, 2 * H])
        iota32 = sb("iota32", [P, CAP])
        inj = sb("inj", [P, 1])

        WA = 4 * 1024 + 3 * E0 * F0 + 3 * (E1 + 1) * F1
        arena = sb("arena", [P, WA])
        at = [0]

        def take(n):
            at[0] += n
            assert at[0] <= WA
            return arena[:, at[0] - n:at[0]]

        w0 = [take(1024) for _ in range(4)]
        f0g, f0u, f0d = take(E0 * F0), take(E0 * F0), take(E0 * F0)
        f1g, f1u, f1d = (take((E1 + 1) * F1) for _ in range(3))
        at[0] = 0
        dnat = take(S * W)
        f2d = dnat
        dskew = take(STEPS * W)
        f2u = dskew[:, 0:E2 * F2]
        edge = take(STEPS * W).bitcast(BF16)
        stay = take(STEPS * (W + 1)).bitcast(BF16)
        onc = take(STEPS * W // 2).bitcast(BF16)
        onu = take(S * W // 2).bitcast(BF16)
        onT = take(T * B * S)
        cnat = take(B * T * D)
        wqk3 = take(2 * P)
        wvo3 = take(3 * P)

        work = sb("work", [P, 8192])
        qT, kT, V, cx = (work[:, 2048 * i:2048 * (i + 1)] for i in range(4))
        probs = sb("probs", [P, 2, 512])
        probsT = sb("probsT", [P, 2, 512])
        logit = sb("logit", [P, 2, 512])
        cxT = cx
        qz = qT[:, 512:512 + NQ * S]
        hid = qT
        sil = probs
        oneh, wone = kT[:, 0:1024], kT[:, 1024:2048]
        hslot = oneh
        woneT = V[:, 0:1024]
        xgT, eout = V[:, 1024:1536], V[:, 1536:2048]
        stt = sb("stt", [P, T * 6])
        mv = sb("mv", [P, T * 2])
        ve = sb("ve", [P, 2])
        neghalf = sb("neghalf", [P, 2])
        tiny = sb("tiny", [P, 1])
        rstd = sb("rstd", [P, 2])
        nmx = sb("nmx", [P, H * T])
        nmz = sb("nmz", [P, H * T])
        sums = sb("sums", [P, H * T])
        rsum = sb("rsum", [P, H * T])
        rwide = sb("rwide", [P, 2, S])
        rinv = sb("rinv", [P, 512])
        lg = sb("lg", [P, T * 16])
        v8 = sb("v8", [P, T * 8])
        ix = sb("ix", [P, T * 8], U32)
        ixf = sb("ixf", [P, T * 8])
        sm = sb("sm", [P, 8])
        coef = sb("coef", [P, T * 16])
        norms = sb("norms", [P, S + W])
        best = sb("best", [P, W])
        qiT = sb("qiT", [P, S], BF16)
        sel = cx[0:E1, 0:4 * S]
        top = sb("top", [16, 8 * 4])
        slot = sb("slot", [P, T * 16])
        coefT = sb("coefT", [8, S])
        tern = sb("tern", [P, D])
        ternT = sb("ternT", [P, D], BF16)
        pk = sb("pk", [P, D], I32)
        wscale = sb("wscale", [P, 1])
        fb3 = sb("fb3", [P, D])
        qi = sb("qi", [P, T * D], BF16)

        names = """
            ld_x ld_b ld_first ld_l0 ld_f0 ld_l1 ld_f1 ld_late ld_f2d ld_f2u
            consts ident_zero stored x_back
            x_done ctb_ready var_ready rstd_ready xn_ready xnT_full xnT_ready
            p0_full p0_act p0_dve y0_out y1_out y3_out v_zero
            p1_full p1_dve p1_act p3_full p3_dve p3_act
            f0_logit f0_nmax f0_prob f0_gu f0_silu f0_hid f0_down f0_acc
            f1_logit f1_exp f1_score f1_byexp f1_slot f1_slotT f1_oneh f1_wone
            f1_sh_gu f1_sh_gelu f1_sh_hid f1_gath f1_xg f1_gu f1_gelu f1_hs f1_hT f1_hid
            f1_wT f1_wTc f1_down f1_eout f1_y
            f2_logit f2_exp f2_coef f2_cT f2_cTc f2_up f2_hidA f2_hidD f2_down f2_acc f2_y
            mask_loaded x_out f2_diff sq_ready norms_full norms_ready
            d_full d_lin d_pos d_ln d_inv d_inv2 d_newton d_done best_ready on_ready
            skew_set stay_set onu_set pv_set cost_set
            skew0 skew1 skew2 skew3 forward moves_ready backward on_kept unskewed
            identb_ready onT_full onT_ready expanded tern_ready ternT_full ternT_ready f3_q f3_qT f3_qTc f3_y
        """.split()
        for a in ("a0", "a1", "a3"):
            names += [f"{a}_{n}" for n in "scores nmax exp pt ptA ptD pv rsum rfull rinv norm".split()]
        names += ["a1_q", "a3_q"]
        sm_ = {n: sem(n) for n in names}
        dve_chain, act_chain, pool_chain = sem("dve_chain"), sem("act_chain"), sem("pool_chain")
        block = ctx.enter_context(nc.Block())

        class Count:

            def __init__(self, eng, b, loop):
                self.eng, self.b, self.loop = eng, b, loop

            def wait(self, name, per, n):
                base = BASE[self.loop].get(name, 0)
                self.eng.wait_ge(sm_[name], self.b * per + (base + n))

        class Chain:

            def __init__(self, eng, s):
                self.eng, self.s, self.n = eng, s, 0

            def restart(self):
                self.eng.sem_clear(self.s)
                self.n = 0

            def empty(self):
                self.n += 1
                self.eng.sem_inc(self.s, 1)
                self.eng.wait_ge(self.s, self.n)

            def __call__(self, ins):
                self.n += 1
                ins.then_inc(self.s, 1)
                self.eng.wait_ge(self.s, self.n)

        BASE = {"A": {}, "B": {n: B * LN_A for n in ("var_ready", "rstd_ready", "xnT_full", "xnT_ready")}
                | {"xn_ready": T * B * LN_A, "x_done": B * XD_A, "ctb_ready": B + 1, "v_zero": B}}

        def v3(ap, c):
            return ap.rearrange("p (a c) -> p a c", c=c)

        y_at = [bY[:, 0:D], bLN[:, 0:D]]

        def add_y(dve):
            for t in range(T):
                v = xb[:, t * D:(t + 1) * D]
                last = dve.tensor_tensor(v, v, y_at[t], ALU.add)
            return last

        def ln_dve(dve, q, link, loop, s):
            per = LN_A if loop == "A" else LN_B
            for t in range(T):
                last = dve.bn_stats(stt[:, 6 * t:6 * t + 6], xb[:, t * D:(t + 1) * D])
            link(last)
            for t in range(T):
                last = dve.bn_aggr(mv[:, 2 * t:2 * t + 2], stt[:, 6 * t:6 * t + 6])
            link(last)
            dve.tensor_scalar(ve[:, :], mv[:, 1:4:2], EPS, None, ALU.add).then_inc(sm_["var_ready"], 1)
            q.wait("rstd_ready", per, s + 1)
            for t in range(T):
                last = dve.tensor_scalar(xn[:, t * D:(t + 1) * D], xb[:, t * D:(t + 1) * D],
                                         mv[:, 2 * t:2 * t + 1], rstd[:, t:t + 1], ALU.subtract, ALU.mult)
                last.then_inc(sm_["xn_ready"], 1)

        def ln_pool(pool, q, loop, s):
            per = LN_A if loop == "A" else LN_B
            q.wait("var_ready", per, s + 1)
            pool.tensor_tensor(rstd[:, :], ve[:, :], neghalf[:, :], ALU.pow).then_inc(sm_["rstd_ready"], 1)

        def ln_pe(pe, q, loop, s):
            for t in range(T):
                q.wait("xn_ready", T * (LN_A if loop == "A" else LN_B), T * s + t + 1)
                last = pe.transpose(bLN[:, t * P:(t + 1) * P], xn[:, t * D:(t + 1) * D], ident[:, :])
            last.then_inc(sm_["xnT_full"], 1)

        def ln_act_copy(act, q, loop, s):
            q.wait("xnT_full", LN_A if loop == "A" else XT_B, s + 1)
            act.copy(xnT[:, :], bLN[:, 0:S]).then_inc(sm_["xnT_ready"], 1)

        NP = H // 2
        scores_at = [*bS, bLN, bY]
        probsT_at = {"a0": [probsT[:, 0, :], probsT[:, 1, :], logit[:, 0, :], logit[:, 1, :]],
                     "a1": [probsT[:, 0, :], probsT[:, 1, :], cx[:, 512:1024], cx[:, 1024:1536]]}
        probsT_at["a3"] = probsT_at["a1"]

        def pt_ready(q, a, g):
            q.wait(a + ("_ptD" if g % 2 else "_ptA"), NP, g // 2 + 1)

        def att_pe(pe, q, a, hs):
            pts = probsT_at[a]
            for p in range(NP + 2):
                if p < NP:
                    if hs == HS:
                        q.wait(a + "_q", H, 2 * p + 2)
                    if p >= 2:
                        q.wait(a + ("_exp" if hs == HS0 else "_nmax"), H, 2 * p - 2)
                    for n in range(T):
                        for i in range(2):
                            h = 2 * p + i
                            if hs == HS0:
                                r = i * HS0
                                qh = qT[r:r + HS0, p * S + n * P:p * S + (n + 1) * P]
                                kh = kT[r:r + HS0, p * S:(p + 1) * S]
                            else:
                                o = (h % NQ) * S
                                qh, kh = qz[:, o + n * P:o + (n + 1) * P], kT[:, 0:S]
                            last = pe.matmul(scores_at[h % 4][:, n * S:(n + 1) * S], qh, kh, start=True, stop=True)
                            if n == T - 1:
                                last.then_inc(sm_[a + "_scores"], 1)
                if 1 <= p <= NP:
                    for g in (2 * p - 2, 2 * p - 1):
                        q.wait(a + "_exp", H, g + 1)
                        if g >= 2:
                            pt_ready(q, a, g - 2)
                        for m in range(T):
                            for n in range(T):
                                last = pe.transpose(bT[g % 2][:, (m * T + n) * P:(m * T + n + 1) * P],
                                                    probs[:, g % 2, n * S + m * P:n * S + (m + 1) * P], ident[:, :])
                        last.then_inc(sm_[a + "_pt"], 1)
                if p >= 2:
                    c = p - 2
                    pt_ready(q, a, 2 * c)
                    pt_ready(q, a, 2 * c + 1)
                    if hs == HS0:
                        if c >= 2:
                            q.wait(a + "_norm", NP, c - 1)
                    elif c == NP // 2:
                        q.wait(a + "_rinv", 2, 1)
                    for m in range(T):
                        for i in range(2):
                            g = 2 * c + i
                            if hs == HS0:
                                w_, o = HS0, bO[c % 2][i * HS0:(i + 1) * HS0, 0:S]
                                first, final = m == 0, m == T - 1
                            else:
                                r = m * 64 + i * 32
                                w_, o = 32, bO[c // 4][r:r + 32, 0:S]
                                first, final = c % 4 == 0, c % 4 == 3
                            vo = (m * H + g) * w_
                            last = pe.matmul(o, V[:, vo:vo + w_], pts[g % 4][:, m * S:(m + 1) * S],
                                             start=first, stop=final)
                    last.then_inc(sm_[a + "_pv"], 1)
                    if hs == HS0:
                        q.wait(a + "_rsum", NP, c + 1)
                        for t in range(T):
                            last = pe.matmul(bO[c % 2][:, S + t * P:S + (t + 1) * P],
                                             rwide[:, c % 2, t * P:(t + 1) * P], ident[:, :], start=True, stop=True)
                        last.then_inc(sm_[a + "_rfull"], 1)
                if hs == HS and p in (NP // 2 + 1, NP):
                    z = p // NP
                    q.wait(a + "_rsum", 2, z + 1)
                    if z:
                        q.wait(a + "_norm", 2, 1)
                    for t in range(T):
                        for m in range(T):
                            last = pe.matmul(bO[1 - z][m * 64:m * 64 + 64, S + t * P:S + (t + 1) * P],
                                             rwide[:, z, t * 64:(t + 1) * 64], ident[:, :], start=True, stop=True)
                    last.then_inc(sm_[a + "_rfull"], 1)

        def att_act(act, q, a, hs):
            pts = probsT_at[a]
            for p in range(NP + 3):
                if hs == HS0 and p >= 3:
                    c = p - 3
                    q.wait(a + "_rfull", NP, c + 1)
                    if c >= 2:
                        q.wait(a + "_norm", NP, c - 1)
                    act.copy(rinv[:, (c % 2) * S:(c % 2 + 1) * S], bO[c % 2][:, S:2 * S]).then_inc(sm_[a + "_rinv"], 1)
                for i in range(2):
                    if p < NP:
                        h = 2 * p + i
                        q.wait(a + "_nmax", H, h + 1)
                        if p >= 1:
                            q.wait(a + "_pt", H, h - 1)
                        for n in range(T):
                            lo, hi = n * S, (n + 1) * S
                            src = scores_at[h % 4][:, lo:hi] if hs == HS0 else logit[:, h % 2, lo:hi]
                            last = act.activation(probs[:, h % 2, lo:hi], src, ACT.Exp,
                                                  bias=nmx[:, T * h + n:T * h + n + 1],
                                                  scale=1.0 if hs == HS0 else -1.0,
                                                  accum_out=sums[:, T * h + n:T * h + n + 1])
                        last.then_inc(sm_[a + "_exp"], 1)
                    if 1 <= p <= NP and i == 0:
                        g = 2 * p - 2 + i
                        q.wait(a + "_pt", H, g + 1)
                        if g >= 4:
                            q.wait(a + "_pv", NP, (g - 4) // 2 + 1)
                        act.copy(pts[g % 4], bT[g % 2][:, :]).then_inc(sm_[a + "_ptA"], 1)
                if hs == HS and p in (NP // 2 + 1, NP + 1):
                    z = p // NP
                    q.wait(a + "_rfull", 2, z + 1)
                    act.copy(rinv[:, z * S:(z + 1) * S], bO[1 - z][:, S:2 * S]).then_inc(sm_[a + "_rinv"], 1)

        def att_dve(dve, q, link, a, hs, slopes, bias):
            pts = probsT_at[a]
            for p in range(NP + 3):
                for h in (2 * p, 2 * p + 1):
                    if h >= H:
                        continue
                    if hs == HS0:
                        q.wait(a + "_scores", H, h + 1)
                        dve.tensor_reduce(nmx[:, T * h:T * h + T], v3(scores_at[h % 4][:, :], S), AX.X, ALU.max,
                                          negate=True).then_inc(sm_[a + "_nmax"], 1)
                        continue
                    q.wait(a + "_scores", H, h + 1)
                    if h >= 2:
                        q.wait(a + "_exp", H, h - 1)
                    link.empty()
                    for n in range(T):
                        lo, hi = n * S, (n + 1) * S
                        last = dve.tensor_tensor_reduce(
                            out=logit[:, h % 2, lo:hi], in0=scores_at[h % 4][:, lo:hi], in1=bias[:, lo:hi],
                            scale=slopes[h], scalar=3e38, op0=ALU.add, op1=ALU.min,
                            accum_out=nmx[:, T * h + n:T * h + n + 1])
                    last.then_inc(sm_[a + "_nmax"], 1)
                if 1 <= p <= NP:
                    g = 2 * p - 1
                    q.wait(a + "_pt", H, g + 1)
                    if g >= 4:
                        q.wait(a + "_pv", NP, (g - 4) // 2 + 1)
                    dve.tensor_copy(pts[g % 4], bT[g % 2][:, :]).then_inc(sm_[a + "_ptD"], 1)
                if hs == HS:
                    if p in (NP // 2, NP):
                        z = p // NP
                        q.wait(a + "_exp", H, 8 * z + 8)
                        rs = rsum[:, 16 * z:16 * z + 16]
                        link(dve.reciprocal(rs, sums[:, 16 * z:16 * z + 16]))
                        for t in range(T):
                            for i in range(2):
                                dst = v3(rwide[:, z, t * 64 + i * 32:t * 64 + (i + 1) * 32], HS)
                                src = rs.rearrange("p (s i t) -> p s i t", s=4, i=2)[:, :, i, t]
                                last = dve.tensor_copy(dst, src.unsqueeze(2).to_broadcast([P, 4, HS]))
                        last.then_inc(sm_[a + "_rsum"], 1)
                    if p in (NP // 2 + 2, NP + 2):
                        z = p // NP
                        q.wait(a + "_pv", NP, NP // 2 * (z + 1))
                        q.wait(a + "_rinv", 2, z + 1)
                        dve.tensor_tensor(cx[:, z * S:(z + 1) * S], bO[z][:, 0:S], rinv[:, z * S:(z + 1) * S],
                                          ALU.mult).then_inc(sm_[a + "_norm"], 1)
                    continue
                if 1 <= p <= NP:
                    c = p - 1
                    q.wait(a + "_exp", H, 2 * c + 2)
                    rs = rsum[:, 2 * T * c:2 * T * (c + 1)]
                    link(dve.reciprocal(rs, sums[:, 2 * T * c:2 * T * (c + 1)]))
                    if c >= 2:
                        q.wait(a + "_rfull", NP, c - 1)
                    dve.tensor_copy(rwide[:, c % 2, :].rearrange("p (t h o) -> p t h o", t=T, o=HS0),
                                    rs.rearrange("p (h t) -> p t h", t=T).unsqueeze(3)
                                    .to_broadcast([P, T, 2, HS0])).then_inc(sm_[a + "_rsum"], 1)
                if p >= 3:
                    c = p - 3
                    q.wait(a + "_pv", NP, c + 1)
                    q.wait(a + "_rinv", NP, c + 1)
                    dve.tensor_tensor(cxT[:, c * S:(c + 1) * S], bO[c % 2][:, 0:S],
                                      rinv[:, (c % 2) * S:(c % 2 + 1) * S], ALU.mult).then_inc(sm_[a + "_norm"], 1)

        def att_pool(pool, q, a, ready, per, masks):
            q.wait(ready, per, per)
            pool.wait_ge(sm_["ld_l1"], 16 * 6)
            for h in range(H):
                if h >= NQ:
                    q.wait(a + "_scores", H, h - NQ + 1)
                o = (h % NQ) * S
                pool.tensor_tensor(qz[:, o:o + S], qT[:, 0:S],
                                   hmask[:, masks + h:masks + h + 1].to_broadcast([P, S]),
                                   ALU.mult).then_inc(sm_[a + "_q"], 1)

        def l0_pe(pe, q):
            banks = [*bS, *bT]
            q.wait("ctb_ready", 1, 1)
            pe.wait_ge(sm_["ld_l0"], 16 * 5)

            def room(f):
                if f >= 4:
                    q.wait("p0_dve" if (f - 4) % 2 else "p0_act", 6, (f - 4) // 2 + 1)

            def heads(f, wt, src):
                room(f)
                for c in range(2):
                    o = ((f % 4) * 2 + c) * P
                    last = pe.matmul(banks[f % 4][:, c * S:(c + 1) * S], wt[:, o:o + P], src[:, :],
                                     start=True, stop=True)
                last.then_inc(sm_["p0_full"], 1)

            for f in range(4):
                heads(f, w0[1], ctb)
            for f in range(4, 8):
                room(f)
                t, j = (f - 4) // 2, f % 2
                pe.matmul(banks[f % 4][:, :], ctb[:, t * P:(t + 1) * P], w0[2][:, j * 512:(j + 1) * 512],
                          start=True, stop=True).then_inc(sm_["p0_full"], 1)
            ln_pe(pe, q, "A", 0)
            q.wait("xnT_ready", LN_A, 1)
            for f in range(8, 12):
                heads(f, w0[0], xnT)
            q.wait("p0_act", 6, 6)
            q.wait("p0_dve", 6, 6)
            att_pe(pe, q, "a0", HS0)
            for c in range(C0):
                q.wait("a0_norm", NP, c + 1)
                for t in range(T):
                    pe.matmul(y_at[t], cxT[:, c * S + t * P:c * S + (t + 1) * P], w0[3][:, c * P:(c + 1) * P],
                              start=(c == 0), stop=False)
            for t in range(T):
                last = pe.matmul(y_at[t], ones[0:1, 0:P], rows[0:1, 0:P], start=False, stop=True)
            last.then_inc(sm_["y0_out"], 1)

        def l0_drain(q, f, copy, scaled):
            q.wait("p0_full", 12, f + 1)
            src = [*bS, *bT][f % 4][:, :]
            o = (f % 4) * 512
            if f < 4:
                return copy(kT[:, o:o + 512], src)
            if f < 8:
                return copy(V[:, o:o + 512], src)
            return scaled(qT[:, o:o + 512], src)

        def l0_act(act, q, link):

            def drain(f):
                l0_drain(q, f, act.copy, lambda o, i: act.mul(o, i, HS0 ** -0.5)).then_inc(sm_["p0_act"], 1)

            for f in (0, 2, 4, 6):
                drain(f)
            ln_act_copy(act, q, "A", 0)
            for f in (8, 10):
                drain(f)
            att_act(act, q, "a0", HS0)

        def l0_dve(dve, q, link):
            ln_dve(dve, q, link, "A", 0)

            def drain(f):
                l0_drain(q, f, dve.tensor_copy,
                         lambda o, i: dve.tensor_scalar(o, i, HS0 ** -0.5, None, ALU.mult)) \
                    .then_inc(sm_["p0_dve"], 1)

            for f in (1, 3, 5, 7, 9, 11):
                drain(f)
            att_dve(dve, q, link, "a0", HS0, None, None)
            q.wait("y0_out", 1, 1)
            add_y(dve).then_inc(sm_["x_done"], 1)

        def f0_pe(pe, q):
            ln_pe(pe, q, "A", 1)
            q.wait("xnT_ready", LN_A, 2)
            pe.wait_ge(sm_["ld_first"], 16 * N_FIRST)
            for t in range(T):
                last = pe.matmul(bLN[:, 256 + t * 8:264 + t * 8], xnT[:, t * P:(t + 1) * P], rt0[:, :],
                                 start=True, stop=True)
            last.then_inc(sm_["f0_logit"], 1)
            pe.wait_ge(sm_["ld_f0"], 16 * 6)

            def down(e):
                q.wait("f0_hid", 2 * E0, 2 * e + 2)
                if e >= 2:
                    q.wait("f0_acc", E0 - 1, e - 1)
                for t in range(T):
                    for c in range(4):
                        last = pe.matmul(bO[e % 2][:, t * D:(t + 1) * D],
                                         hid[:, (e % 2) * 1024 + c * S + t * P:(e % 2) * 1024 + c * S + (t + 1) * P],
                                         f0d[:, (e * 4 + c) * D:(e * 4 + c + 1) * D], start=(c == 0), stop=(c == 3))
                last.then_inc(sm_["f0_down"], 1)

            for e in range(E0):
                for j in range(2):
                    n = 2 * e + j
                    if n >= 2:
                        q.wait("f0_hid", 2 * E0, n - 1)
                    for wt, bk in ((f0g, bS), (f0u, bT)):
                        for c in range(2):
                            o = e * F0 + (2 * j + c) * P
                            last = pe.matmul(bk[n % 2][:, c * S:(c + 1) * S], wt[:, o:o + P], xnT[:, :],
                                             start=True, stop=True)
                    last.then_inc(sm_["f0_gu"], 1)
                if e:
                    down(e - 1)
            down(E0 - 1)

        def f0_act(act, q, link):
            ln_act_copy(act, q, "A", 1)
            q.wait("f0_nmax", 1, 1)
            for t in range(T):
                last = act.activation(v8[:, 8 * t:8 * t + 8], lg[:, 8 * t:8 * t + 8], ACT.Exp,
                                      bias=nmz[:, t:t + 1], accum_out=sm[:, t:t + 1])
            last.then_inc(sm_["f0_prob"], 1)
            for n in range(2 * E0):
                q.wait("f0_gu", 2 * E0, n + 1)
                if n >= 2:
                    q.wait("f0_hid", 2 * E0, n - 1)
                act.activation(sil[:, n % 2, :], bS[n % 2][:, :], ACT.Silu).then_inc(sm_["f0_silu"], 1)

        def top_index(dve, link, ne):
            for t in range(T):
                last = dve.max(v8[:, 8 * t:8 * t + 8], lg[:, ne * t:ne * t + ne])
            link(last)
            for t in range(T):
                last = dve.max_index(ix[:, 8 * t:8 * t + 8], v8[:, 8 * t:8 * t + 8], lg[:, ne * t:ne * t + ne])
            link(last)
            link(dve.tensor_copy(ixf[:, :], ix[:, :]))

        def f0_dve(dve, q, link):
            ln_dve(dve, q, link, "A", 1)
            q.wait("f0_logit", 1, 1)
            dve.wait_ge(sm_["ld_first"], 16 * N_FIRST)
            link(dve.tensor_copy(lg[:, 0:T * 8], bLN[:, 256:256 + T * 8]))
            top_index(dve, link, E0)
            dve.tensor_scalar(nmz[:, 0:T], v8[:, 0:T * 8:8], -1.0, None, ALU.mult).then_inc(sm_["f0_nmax"], 1)
            q.wait("f0_prob", 1, 1)
            link(dve.reciprocal(sm[:, 2:4], sm[:, 0:2]))
            link(dve.tensor_scalar(sm[:, 4:6], sm[:, 2:4], 2.0, None, ALU.mult))
            for t in range(T):
                last = dve.tensor_scalar(coef[:, 8 * t:8 * t + 8], iota8[:, :], ixf[:, 8 * t:8 * t + 1],
                                         sm[:, 4 + t:5 + t], ALU.is_equal, ALU.mult)
            link(last)
            link(dve.memset(coef[:, 7:16:8], 1.0))
            for n in range(2 * E0 + 2):
                if n < 2 * E0:
                    e, j = n // 2, n % 2
                    q.wait("f0_silu", 2 * E0, n + 1)
                    if e >= 2:
                        q.wait("f0_down", E0, e - 1)
                    o = (e % 2) * 1024 + j * 512
                    dve.tensor_tensor(hid[:, o:o + 512], sil[:, n % 2, :], bT[n % 2][:, :],
                                      ALU.mult).then_inc(sm_["f0_hid"], 1)
                if n >= 2 and n % 2 == 1:
                    e = (n - 2) // 2
                    q.wait("f0_down", E0, e + 1)
                    if e:
                        q.wait("f0_acc", E0 - 1, e)
                    for t in range(T):
                        last = dve.scalar_tensor_tensor(
                            out=xb[:, t * D:(t + 1) * D], in0=bO[e % 2][:, t * D:(t + 1) * D],
                            scalar=coef[:, 8 * t + e:8 * t + e + 1], in1=xb[:, t * D:(t + 1) * D],
                            op0=ALU.mult, op1=ALU.add)
                    last.then_inc(sm_["f0_acc" if e < E0 - 1 else "x_done"], 1)

        def proj(pe, o, wt, src):
            return pe.matmul(o, wt, src[:, :], start=True, stop=True)

        def values(pe, bk, wv, brow):
            for t in range(T):
                pe.matmul(bk[:, t * D:(t + 1) * D], ctb[:, t * P:(t + 1) * P], wv, start=True, stop=False)
                last = pe.matmul(bk[:, t * D:(t + 1) * D], ones[0:1, 0:P], rows[0:1, brow * P:(brow + 1) * P],
                                 start=False, stop=True)
            return last

        def values_act(act, q):
            q.wait("v_zero", 1, 1)
            for t in range(T):
                for i in range(2):
                    vt = V[:, t * 512:(t + 1) * 512].rearrange("p (z x e) -> p z x e", z=2, e=HS)
                    src = bO[0][:, t * D:(t + 1) * D].rearrange("p (z s i e) -> p z s i e", z=2, s=4, i=2)
                    last = act.copy(vt[:, :, 4 * i:4 * i + 28:9, :], src[:, :, :, i, :])
            return last

        def attn_out(pe, q, k, wo, brow, name_y):
            for z in range(2):
                q.wait(f"a{k}_norm", 2, z + 1)
                for t in range(T):
                    pe.matmul(y_at[t], cx[:, z * S + t * P:z * S + (t + 1) * P],
                              wo[:, z * D:(z + 1) * D], start=(z == 0), stop=False)
            for t in range(T):
                last = pe.matmul(y_at[t], ones[0:1, 0:P], rows[0:1, brow * P:(brow + 1) * P], start=False, stop=True)
            last.then_inc(sm_[name_y], 1)

        def l1_pe(pe, q):
            q.wait("x_done", XD_A, 3)
            pe.wait_ge(sm_["ld_l1"], 16 * 6)

            def pair(bk, wt, src):
                for sw in range(2):
                    last = proj(pe, bk[:, sw * S:(sw + 1) * S], wqk1[:, (wt + sw) * P:(wt + sw + 1) * P], src)
                last.then_inc(sm_["p1_full"], 1)

            pair(bS[0], 2, ctb)
            values(pe, bO[0], wvo1[:, 0:P], 1).then_inc(sm_["p1_full"], 1)
            ln_pe(pe, q, "A", 2)
            q.wait("xnT_ready", LN_A, 3)
            pair(bS[1], 0, xnT)
            q.wait("p1_dve", 2, 2)
            q.wait("p1_act", 1, 1)
            att_pe(pe, q, "a1", HS)
            attn_out(pe, q, 1, wvo1[:, P:3 * P], 2, "y1_out")

        def l1_act(act, q, link):
            q.wait("p1_full", 3, 2)
            values_act(act, q).then_inc(sm_["p1_act"], 1)
            ln_act_copy(act, q, "A", 2)
            att_act(act, q, "a1", HS)

        def l1_dve(dve, q, link):
            ln_dve(dve, q, link, "A", 2)

            dve.wait_ge(sm_["ld_l1"], 16 * 6)

            def rope(dst, bk, qb, full):
                q.wait("p1_full", 3, full)
                for sw, tab in ((0, cosT), (1, sinT)):
                    last = dve.scalar_tensor_tensor(
                        out=logit[:, 0, sw * S:(sw + 1) * S], in0=bk[:, sw * S:(sw + 1) * S],
                        scalar=qb1[:, qb + sw:qb + sw + 1], in1=tab[:, :], op0=ALU.add, op1=ALU.mult)
                link(last)
                dve.tensor_tensor(dst[:, 0:S], logit[:, 0, 0:S], logit[:, 0, S:2 * S],
                                  ALU.add).then_inc(sm_["p1_dve"], 1)

            rope(kT, bS[0], 2, 1)
            q.wait("p1_dve", 2, 1)
            rope(qT, bS[1], 0, 3)
            att_dve(dve, q, link, "a1", HS, SLOPES, dmask)
            q.wait("y1_out", 1, 1)
            add_y(dve).then_inc(sm_["x_done"], 1)

        NE = E1 * CAP

        def f1_pe(pe, q):
            ln_pe(pe, q, "A", 3)
            q.wait("xnT_ready", LN_A, 4)
            pe.wait_ge(sm_["ld_f1"], 16 * 5)
            for t in range(T):
                last = pe.matmul(bLN[:, 256 + t * E1:256 + (t + 1) * E1], xnT[:, t * P:(t + 1) * P], rt1[:, :],
                                 start=True, stop=True)
            last.then_inc(sm_["f1_logit"], 1)
            q.wait("f1_score", 1, 1)
            for t in range(T):
                last = pe.transpose(bY[0:E1, t * P:(t + 1) * P], coef[:, t * E1:(t + 1) * E1], ident[:, :])
            last.then_inc(sm_["f1_byexp"], 1)
            for wt, bk in ((f1g, bT[0]), (f1u, bT[1])):
                for j in range(2):
                    o = E1 * F1 + j * P
                    last = pe.matmul(bk[:, j * S:(j + 1) * S], wt[:, o:o + P], xnT[:, :], start=True, stop=True)
            last.then_inc(sm_["f1_sh_gu"], 1)
            q.wait("f1_slot", 1, 1)
            for t in range(T):
                last = pe.matmul(bLN[:, 256 + t * E1:256 + (t + 1) * E1], sel[:, S + t * P:S + (t + 1) * P],
                                 ident[0:E1, 0:E1], start=True, stop=True)
            last.then_inc(sm_["f1_slotT"], 1)
            for t in range(T):
                q.wait("f1_oneh", T, t + 1)
                last = pe.matmul(bS[0][:, :], xn[:, t * D:(t + 1) * D], oneh[:, t * NE:(t + 1) * NE],
                                 start=(t == 0), stop=(t == T - 1))
            last.then_inc(sm_["f1_gath"], 1)
            q.wait("f1_sh_hid", 1, 1)
            q.wait("f1_wone", 1, 1)
            for g in range(4):
                for t in range(T):
                    last = pe.transpose(bT[g // 2][:, (g % 2) * S + t * P:(g % 2) * S + (t + 1) * P],
                                        wone[:, t * NE + g * P:t * NE + (g + 1) * P], ident[:, :])
            last.then_inc(sm_["f1_wT"], 1)
            q.wait("f1_xg", 1, 1)
            for z in range(2):
                for g in range(2):
                    for wt, bk in ((f1g, bS[z]), (f1u, bO[z])):
                        for e in range(8 * z + 4 * g, 8 * z + 4 * g + 4):
                            r = 32 * (e % 4)
                            last = pe.matmul(bk[r:r + CAP, g * F1:(g + 1) * F1], xgT[:, e * CAP:(e + 1) * CAP],
                                             wt[:, e * F1:(e + 1) * F1], start=True, stop=True)
                last.then_inc(sm_["f1_gu"], 1)
            for j in range(2):
                for t in range(T):
                    pe.matmul(y_at[t], hid[:, j * S + t * P:j * S + (t + 1) * P],
                              f1d[:, (2 * E1 + j) * D:(2 * E1 + j + 1) * D], start=(j == 0), stop=False)
            q.wait("f1_wTc", 1, 1)
            for z in range(2):
                q.wait("f1_hs", 2, z + 1)
                for g in range(2):
                    for j in range(2):
                        o = (2 * z + g) * P
                        last = pe.transpose(bT[j][:, o:o + P],
                                            hslot[:, (2 * z + g) * F1 + j * P:(2 * z + g) * F1 + (j + 1) * P],
                                            ident[:, :])
            last.then_inc(sm_["f1_hT"], 1)
            q.wait("f1_hid", 2, 2)
            for e in range(E1):
                r = 32 * (e % 4)
                for j in range(2):
                    o = 512 + j * 512 + e * CAP
                    last = pe.matmul(bS[0][r:r + CAP, (e // 4) * D:(e // 4 + 1) * D], hid[:, o:o + CAP],
                                     f1d[:, (e * 2 + j) * D:(e * 2 + j + 1) * D], start=(j == 0), stop=(j == 1))
            last.then_inc(sm_["f1_down"], 1)
            q.wait("f1_eout", 1, 1)
            for t in range(T):
                for g in range(4):
                    last = pe.matmul(y_at[t], woneT[:, g * S + t * P:g * S + (t + 1) * P], eout[:, g * D:(g + 1) * D],
                                     start=False, stop=(g == 3))
            last.then_inc(sm_["f1_y"], 1)

        def f1_act(act, q, link):
            ln_act_copy(act, q, "A", 3)
            q.wait("f1_logit", 2, 2)
            for t in range(T):
                last = act.activation(lg[:, t * E1:(t + 1) * E1], bLN[:, 256 + t * E1:256 + (t + 1) * E1], ACT.Exp,
                                      bias=nmz[:, t:t + 1], accum_out=sm[:, t:t + 1])
            last.then_inc(sm_["f1_exp"], 1)
            q.wait("f1_sh_gu", 1, 1)
            act.activation(sil[:, 0, :], bT[0][:, :], ACT.Gelu).then_inc(sm_["f1_sh_gelu"], 1)
            q.wait("f1_gath", 1, 1)
            act.copy(xgT, bS[0][:, :]).then_inc(sm_["f1_xg"], 1)
            q.wait("f1_wT", 1, 1)
            for i in range(2):
                last = act.copy(woneT[:, i * 512:(i + 1) * 512], bT[i][:, :])
            last.then_inc(sm_["f1_wTc"], 1)
            for j in range(2):
                q.wait("f1_gu", 2, j + 1)
                if j == 0:
                    q.wait("f1_sh_hid", 1, 1)
                act.activation(sil[:, j, :], bS[j][:, :], ACT.Gelu).then_inc(sm_["f1_gelu"], 1)
            q.wait("f1_hT", 1, 1)
            act.copy(hid[:, 512:1024], bT[0][:, :]).then_inc(sm_["f1_hid"], 1)
            q.wait("f1_down", 1, 1)
            act.copy(eout, bS[0][:, :]).then_inc(sm_["f1_eout"], 1)

        def f1_dve(dve, q, link):
            ln_dve(dve, q, link, "A", 3)
            q.wait("f1_logit", 2, 1)
            dve.tensor_reduce(nmz[:, 0:T], v3(bLN[:, 256:256 + T * E1], E1), AX.X, ALU.max,
                              negate=True).then_inc(sm_["f1_logit"], 1)
            q.wait("f1_exp", 1, 1)
            link(dve.reciprocal(sm[:, 2:4], sm[:, 0:2]))
            for t in range(T):
                last = dve.tensor_scalar(coef[:, t * E1:(t + 1) * E1], lg[:, t * E1:(t + 1) * E1],
                                         sm[:, 2 + t:3 + t], None, ALU.mult)
            last.then_inc(sm_["f1_score"], 1)
            q.wait("f1_byexp", 1, 1)
            link(dve.tensor_copy(sel[:, 0:S], bY[0:E1, 0:S]))
            for r in range(CAP // 8):
                cur, nxt = sel[:, (r % 2) * S:(r % 2 + 1) * S], sel[:, ((r + 1) % 2) * S:((r + 1) % 2 + 1) * S]
                link(dve.max(top[:, 8 * r:8 * r + 8], cur))
                link(dve.match_replace(nxt, top[:, 8 * r:8 * r + 8], cur, -1.0))
            link(dve.tensor_scalar(sel[:, 2 * S:3 * S], sel[:, 0:S], 0.0, None, ALU.is_lt))
            link(dve.tensor_tensor_scan(sel[:, 3 * S:4 * S], ones[0:E1, 0:S], sel[:, 2 * S:3 * S], 0.0,
                                        ALU.mult, ALU.add))
            dve.tensor_tensor(sel[:, S:2 * S], sel[:, 2 * S:3 * S], sel[:, 3 * S:4 * S],
                              ALU.mult).then_inc(sm_["f1_slot"], 1)
            q.wait("f1_sh_gelu", 1, 1)
            dve.tensor_tensor(hid[:, 0:512], sil[:, 0, :], bT[1][:, :], ALU.mult).then_inc(sm_["f1_sh_hid"], 1)
            q.wait("f1_slotT", 1, 1)
            dve.wait_ge(sm_["ld_f1"], 16 * 5)
            link(dve.tensor_copy(slot[:, :], bLN[:, 256:256 + T * E1]))
            o3, w3 = v3(oneh, CAP), v3(wone, CAP)
            for t in range(T):
                lo, hi = t * E1, (t + 1) * E1
                dve.tensor_tensor(o3[:, lo:hi], slot[:, lo:hi].unsqueeze(2).to_broadcast([P, E1, CAP]),
                                  iota32[:, :].unsqueeze(1).to_broadcast([P, E1, CAP]),
                                  ALU.is_equal).then_inc(sm_["f1_oneh"], 1)
            q.wait("f1_oneh", T, T)
            dve.tensor_tensor(w3, o3, coef[:, 0:T * E1].unsqueeze(2).to_broadcast([P, T * E1, CAP]),
                              ALU.mult).then_inc(sm_["f1_wone"], 1)
            for j in range(2):
                q.wait("f1_gelu", 2, j + 1)
                dve.tensor_tensor(hslot[:, 512 * j:512 * (j + 1)], sil[:, j, :], bO[j][:, :],
                                  ALU.mult).then_inc(sm_["f1_hs"], 1)
            q.wait("f1_hT", 1, 1)
            dve.tensor_copy(hid[:, 1024:1536], bT[1][:, :]).then_inc(sm_["f1_hid"], 1)
            q.wait("f1_y", 1, 1)
            add_y(dve).then_inc(sm_["x_done"], 1)

        banks4 = [*bS, *bT]
        sqc, sqx = work[:, 0:B * S], work[:, 1024:1024 + (B + 1) * S]
        DC, DCW = 4, S * W // 4
        d2 = edge.bitcast(F32)[:, 0:S * W]
        dinv = stay.bitcast(F32)[:, 0:S * W]
        dtmp = work[:, 2304:2304 + S * W]
        NROUND = W // 2
        KEEP = 11
        NKEEP = STEPS // KEEP
        assert NKEEP * KEEP == STEPS
        BW = W + 1
        SW = 2 * W + 2
        PW = 2 * W + 2
        PR = 3 * KEEP
        pv = work[:, 0:PR * PW].bitcast(BF16)
        cost = work[:, 0:(STEPS + 1) * BW]
        CH = 16
        chs = work[:, 6144:6144 + 3 * CH * W]
        chb = work[:, 7168:7168 + 2 * CH * W].bitcast(BF16)
        cost3 = cost.rearrange("p (s c) -> p s c", c=BW)
        edge4 = edge.rearrange("p (s c q) -> p s c q", c=W, q=2)
        stay3 = stay.rearrange("p (s c) -> p s c", c=SW)
        onc3 = onc.rearrange("p (s c) -> p s c", c=W)

        def small_act(act):
            act.wait_ge(sm_["ld_x"], 16 * 4)
            act.activation(sqc, CT[:, 0:B * S], ACT.Square).then_inc(sm_["sq_ready"], 1)

        def small_pe(pe):
            pe.wait_ge(sm_["sq_ready"], 1)
            for b in range(B):
                last = pe.matmul(bY[32 * b:32 * b + 32, 0:S], ones[:, 0:32], sqc[:, b * S:(b + 1) * S],
                                 start=True, stop=True)
            last.then_inc(sm_["norms_full"], 1)

        def small_dve(dve, link):
            dve.wait_ge(sm_["norms_full"], 1)
            link(dve.tensor_copy(norms[:, 0:S], bY[:, 0:S]))

        def dist_pe(pe):
            pe.wait_ge(sm_["xnT_ready"], B * LN_A)
            for r in range(NROUND):
                if r == 4:
                    pe.wait_ge(sm_["sq_ready"], 2)
                    for b in range(B):
                        for c in range(W):
                            o = b * S + c
                            last = pe.matmul(bY[32 * b:32 * b + 32, S + c:S + c + 1], sqx[:, o:o + 31 * W + 1:W],
                                             ones[:, 0:1], start=True, stop=True)
                    last.then_inc(sm_["norms_full"], 1)
                if r >= 4:
                    pe.wait_ge(sm_["d_lin"], r - 3)
                for b in range(B):
                    for c in range(2):
                        o = b * S + 2 * r + c
                        last = pe.matmul(banks4[r % 4][32 * b:32 * b + 32, c * S:(c + 1) * S],
                                         XNT[:, o:o + 31 * W + 1:W], CT[:, b * S:(b + 1) * S],
                                         start=True, stop=True)
                last.then_inc(sm_["d_full"], 1)

        def dist_dve(dve, link):
            for r in range(NROUND):
                dve.wait_ge(sm_["d_full"], r + 1)
                for c in range(2):
                    o = (2 * r + c) * S
                    last = dve.scalar_tensor_tensor(out=d2[:, o:o + S], in0=banks4[r % 4][:, c * S:(c + 1) * S],
                                                    scalar=-2.0, in1=norms[:, 0:S], op0=ALU.mult, op1=ALU.add)
                last.then_inc(sm_["d_lin"], 1)
                if r == 3:
                    dve.wait_ge(sm_["norms_full"], 2)
                    dve.tensor_copy(norms[:, S:S + W], bY[:, S:S + W]).then_inc(sm_["norms_ready"], 1)
            for k in range(DC):
                a, y = (v[:, k * DCW:(k + 1) * DCW] for v in (d2, dinv))
                t = dtmp[:, k * DCW:(k + 1) * DCW]
                dve.wait_ge(sm_["d_inv2"], k + 1)
                link(dve.scalar_tensor_tensor(out=t, in0=t, scalar=-0.5, in1=a, op0=ALU.mult, op1=ALU.mult))
                dve.scalar_tensor_tensor(out=t, in0=t, scalar=1.5, in1=y, op0=ALU.add,
                                         op1=ALU.mult).then_inc(sm_["d_newton"], 1)
            dve.wait_ge(sm_["d_done"], DC)

        def dist_act(act):
            act.wait_ge(sm_["ld_b"], 16 * 11)
            act.activation(sqx, XNT[:, :], ACT.Square).then_inc(sm_["sq_ready"], 1)
            act.wait_ge(sm_["norms_ready"], 1)
            for r in range(NROUND):
                act.wait_ge(sm_["d_lin"], r + 1)
                for c in range(2):
                    w_ = 2 * r + c
                    last = act.activation(d2[:, w_ * S:(w_ + 1) * S], d2[:, w_ * S:(w_ + 1) * S], ACT.Relu,
                                          bias=norms[:, S + w_:S + w_ + 1])
                last.then_inc(sm_["d_pos"], 1)
                if r % 2 == 1:
                    k = r // 2
                    act.wait_ge(sm_["d_pos"], r + 1)
                    act.activation(dinv[:, k * DCW:(k + 1) * DCW], d2[:, k * DCW:(k + 1) * DCW], ACT.Ln,
                                   bias=tiny[:, :]).then_inc(sm_["d_ln"], 1)
            for k in range(DC):
                y = dinv[:, k * DCW:(k + 1) * DCW]
                act.wait_ge(sm_["d_ln"], k + 1)
                act.activation(y, y, ACT.Exp, scale=-0.5).then_inc(sm_["d_inv"], 1)
                act.wait_ge(sm_["d_inv"], k + 1)
                act.activation(dtmp[:, k * DCW:(k + 1) * DCW], y, ACT.Square).then_inc(sm_["d_inv2"], 1)

        def dist_pool(pool):
            pool.memset(dskew, BIG).then_inc(sm_["skew_set"], 1)
            pool.wait_ge(sm_["skew_set"], 1)
            dn = dnat.rearrange("p (i c) -> p c i", c=W)
            for k in range(DC):
                t = dtmp[:, k * DCW:(k + 1) * DCW]
                pool.wait_ge(sm_["d_newton"], k + 1)
                pool.tensor_tensor(dn[:, k * (W // DC):(k + 1) * (W // DC), :], t.rearrange("p (c i) -> p c i", i=S),
                                   d2[:, k * DCW:(k + 1) * DCW].rearrange("p (c i) -> p c i", i=S),
                                   ALU.mult).then_inc(sm_["d_done"], 1)
            pool.wait_ge(sm_["d_done"], DC)
            pool.memset(cost3[:, 0:1, :], BIG).then_inc(sm_["cost_set"], 1)
            pool.memset(cost3[:, 1:1 + LAG, 0:1], BIG).then_inc(sm_["cost_set"], 1)
            pool.wait_ge(sm_["cost_set"], 2)
            for b in range(B):
                pool.memset(cost[32 * b:32 * b + 1, 0:1], 0.0).then_inc(sm_["cost_set"], 1)
            pool.wait_ge(sm_["cost_set"], 2 + B)
            pool.memset(stay, 1.0).then_inc(sm_["stay_set"], 1)
            pool.memset(onu, 0.0).then_inc(sm_["onu_set"], 1)

        SKEW = [(0, 2), (2, 6), (6, 11), (11, K)]

        def skew(eng):
            eng.wait_ge(sm_["d_done"], DC)
            eng.wait_ge(sm_["skew_set"], 1)
            for n, (lo, hi) in enumerate(SKEW):
                for k in range(lo, hi):
                    eng.dma_start(dskew[k:P:32, LAG * k * W:(LAG * k + S) * W], dnat[k:P:32, :]) \
                        .then_inc(sm_[f"skew{n}"], 16)

        def unskew(eng):
            eng.wait_ge(sm_["onu_set"], 1)
            for k in reversed(range(K)):
                eng.wait_ge(sm_["on_kept"], NKEEP - LAG * k // KEEP)
                eng.dma_start(onu[k:P:32, :], onc[k:P:32, LAG * k * W:(LAG * k + S) * W]) \
                    .then_inc(sm_["unskewed"], 16)

        def forward_dve(dve, link):
            dve.wait_ge(sm_["cost_set"], 2 + B)
            marks = 0
            for s in range(STEPS):
                for n, (lo, hi) in enumerate(SKEW):
                    if s == LAG * lo:
                        dve.wait_ge(sm_[f"skew{n}"], 16 * (hi - lo))
                if s:
                    dve.wait_ge(sm_["forward"], s)
                dve.tensor_tensor(best[:, :], cost3[:, s, 1:BW], cost3[:, s, 0:W],
                                  ALU.min).then_inc(sm_["best_ready"], 1)
                marks += 1
                at_best = marks
                if 1 <= s <= STEPS - LAG:
                    dve.stream_shuffle(cost3[:, s + LAG, 0:1], cost3[:, s, W:BW],
                                       [31, *range(31)]).then_inc(sm_["best_ready"], 1)
                    marks += 1
                dve.wait_ge(sm_["best_ready"], at_best)
                dve.tensor_tensor_scan(cost3[:, s + 1, 1:BW], best[:, :], dskew[:, s * W:(s + 1) * W],
                                       cost3[:, s + 1, 0:1], ALU.min, ALU.add).then_inc(sm_["forward"], 1)
            dve.wait_ge(sm_["best_ready"], marks)

        TAIL = STEPS // CH * CH

        def moves(eng, lo, r, step, chs, chb):
            up, diag = cost3[:, lo:lo + r, 1:BW], cost3[:, lo:lo + r, 0:W]
            left = cost3[:, lo + 1:lo + 1 + r, 0:W]
            v4 = chs[:, 0:3 * r * W].rearrange("p (n s c) -> p n s c", n=3, c=W)
            eng.tensor_tensor(v4[:, 0], up, left, ALU.subtract)
            eng.tensor_tensor(v4[:, 1], diag, up, ALU.subtract)
            step(eng.tensor_tensor(v4[:, 2], diag, left, ALU.subtract))
            step(eng.tensor_scalar(chb[:, 0:3 * r * W], chs[:, 0:3 * r * W], 0.0, None, ALU.is_le))
            m, g1, g2 = (chb[:, i * r * W:(i + 1) * r * W].rearrange("p (s c) -> p s c", c=W) for i in range(3))
            by_diag, by_up = edge4[:, lo:lo + r, ::-1, 1], edge4[:, lo:lo + r, ::-1, 0]
            step(eng.tensor_tensor(by_diag, g1, g2, ALU.mult))
            other = chb[:, 3 * r * W:4 * r * W].rearrange("p (s c) -> p s c", c=W)
            step(eng.tensor_scalar(other, by_diag, -1.0, 1.0, ALU.mult, ALU.add))
            step(eng.tensor_tensor(by_up, m, other, ALU.mult))
            return eng.tensor_tensor(stay3[:, lo:lo + r, SW - 2:0:-2], other, by_up, ALU.subtract)

        def moves_pool(pool, link):
            for n in range(TAIL // CH):
                lo = n * CH
                pool.wait_ge(sm_["forward"], lo + CH)
                if lo == 0:
                    pool.wait_ge(sm_["stay_set"], 1)
                if lo == 5 * CH:
                    assert PR * PW <= (lo - 1) * BW
                    pool.memset(pv, 0.0).then_inc(sm_["pv_set"], 1)
                moves(pool, lo, CH, link, chs, chb).then_inc(sm_["moves_ready"], 1)
                pool.wait_ge(sm_["moves_ready"], n + 1)

        def moves_dve(dve, link):
            dve.wait_ge(sm_["forward"], STEPS)
            dve.wait_ge(sm_["stay_set"], 1)
            link(moves(dve, TAIL, STEPS - TAIL, link, work[:, 4900:5644], work[:, 5644:6144].bitcast(BF16)))

        def backward_dve(dve, link):
            moves_dve(dve, link)
            dve.wait_ge(sm_["moves_ready"], TAIL // CH)
            dve.wait_ge(sm_["pv_set"], 1)
            n = STEPS - LAG
            link(dve.stream_shuffle(stay3[:, 0:n, 0], stay3[:, LAG:STEPS, SW - 2], [*range(1, 32), 31]))
            link(dve.memset(stay3[:, n:STEPS, 0:1], 0.0))
            link(dve.tensor_copy(stay3[:, STEPS - 1, 0:1], inj[:, :]))
            pv4 = pv[:, :].rearrange("p (s q c) -> p s q c", q=2, c=PW)
            link(dve.tensor_copy(pv4[:, (STEPS - 1) % PR, 0, 0:1], inj[:, :]))
            marks = 0
            for s in reversed(range(STEPS)):
                r, nx = s % PR, (s + 1) % PR
                kept = (STEPS - s) // KEEP - 2
                if s % KEEP == 0 and kept > 0:
                    dve.wait_ge(sm_["on_kept"], kept)
                if s < STEPS - 1:
                    dve.wait_ge(sm_["backward"], STEPS - 1 - s)
                dve.tensor_tensor_scan(pv4[:, r, 0, 1:2 * W + 1], stay3[:, s, 0:2 * W], pv4[:, nx, 1, 0:2 * W],
                                       pv4[:, r, 0, 0:1], ALU.mult, ALU.add).then_inc(sm_["on_ready"], 1)
                marks += 1
                at_scan = marks
                if LAG - 1 <= s < STEPS - 1:
                    dve.stream_shuffle(pv4[:, (s + 1 - LAG) % PR, :, 0], pv4[:, nx, :, 2 * W],
                                       [*range(1, 32), 31]).then_inc(sm_["on_ready"], 1)
                    marks += 1
                dve.wait_ge(sm_["on_ready"], at_scan)
                dve.tensor_tensor(pv4[:, r, 1, 1:2 * W + 1].rearrange("p (c q) -> p c q", q=2), edge4[:, s],
                                  pv4[:, r, 0, 2:2 * W + 2:2].unsqueeze(2).to_broadcast([P, W, 2]),
                                  ALU.mult).then_inc(sm_["backward"], 1)
            dve.wait_ge(sm_["on_ready"], marks)

        def backward_act(act):
            pv4 = pv[:, :].rearrange("p (s q c) -> p s q c", q=2, c=PW)
            for i, g in enumerate(reversed(range(NKEEP))):
                act.wait_ge(sm_["backward"], (i + 1) * KEEP)
                a = (g * KEEP) % PR
                act.copy(onc3[:, g * KEEP:(g + 1) * KEEP, :],
                         pv4[:, a:a + KEEP, 0, 2:2 * W + 2:2]).then_inc(sm_["on_kept"], 1)

        def expand_pe(pe):
            pe.wait_ge(sm_["unskewed"], 16 * K)
            pe.wait_ge(sm_["identb_ready"], 1)
            for n in range(4):
                for c in range(W // 2):
                    o = (n // 2) * P * W + W - 1 - ((n % 2) * (W // 2) + c)
                    last = pe.transpose(banks4[n][:, :].bitcast(BF16)[:, c * P:(c + 1) * P],
                                        onu[:, o:o + (P - 1) * W + 1:W], identb[:, :])
                last.then_inc(sm_["onT_full"], 1)
            pe.wait_ge(sm_["onT_ready"], 4)
            pe.wait_ge(sm_["ld_late"], 16 * N_LATE)
            for b in range(B):
                for jt in range(T):
                    for h in range(T):
                        o = (h * B + b) * S + jt * P
                        last = pe.matmul(bO[b // 2][:, ((b % 2) * T + jt) * D:((b % 2) * T + jt + 1) * D],
                                         onT[:, o:o + P], cnat[:, (b * T + h) * D:(b * T + h + 1) * D],
                                         start=(h == 0), stop=(h == T - 1))
            last.then_inc(sm_["expanded"], 1)

        def expand_dve(dve, link):
            for n in range(4):
                dve.wait_ge(sm_["onT_full"], n + 1)
                src = banks4[n][:, :].bitcast(BF16).rearrange("p (c b k) -> p c b k", b=B, k=32)
                h = n // 2
                dst = onT[:, h * B * S:(h + 1) * B * S].rearrange("p (b k c) -> p b k c", b=B, c=W)
                for b in range(B):
                    last = dve.tensor_copy(dst[:, b, :, (n % 2) * (W // 2):(n % 2 + 1) * (W // 2)],
                                           src[:, :, b, 0:K].rearrange("p c k -> p k c"))
                last.then_inc(sm_["onT_ready"], 1)
            dve.wait_ge(sm_["expanded"], 1)
            for i in range(2):
                v = X[:, i * 512:(i + 1) * 512]
                last = dve.tensor_tensor(v, v, bO[i][:, :], ALU.add)
            link(last)

        def f2_pe(pe, q):
            ln_pe(pe, q, "B", 0)
            q.wait("xnT_ready", XT_B, 1)
            for t in range(T):
                last = pe.matmul(bLN[:, 256 + t * 8:264 + t * 8], xnT[:, t * P:(t + 1) * P], rt2[:, :],
                                 start=True, stop=True)
            last.then_inc(sm_["f2_logit"], 1)
            pe.wait_ge(sm_["ld_f2d"], 16)
            pe.wait_ge(sm_["ld_f2u"], 16)

            def down(e):
                q.wait("f2_hidA", E2, e + 1)
                q.wait("f2_hidD", E2, e + 1)
                if e >= 2:
                    q.wait("f2_acc", E2, e - 1)
                for t in range(T):
                    for c in range(4):
                        o = (e % 2) * 1024 + c * S + t * P
                        last = pe.matmul(bO[e % 2][:, t * D:(t + 1) * D], hid[:, o:o + P],
                                         f2d[:, (e * 4 + c) * D:(e * 4 + c + 1) * D], start=(c == 0), stop=(c == 3))
                last.then_inc(sm_["f2_down"], 1)

            for e in range(E2):
                for j in range(2):
                    n = 2 * e + j
                    if n >= 4:
                        q.wait("f2_hidD" if j else "f2_hidA", E2, e - 1)
                    for c in range(2):
                        o = e * F2 + (2 * j + c) * P
                        last = pe.matmul(banks4[n % 4][:, c * S:(c + 1) * S], f2u[:, o:o + P], xnT[:, :],
                                         start=True, stop=True)
                    last.then_inc(sm_["f2_up"], 1)
                if e == 1:
                    q.wait("f2_coef", 1, 1)
                    for t in range(T):
                        last = pe.transpose(bLN[0:E2, t * P:(t + 1) * P], coef[:, 8 * t:8 * t + 8], ident[:, :])
                    last.then_inc(sm_["f2_cT"], 1)
                if e:
                    down(e - 1)
            down(E2 - 1)
            q.wait("f2_cTc", 1, 1)
            for t in range(T):
                last = pe.matmul(bY[:, t * D:(t + 1) * D], coefT[:, t * P:(t + 1) * P], b2t[:, :],
                                 start=True, stop=True)
            last.then_inc(sm_["f2_y"], 1)

        def f2_act(act, q, link):
            ln_act_copy(act, q, "B", 0)
            q.wait("f2_diff", 1, 1)
            act.activation(sm[:, 2:4], sm[:, 0:2], ACT.Exp).then_inc(sm_["f2_exp"], 1)
            for e in range(E2):
                if e == 2:
                    q.wait("f2_cT", 1, 1)
                    act.copy(coefT[:, :], bLN[0:E2, 0:S]).then_inc(sm_["f2_cTc"], 1)
                q.wait("f2_up", 2 * E2, 2 * e + 1)
                if e >= 2:
                    q.wait("f2_down", E2, e - 1)
                for c in range(2):
                    o = (e % 2) * 1024 + c * S
                    last = act.activation(hid[:, o:o + S], banks4[(2 * e) % 4][:, c * S:(c + 1) * S], ACT.Relu,
                                          bias=b1t[:, e * 4 + c:e * 4 + c + 1])
                last.then_inc(sm_["f2_hidA"], 1)

        def f2_dve(dve, q, link):
            ln_dve(dve, q, link, "B", 0)
            q.wait("f2_logit", 1, 1)
            link(dve.tensor_copy(lg[:, 0:T * 8], bLN[:, 256:256 + T * 8]))
            top_index(dve, link, E2)
            dve.tensor_tensor(sm[:, 0:2], v8[:, 1:T * 8:8], v8[:, 0:T * 8:8],
                              ALU.subtract).then_inc(sm_["f2_diff"], 1)
            q.wait("f2_exp", 1, 1)
            link(dve.tensor_scalar(sm[:, 4:6], sm[:, 2:4], 1.0, None, ALU.add))
            link(dve.reciprocal(sm[:, 6:8], sm[:, 4:6]))
            link(dve.tensor_tensor(sm[:, 4:6], sm[:, 2:4], sm[:, 6:8], ALU.mult))
            for t in range(T):
                dve.tensor_scalar(coef[:, 8 * t:8 * t + 8], iota8[:, :], ixf[:, 8 * t:8 * t + 1],
                                  sm[:, 6 + t:7 + t], ALU.is_equal, ALU.mult)
                last = dve.tensor_scalar(coef[:, 16 + 8 * t:24 + 8 * t], iota8[:, :], ixf[:, 8 * t + 1:8 * t + 2],
                                         sm[:, 4 + t:5 + t], ALU.is_equal, ALU.mult)
            link(last)
            dve.tensor_tensor(coef[:, 0:16], coef[:, 0:16], coef[:, 16:32], ALU.add).then_inc(sm_["f2_coef"], 1)
            q.wait("f2_coef", 1, 1)
            for e in range(E2 + 2):
                if e < E2:
                    q.wait("f2_up", 2 * E2, 2 * e + 2)
                    if e >= 2:
                        q.wait("f2_down", E2, e - 1)
                    for c in range(2):
                        o = (e % 2) * 1024 + (2 + c) * S
                        last = dve.tensor_scalar(hid[:, o:o + S], banks4[(2 * e + 1) % 4][:, c * S:(c + 1) * S],
                                                 b1t[:, e * 4 + 2 + c:e * 4 + 3 + c], 0.0, ALU.add, ALU.max)
                    last.then_inc(sm_["f2_hidD"], 1)
                if 1 <= e <= E2:
                    p = e - 1
                    q.wait("f2_down", E2, p + 1)
                    if p:
                        q.wait("f2_acc", E2, p)
                    for t in range(T):
                        last = dve.scalar_tensor_tensor(
                            out=xb[:, t * D:(t + 1) * D], in0=bO[p % 2][:, t * D:(t + 1) * D],
                            scalar=coef[:, 8 * t + p:8 * t + p + 1], in1=xb[:, t * D:(t + 1) * D],
                            op0=ALU.mult, op1=ALU.add)
                    last.then_inc(sm_["f2_acc"], 1)
            q.wait("f2_acc", E2, E2)
            q.wait("f2_y", 1, 1)
            dve.tensor_tensor(xb[:, :], xb[:, :], bY[:, 0:T * D], ALU.add).then_inc(sm_["x_done"], 1)

        def l3_pe(pe, q):
            q.wait("ctb_ready", 1, 1)
            q.wait("x_done", XD_B, 2)
            proj(pe, bS[0][:, 0:S], wqk3[:, P:2 * P], ctb)
            values(pe, bO[0], wvo3[:, 0:P], 3).then_inc(sm_["p3_full"], 1)
            ln_pe(pe, q, "B", 1)
            q.wait("xnT_ready", XT_B, 2)
            proj(pe, bS[1][:, 0:S], wqk3[:, 0:P], xnT).then_inc(sm_["p3_full"], 1)
            q.wait("p3_act", 1, 1)
            q.wait("p3_dve", 1, 1)
            att_pe(pe, q, "a3", HS)
            attn_out(pe, q, 3, wvo3[:, P:3 * P], 4, "y3_out")

        def l3_act(act, q, link):
            q.wait("p3_full", 2, 1)
            act.activation(kT[:, 0:S], bS[0][:, 0:S], ACT.Identity, bias=qb3[:, 1:2])
            values_act(act, q).then_inc(sm_["p3_act"], 1)
            ln_act_copy(act, q, "B", 1)
            att_act(act, q, "a3", HS)

        def l3_dve(dve, q, link):
            ln_dve(dve, q, link, "B", 1)
            q.wait("mask_loaded", 16, 16)
            link(dve.tensor_scalar(mbig[:, :], mload, 0.0, BIG, ALU.is_equal, ALU.mult))
            q.wait("p3_full", 2, 2)
            dve.tensor_scalar(qT[:, 0:S], bS[1][:, 0:S], qb3[:, 0:1], None, ALU.add).then_inc(sm_["p3_dve"], 1)
            att_dve(dve, q, link, "a3", HS, [1.0] * H, mbig)
            q.wait("y3_out", 1, 1)
            add_y(dve).then_inc(sm_["x_done"], 1)

        def tern_dve(dve, link):
            dve.wait_ge(sm_["ld_b"], 16 * 11)
            for s in range(4):
                p = pk[32 * s:32 * s + 32, :]
                last = dve.tensor_scalar(p, p, 2 * s, 3, ALU.logical_shift_right, ALU.bitwise_and)
            link(last)
            dve.tensor_scalar(tern[:, :], pk[:, :], 1.0, None, ALU.subtract).then_inc(sm_["tern_ready"], 1)
            dve.wait_ge(sm_["ternT_full"], 1)
            dve.tensor_copy(ternT[:, :], bY[:, 0:D]).then_inc(sm_["ternT_ready"], 1)

        def tern_pe(pe):
            pe.wait_ge(sm_["tern_ready"], 1)
            pe.transpose(bY[:, 0:D], tern[:, :], ident[:, :]).then_inc(sm_["ternT_full"], 1)
            pe.wait_ge(sm_["ternT_ready"], 1)
            pe.wait_ge(sm_["ld_b"], 16 * 11)

        def f3_pe(pe, q):
            q.wait("f3_q", 1, 1)
            qp = bLN[:, :].bitcast(BF16)
            for t in range(T):
                last = pe.transpose(qp[:, t * P:(t + 1) * P], qi[:, t * D:(t + 1) * D], identb[:, :])
            last.then_inc(sm_["f3_qT"], 1)
            q.wait("f3_qTc", 1, 1)
            for t in range(T):
                last = pe.matmul(bY[:, t * D:(t + 1) * D], qiT[:, t * P:(t + 1) * P], ternT[:, :],
                                 start=True, stop=True)
            last.then_inc(sm_["f3_y"], 1)

        def f3_act(act, q, link):
            q.wait("f3_qT", 1, 1)
            act.copy(qiT[:, :], bLN[:, :].bitcast(BF16)[:, 0:S]).then_inc(sm_["f3_qTc"], 1)

        ROUND = 1.5 * 2.0 ** 23

        def f3_dve(dve, q, link, b):
            ln_dve(dve, q, link, "B", 2)
            q.wait("xn_ready", T * LN_B, T * 3)
            link(dve.tensor_reduce(sm[:, 0:2], v3(xn[:, :], D), AX.X, ALU.max, apply_absolute_value=True))
            link(dve.tensor_scalar(sm[:, 2:4], sm[:, 0:2], 1e-5, None, ALU.max))
            link(dve.reciprocal(sm[:, 4:6], sm[:, 2:4]))
            link(dve.tensor_scalar(sm[:, 0:2], sm[:, 4:6], 127.0, None, ALU.mult))
            for t in range(T):
                last = dve.tensor_scalar(cx[:, t * D:(t + 1) * D], xn[:, t * D:(t + 1) * D], sm[:, t:t + 1],
                                         ROUND, ALU.mult, ALU.add)
            link(last)
            link(dve.tensor_scalar(cx[:, 512:512 + T * D], cx[:, 0:T * D], ROUND, 127.0, ALU.subtract, ALU.min))
            dve.tensor_scalar(qi[:, :], cx[:, 512:512 + T * D], -128.0, None, ALU.max).then_inc(sm_["f3_q"], 1)
            link(dve.tensor_scalar(sm[:, 4:6], sm[:, 2:4], wscale[:, 0:1], 1.0 / 127.0, ALU.mult, ALU.mult))
            q.wait("f3_y", 1, 1)
            for t in range(T):
                last = dve.scalar_tensor_tensor(out=cx[:, 1024 + t * D:1024 + (t + 1) * D],
                                                in0=bY[:, t * D:(t + 1) * D], scalar=sm[:, 4 + t:5 + t],
                                                in1=fb3[:, :], op0=ALU.mult, op1=ALU.add)
            link(last)
            dve.tensor_tensor(X[:, bass.ds(b * T * D, T * D)], xb[:, :], cx[:, 1024:1024 + T * D],
                              ALU.add).then_inc(sm_["x_out"], 1)
            q.wait("x_out", 1, 1)

        def each_batch(f, eng, chain, loop):
            with eng.Fori(0, B) as b:
                if chain is not None:
                    chain.restart()
                f(Count(eng, b, loop), b)

        @block.sync
        def _(sp):
            def load(name, *pairs):
                for o, i in pairs:
                    sp.dma_start(o, i).then_inc(sm_[name], 16)

            load("ld_x", (v3(X[:, :], D), x.rearrange("b (t p) d -> p (b t) d", p=P)), (CT[:, 0:B * S], ctxT),
                 (m8[:, :].rearrange("p (t m) -> p t m", t=T), mask1.rearrange("(t p) m -> p t m", p=P)),
                 (dmask[:, :], w["dist"]))
            load("ld_l0", (w0[1], w["wk0"]), (w0[2], w["wv0"]), (w0[0], w["wq0"]), (w0[3], w["wo0"]),
                 (rows[:, :], w["rows"]))
            load("ld_first", (iota8[:, :], w["iota8"]), (rt0[:, :], w["rt0"]))
            ne = E0 - 1
            load("ld_f0",
                 (v3(f0g[:, 0:ne * F0], F0), w["gate0"].rearrange("e d h -> d e h")),
                 (v3(f0u[:, 0:ne * F0], F0), w["up0"].rearrange("e d h -> d e h")),
                 (v3(f0d[:, 0:ne * F0], D), w["down0"].rearrange("e (c p) d -> p (e c) d", p=P)),
                 (f0g[:, ne * F0:], w["sgate0"]), (f0u[:, ne * F0:], w["sup0"]),
                 (v3(f0d[:, ne * F0:], D), w["sdown0"].rearrange("(c p) d -> p c d", p=P)))
            load("ld_l1", (wqk1[:, :], w["wqk1"]), (wvo1[:, :], w["wvo1"]), (qb1[:, :], w["qb1"]),
                 (cosT[:, :], w["cosT"]), (sinT[:, :], w["sinT"]), (hmask[:, :], w["hmask"]))
            load("ld_f1", (f1g, w["g1"]), (f1u, w["u1"]), (f1d, w["d1"]), (rt1[:, :], w["rt1"]),
                 (iota32[:, :], w["iota32"]))
            load("ld_b", (inj[:, :], w["inj"]), (rt2[:, :], w["rt2"]), (qb3[:, :], w["qb3"]),
                 (b1t[:, :], w["b1_2"]), (b2t[:, :], w["b2_2"]),
                 (wscale[:, :], w["wscale"].to_broadcast([P, 1])), (fb3[:, :], w["fb3"].to_broadcast([P, D])),
                 *[(pk[32 * s:32 * s + 32, :], w["packed"]) for s in range(4)])
            sp.wait_ge(sm_["x_back"], B)
            load("ld_late", (cnat.rearrange("p (n d) -> p n d", d=D), ctxm.rearrange("b (t p) d -> p (b t) d", p=P)),
                 (wqk3, w["wqk3"]), (wvo3, w["wvo3"]))
            skew(sp)
            for n, (lo, hi) in enumerate(SKEW):
                sp.wait_ge(sm_[f"skew{n}"], 16 * (hi - lo))
            load("ld_f2d", (v3(f2d, D), w["w2_2"].rearrange("e (c p) d -> p (e c) d", p=P)))
            sp.wait_ge(sm_["forward"], STEPS)
            load("ld_f2u", (v3(f2u, F2), w["w1_2"].rearrange("e d h -> d e h")))
            unskew(sp)

            def batch(q, b):
                q.wait("x_done", XD_B, 1)
                sp.dma_start(v3(mload, S), mask3[bass.ds(b, 1)].rearrange("a (t p) m -> p (a t) m", p=P)) \
                    .then_inc(sm_["mask_loaded"], 16)
                q.wait("x_out", 1, 1)
                sp.dma_start(out[bass.ds(b, 1)].rearrange("a (t p) d -> p (a t) d", p=P),
                             v3(X[:, bass.ds(b * T * D, T * D)], D)).then_inc(sm_["stored"], 16)

            each_batch(batch, sp, None, "B")
            sp.wait_ge(sm_["stored"], 16 * B)

        @block.gpsimd
        def _(pool):
            pool.memset(ident[:, :], 0.0).then_inc(sm_["ident_zero"], 1)
            pool.memset(neghalf[:, :], -0.5).then_inc(sm_["consts"], 1)
            pool.memset(tiny[:, :], 1e-30).then_inc(sm_["consts"], 1)
            pool.memset(ones[:, :], 1.0).then_inc(sm_["consts"], 1)
            pool.memset(XNT[:, B * S:], 0.0).then_inc(sm_["consts"], 1)
            pool.memset(CT[:, B * S:], 0.0).then_inc(sm_["consts"], 1)
            pool.wait_ge(sm_["ident_zero"], 1)
            pool.affine_select(out=ident[:, :], in_=ident[:, :], compare_op=ALU.not_equal, fill=1.0, base=0,
                               pattern=[[-1, P]], channel_multiplier=1).then_inc(sm_["consts"], 1)
            pool.wait_ge(sm_["consts"], 6)
            pool.tensor_copy(identb[:, :], ident[:, :]).then_inc(sm_["identb_ready"], 1)
            pool.wait_ge(sm_["ld_x"], 16 * 4)

            def batch(q, b):
                a = q.loop == "A"
                for n in range(2 if a else 1):
                    ln_pool(pool, q, q.loop, n)
                q.wait("x_done", XD_A if a else XD_B, 2 if a else 1)
                zero = XNT[:, B * S:].unsqueeze(1).to_broadcast([P, 1024 // S, S])
                pool.tensor_tensor(v3(V[:, 0:1024], S), zero, zero, ALU.add).then_inc(sm_["v_zero"], 1)
                ln_pool(pool, q, q.loop, 2 if a else 1)
                if a:
                    att_pool(pool, q, "a1", "p1_dve", 2, H)
                else:
                    att_pool(pool, q, "a3", "p3_dve", 1, 0)
                pool.tensor_copy(ctb[:, :], CT[:, bass.ds(b * S + S, S)]).then_inc(sm_["ctb_ready"], 1)
                for n in ((3, 4) if a else (2,)):
                    ln_pool(pool, q, q.loop, n)

            pool.tensor_copy(ctb[:, :], CT[:, 0:S]).then_inc(sm_["ctb_ready"], 1)
            each_batch(batch, pool, None, "A")
            pool.wait_ge(sm_["x_back"], B)
            dist_pool(pool)
            moves_pool(pool, Chain(pool, pool_chain))
            pool.wait_ge(sm_["ctb_ready"], B + 1)
            pool.tensor_copy(ctb[:, :], CT[:, 0:S]).then_inc(sm_["ctb_ready"], 1)
            each_batch(batch, pool, None, "B")

        @block.tensor
        def _(pe):
            pe.wait_ge(sm_["consts"], 6)

            small_pe(pe)

            def batch_a(q, b):
                l0_pe(pe, q)
                f0_pe(pe, q)
                l1_pe(pe, q)
                f1_pe(pe, q)
                ln_pe(pe, q, "A", 4)

            each_batch(batch_a, pe, None, "A")
            tern_pe(pe)
            dist_pe(pe)
            expand_pe(pe)

            def batch_b(q, b):
                f2_pe(pe, q)
                l3_pe(pe, q)
                f3_pe(pe, q)

            each_batch(batch_b, pe, None, "B")

        @block.scalar
        def _(act):
            link = Chain(act, act_chain)

            small_act(act)

            def batch_a(q, b):
                l0_act(act, q, link)
                f0_act(act, q, link)
                l1_act(act, q, link)
                f1_act(act, q, link)
                q.wait("xnT_full", LN_A, 5)
                act.copy(XNT[:, bass.ds(b * S, S)], bLN[:, 0:S]).then_inc(sm_["xnT_ready"], 1)
                q.wait("xnT_ready", LN_A, 5)

            each_batch(batch_a, act, link, "A")
            act.wait_ge(sm_["x_back"], B)
            dist_act(act)
            backward_act(act)

            def batch_b(q, b):
                f2_act(act, q, link)
                l3_act(act, q, link)
                f3_act(act, q, link)

            each_batch(batch_b, act, link, "B")

        @block.vector
        def _(dve):
            link = Chain(dve, dve_chain)
            dve.wait_ge(sm_["ld_x"], 16 * 4)
            dve.wait_ge(sm_["consts"], 6)
            link(dve.tensor_scalar(mbig[:, :], m8[:, :], 0.0, BIG, ALU.is_equal, ALU.mult))
            link(dve.tensor_tensor(dmask[:, :], dmask[:, :], mbig[:, :], ALU.add))

            small_dve(dve, link)

            def batch_a(q, b):
                dve.tensor_copy(xb[:, :], X[:, bass.ds(b * T * D, T * D)]).then_inc(sm_["x_done"], 1)
                q.wait("x_done", XD_A, 1)
                l0_dve(dve, q, link)
                q.wait("x_done", XD_A, 2)
                f0_dve(dve, q, link)
                q.wait("x_done", XD_A, 3)
                l1_dve(dve, q, link)
                q.wait("x_done", XD_A, 4)
                f1_dve(dve, q, link)
                q.wait("x_done", XD_A, 5)
                ln_dve(dve, q, link, "A", 4)
                dve.tensor_scalar(X[:, bass.ds(b * T * D, T * D)], xb[:, :], 1.0, None,
                                  ALU.mult).then_inc(sm_["x_back"], 1)
                q.wait("x_back", 1, 1)
                q.wait("xnT_full", LN_A, 5)

            each_batch(batch_a, dve, link, "A")
            link.restart()
            tern_dve(dve, link)
            dist_dve(dve, link)
            forward_dve(dve, link)
            backward_dve(dve, link)
            expand_dve(dve, link)

            def batch_b(q, b):
                dve.tensor_copy(xb[:, :], X[:, bass.ds(b * T * D, T * D)]).then_inc(sm_["x_done"], 1)
                q.wait("x_done", XD_B, 1)
                f2_dve(dve, q, link)
                q.wait("x_done", XD_B, 2)
                l3_dve(dve, q, link)
                q.wait("x_done", XD_B, 3)
                f3_dve(dve, q, link, b)

            each_batch(batch_b, dve, link, "B")


N_FIRST = 2
N_LATE = 3


def kernel(**inputs):
    import numpy as np
    import concourse.bacc as bacc
    from concourse.bass_utils import run_bass_kernel_spmd

    g = {k: np.asarray(v) for k, v in inputs.items()}

    def cat(*a):
        return np.concatenate(a, axis=1)

    swap = (np.arange(P) // HS) * HS + (np.arange(P) + HS // 2) % HS
    inv = 1.0 / 10000.0 ** (np.arange(0, HS, 2, dtype=np.float32) / HS)
    fr = np.outer(np.arange(S, dtype=np.float32), inv)
    emb = np.concatenate([fr, fr], axis=-1)
    sign = np.where(np.arange(HS) < HS // 2, -1.0, 1.0).astype(np.float32)
    cosT, sinT = np.tile(np.cos(emb).T, (H, 1)), np.tile((np.sin(emb) * sign).T, (H, 1))
    on_head = (np.arange(P)[:, None] // HS == np.arange(H)[None]) * -HS ** -0.5
    hmask = np.concatenate([on_head, on_head / np.array(SLOPES)], axis=1)
    pos = np.arange(S, dtype=np.float32)
    dist = np.abs(pos[:, None] - pos[None, :]).reshape(T, P, S)
    q1, k1 = g["L1_xattn_Wq"].T, g["L1_xattn_Wk"].T
    bq1, bk1 = g["L1_xattn_bq"], g["L1_xattn_bk"]
    q3 = g["L3_xattn_Wq"].transpose(1, 0, 2).reshape(D, P)
    k3 = g["L3_xattn_Wk"].transpose(1, 0, 2).reshape(D, P)

    def wo8(wt):
        a = wt.reshape(2, 1, 4, 2, HS, D).transpose(0, 1, 3, 2, 4, 5)
        return np.broadcast_to(a, (2, T, 2, 4, HS, D)).reshape(2, P, D).transpose(1, 0, 2).reshape(P, 2 * D)

    def up1(routed, shared):
        return cat(routed.transpose(2, 0, 1).reshape(D, E1 * F1), shared.T)

    def down1(routed, shared):
        a = np.concatenate([routed, shared[None]], axis=0).transpose(0, 2, 1).reshape(E1 + 1, 2, P, D)
        return a.transpose(2, 0, 1, 3).reshape(P, -1)

    consts = {
        "rows": np.concatenate([g["L0_xattn_projection_bias"], g["L1_xattn_bv"], g["L1_xattn_bo"],
                                g["L3_xattn_bv"].reshape(-1), g["L3_xattn_bo"]])[None],
        "cosT": cosT, "sinT": sinT, "hmask": hmask.astype(np.float32),
        "dist": dist.transpose(1, 0, 2).reshape(P, T * S),
        "iota8": np.tile(np.arange(8, dtype=np.float32), (P, 1)),
        "iota32": np.tile(np.arange(1, CAP + 1, dtype=np.float32), (P, 1)),
        "inj": (np.arange(P) % 32 == K - 1).astype(np.float32)[:, None],
        "rt0": g["L0_ffn_router_w"], "rt1": g["L1_ffn_gate_w"].T, "rt2": g["L2_ffn_Wg"],
        "qb1": np.stack([bq1, bq1[swap], bk1, bk1[swap]], axis=1),
        "qb3": np.stack([g["L3_xattn_bq"].reshape(-1), g["L3_xattn_bk"].reshape(-1)], axis=1),
        "wq0": g["L0_xattn_query_kernel"].transpose(1, 0, 2).reshape(D, H * HS0),
        "wk0": g["L0_xattn_key_kernel"].transpose(1, 0, 2).reshape(D, H * HS0),
        "wv0": g["L0_xattn_value_kernel"].transpose(1, 0, 2).reshape(D, H * HS0),
        "wo0": g["L0_xattn_projection_kernel"].reshape(C0, P, D).transpose(1, 0, 2).reshape(P, C0 * D),
        "gate0": g["L0_ffn_gate_w"], "up0": g["L0_ffn_up_w"], "down0": g["L0_ffn_down_w"],
        "sgate0": g["L0_ffn_shared_gate_w"], "sup0": g["L0_ffn_shared_up_w"], "sdown0": g["L0_ffn_shared_down_w"],
        "wqk1": cat(q1, q1[:, swap], k1, k1[:, swap]),
        "wvo1": cat(g["L1_xattn_Wv"].T, wo8(g["L1_xattn_Wo"].T)),
        "g1": up1(g["L1_ffn_Wg"], g["L1_ffn_Ws_g"]), "u1": up1(g["L1_ffn_Wu"], g["L1_ffn_Ws_u"]),
        "d1": down1(g["L1_ffn_Wd"], g["L1_ffn_Ws_d"]),
        "wqk3": cat(q3, k3),
        "wvo3": cat(g["L3_xattn_Wv"].transpose(1, 0, 2).reshape(D, P), wo8(g["L3_xattn_Wo"])),
        "w1_2": g["L2_ffn_W1"], "w2_2": g["L2_ffn_W2"],
        "b1_2": g["L2_ffn_b1"].reshape(E2 * 4, P).T, "b2_2": g["L2_ffn_b2"],
        "packed": g["L3_ffn_packed_weight"].reshape(32, P), "wscale": g["L3_ffn_weight_scale"].reshape(1, 1),
        "fb3": g["L3_ffn_bias"].reshape(1, D),
    }
    nc = bacc.Bacc("TRN2", target_bir_lowering=False, num_devices=1)
    arrays = {}

    def dram(name, a):
        a = np.ascontiguousarray(a)
        arrays[name] = a
        return nc.dram_tensor(name, a.shape, mybir.dt.from_np(a.dtype), kind="ExternalInput").ap()

    xd = dram("x", g["x"])
    cm = dram("ctx", g["ctx_1024"])
    ct = dram("ctxT", g["ctx_1024"].transpose(2, 0, 1).reshape(D, B * S))
    m1 = dram("mask1", g["mask_1x1xSxS2_bk0"].reshape(S, S))
    m3 = dram("mask3", g["mask_BxSxS2_ik0"])
    w = {k: dram("w_" + k, a) for k, a in consts.items()}
    o = nc.dram_tensor("out", (B, S, D), F32, kind="ExternalOutput").ap()
    build(nc, xd, cm, ct, m1, m3, w, o)
    r = run_bass_kernel_spmd(nc, [arrays], core_ids=[0])
    return r.results[0]["out"]
```
